# Optimizing a Trainium2 kernel written in Bass

```python
import numpy as np
import jax
import jax.numpy as jnp

def _softmax(x, axis=-1):
    return jax.nn.softmax(x, axis=axis)

def _gelu(x):
    return jax.nn.gelu(x, approximate=True)

def _silu(x):
    return jax.nn.silu(x)

def _sigmoid(x):
    return jax.nn.sigmoid(x)

def _layernorm(x, axis=-1, eps=1e-05):
    m = jnp.mean(x, axis=axis, keepdims=True)
    v = jnp.var(x, axis=axis, keepdims=True)
    return (x - m) / jnp.sqrt(v + eps)

def _scatter_add(tgt, idx, src, axis=0):
    return tgt.at[idx].add(src)

def _segment_sum(src, seg, n):
    return jax.ops.segment_sum(src, seg, n)
kernel_name = 'mk_seq_postln_d1_jaxref_r8_e8b795'

def setup_inputs(seed: int=0):
    np.random.seed(seed)
    _w = jnp.asarray

    def _L0_attn_setup():
        import jax, jax.numpy as jnp
        import numpy as np
        B, S, E = (4, 256, 128)
        H, KVH = (16, 4)
        D = E // H
        QL, KVL = (64, 32)
        ROPE_BASE = 10000.0

        def _rope(x):
            d = x.shape[-1]
            inv_freq = 1.0 / ROPE_BASE ** (jnp.arange(0, d, 2, dtype=jnp.float32) / d)
            t = jnp.arange(x.shape[1], dtype=jnp.float32)
            freqs = jnp.outer(t, inv_freq)
            cos = jnp.cos(freqs)[None, :, None, :].astype(x.dtype)
            sin = jnp.sin(freqs)[None, :, None, :].astype(x.dtype)
            x1, x2 = (x[..., ::2], x[..., 1::2])
            r1 = x1 * cos - x2 * sin
            r2 = x1 * sin + x2 * cos
            return jnp.stack([r1, r2], axis=-1).reshape(x.shape)
        key = jax.random.key(seed)
        ks = jax.random.split(key, 7)
        s = 0.02
        return {'x': jax.random.normal(ks[0], (B, S, E), dtype=jnp.float32), 'Wqa': jax.random.normal(ks[1], (E, QL), dtype=jnp.float32) * s, 'Wqb': jax.random.normal(ks[2], (QL, E), dtype=jnp.float32) * s, 'Wkva': jax.random.normal(ks[3], (E, KVL), dtype=jnp.float32) * s, 'Wkvb': jax.random.normal(ks[4], (KVL, KVH * D * 2), dtype=jnp.float32) * s, 'Wout': jax.random.normal(ks[5], (E, E), dtype=jnp.float32) * s, 'bout': jax.random.normal(ks[6], (E,), dtype=jnp.float32) * s}
    _L0_attn_in = _L0_attn_setup()

    def _L0_ffn_setup():
        import jax, jax.numpy as jnp
        import numpy as np
        DIM = 128
        DEPTH = 6
        HEADS = 16
        DIM_HEAD = 64
        WINDOW = 32
        INNER = HEADS * DIM_HEAD
        DIM_INNER = int(DIM * 4 * 2 / 3)
        QK_SCALE = 8.0

        def shift_tokens(t):
            a, s = jnp.split(t, 2, -1)
            s = jnp.pad(s, ((0, 0), (1, 0), (0, 0)))[:, :-1]
            return jnp.concatenate([a, s], -1)

        def l2norm(t):
            return t / jnp.maximum(jnp.linalg.norm(t, axis=-1, keepdims=True), 1e-12)

        def rotate_half(x):
            x1, x2 = jnp.split(x, 2, -1)
            return jnp.concatenate([-x2, x1], -1)

        def rotary_tables(n):
            half = jnp.arange(0, DIM_HEAD, 2, dtype=jnp.float32)
            inv_freq = 1.0 / 10000.0 ** (half / DIM_HEAD)
            t = jnp.arange(n, dtype=jnp.float32)
            freqs = t[:, None] * inv_freq[None, :]
            freqs = jnp.concatenate([freqs, freqs], -1)
            base_scale = (half + 0.4 * DIM_HEAD) / (1.4 * DIM_HEAD)
            power = (t - n // 2) / (WINDOW // 2)
            scale = base_scale[None, :] ** power[:, None]
            scale = jnp.concatenate([scale, scale], -1)
            return (freqs, scale)

        def local_attention(q, k, v):
            b, h, n, d = q.shape
            w = WINDOW
            nw = n // w
            bq = q.reshape(b, h, nw, w, d)
            bk = k.reshape(b, h, nw, w, d)
            bv = v.reshape(b, h, nw, w, d)

            def look(t):
                p = jnp.pad(t, ((0, 0), (0, 0), (1, 0), (0, 0), (0, 0)))
                return jnp.concatenate([p[:, :, :nw], p[:, :, 1:]], axis=3)
            bk2, bv2 = (look(bk), look(bv))
            seq = jnp.arange(n).reshape(nw, w)
            seq_p = jnp.pad(seq, ((1, 0), (0, 0)), constant_values=-1)
            jt = jnp.concatenate([seq_p[:nw], seq_p[1:]], axis=1)
            it = seq[:, :, None]
            jb = jt[:, None, :]
            mask = (it < jb) | (it > jb + w) | (jb == -1)
            sim = jnp.einsum('bhwie,bhwje->bhwij', bq, bk2) * QK_SCALE
            sim = jnp.where(mask, -jnp.finfo(sim.dtype).max, sim)
            attn = jax.nn.softmax(sim, -1)
            out = jnp.einsum('bhwij,bhwje->bhwie', attn, bv2)
            return out.reshape(b, h, n, d)

        def attn_layer(x, Wqkv, qs, ksc, Wo):
            b, n, _ = x.shape
            qkv = x @ Wqkv
            q, k, v = jnp.split(qkv, 3, -1)
            sh = lambda t: t.reshape(b, n, HEADS, DIM_HEAD).transpose(0, 2, 1, 3)
            q, k, v = (sh(q), sh(k), sh(v))
            q = l2norm(q) * qs
            k = l2norm(k) * ksc
            freqs, scale = rotary_tables(n)
            cos, sin = (jnp.cos(freqs), jnp.sin(freqs))
            q = q * cos * scale + rotate_half(q) * sin * scale
            inv = 1.0 / scale
            k = k * cos * inv + rotate_half(k) * sin * inv
            out = local_attention(q, k, v)
            out = out.transpose(0, 2, 1, 3).reshape(b, n, INNER)
            return out @ Wo

        def ffn_layer(x, g, bln, W1, b1, W2, b2):
            mu = x.mean(-1, keepdims=True)
            var = ((x - mu) ** 2).mean(-1, keepdims=True)
            xn = (x - mu) / jnp.sqrt(var + 1e-05) * g + bln
            hg = xn @ W1 + b1
            a, gate = jnp.split(hg, 2, -1)
            return a * jax.nn.gelu(gate, approximate=False) @ W2 + b2
        key = jax.random.key(seed)
        ks = jax.random.split(key, 8)
        B, N = (2, 256)
        init = lambda k, shape: jax.random.normal(k, shape, jnp.float32) * 0.02
        return {'x': jax.random.normal(ks[0], (B, N, DIM), jnp.float32), 'Wqkv': init(ks[1], (DEPTH, DIM, 3 * INNER)), 'q_scale': jnp.ones((DEPTH, DIM_HEAD), jnp.float32), 'k_scale': jnp.ones((DEPTH, DIM_HEAD), jnp.float32), 'Wo': init(ks[2], (DEPTH, INNER, DIM)), 'ln_g': jnp.ones((DEPTH, DIM), jnp.float32), 'ln_b': jnp.zeros((DEPTH, DIM), jnp.float32), 'W1': init(ks[3], (DEPTH, DIM, 2 * DIM_INNER)), 'b1': jnp.zeros((DEPTH, 2 * DIM_INNER), jnp.float32), 'W2': init(ks[4], (DEPTH, DIM_INNER, DIM)), 'b2': jnp.zeros((DEPTH, DIM), jnp.float32)}
    _L0_ffn_in = _L0_ffn_setup()
    _d = {'L0_attn_x': _L0_attn_in['x'], 'L0_attn_Wqa': _L0_attn_in['Wqa'], 'L0_attn_Wqb': _L0_attn_in['Wqb'], 'L0_attn_Wkva': _L0_attn_in['Wkva'], 'L0_attn_Wkvb': _L0_attn_in['Wkvb'], 'L0_attn_Wout': _L0_attn_in['Wout'], 'L0_attn_bout': _L0_attn_in['bout'], 'L0_ffn_Wqkv': _L0_ffn_in['Wqkv'], 'L0_ffn_q_scale': _L0_ffn_in['q_scale'], 'L0_ffn_k_scale': _L0_ffn_in['k_scale'], 'L0_ffn_Wo': _L0_ffn_in['Wo'], 'L0_ffn_ln_g': _L0_ffn_in['ln_g'], 'L0_ffn_ln_b': _L0_ffn_in['ln_b'], 'L0_ffn_W1': _L0_ffn_in['W1'], 'L0_ffn_b1': _L0_ffn_in['b1'], 'L0_ffn_W2': _L0_ffn_in['W2'], 'L0_ffn_b2': _L0_ffn_in['b2']}
    _x0 = _d['L0_attn_x']
    _d['L0_attn_x'] = jax.random.normal(jax.random.fold_in(jax.random.key(seed), 1), (4, 1024, 128), dtype=_x0.dtype)
    del _x0
    return _d

def reference(L0_attn_x, L0_attn_Wqa, L0_attn_Wqb, L0_attn_Wkva, L0_attn_Wkvb, L0_attn_Wout, L0_attn_bout, L0_ffn_Wqkv, L0_ffn_q_scale, L0_ffn_k_scale, L0_ffn_Wo, L0_ffn_ln_g, L0_ffn_ln_b, L0_ffn_W1, L0_ffn_b1, L0_ffn_W2, L0_ffn_b2):

    def _L0_attn_ref(x, Wqa, Wqb, Wkva, Wkvb, Wout, bout):
        import jax, jax.numpy as jnp
        import numpy as np
        B, S, E = (4, 256, 128)
        H, KVH = (16, 4)
        D = E // H
        QL, KVL = (64, 32)
        ROPE_BASE = 10000.0

        def _rope(x):
            d = x.shape[-1]
            inv_freq = 1.0 / ROPE_BASE ** (jnp.arange(0, d, 2, dtype=jnp.float32) / d)
            t = jnp.arange(x.shape[1], dtype=jnp.float32)
            freqs = jnp.outer(t, inv_freq)
            cos = jnp.cos(freqs)[None, :, None, :].astype(x.dtype)
            sin = jnp.sin(freqs)[None, :, None, :].astype(x.dtype)
            x1, x2 = (x[..., ::2], x[..., 1::2])
            r1 = x1 * cos - x2 * sin
            r2 = x1 * sin + x2 * cos
            return jnp.stack([r1, r2], axis=-1).reshape(x.shape)
        b, s, _ = x.shape
        scale = D ** (-0.5)
        q = (x @ Wqa @ Wqb).reshape(b, s, H, D)
        kv = (x @ Wkva @ Wkvb).reshape(b, s, KVH, D, 2)
        k, v = (kv[..., 0], kv[..., 1])
        q = _rope(q)
        k = _rope(k)
        g = H // KVH
        k = jnp.repeat(k, g, axis=2)
        v = jnp.repeat(v, g, axis=2)
        scores = jnp.einsum('bqhd,bkhd->bhqk', q, k) * scale
        causal = jnp.triu(jnp.ones((s, s), dtype=bool), k=1)
        scores = jnp.where(causal[None, None], -jnp.inf, scores)
        w = jax.nn.softmax(scores, axis=-1)
        out = jnp.einsum('bhqk,bkhd->bqhd', w, v).reshape(b, s, E)
        return out @ Wout + bout

    def _L0_ffn_ref(x, Wqkv, q_scale, k_scale, Wo, ln_g, ln_b, W1, b1, W2, b2):
        import jax, jax.numpy as jnp
        import numpy as np
        DIM = 128
        DEPTH = 6
        HEADS = 16
        DIM_HEAD = 64
        WINDOW = 32
        INNER = HEADS * DIM_HEAD
        DIM_INNER = int(DIM * 4 * 2 / 3)
        QK_SCALE = 8.0

        def shift_tokens(t):
            a, s = jnp.split(t, 2, -1)
            s = jnp.pad(s, ((0, 0), (1, 0), (0, 0)))[:, :-1]
            return jnp.concatenate([a, s], -1)

        def l2norm(t):
            return t / jnp.maximum(jnp.linalg.norm(t, axis=-1, keepdims=True), 1e-12)

        def rotate_half(x):
            x1, x2 = jnp.split(x, 2, -1)
            return jnp.concatenate([-x2, x1], -1)

        def rotary_tables(n):
            half = jnp.arange(0, DIM_HEAD, 2, dtype=jnp.float32)
            inv_freq = 1.0 / 10000.0 ** (half / DIM_HEAD)
            t = jnp.arange(n, dtype=jnp.float32)
            freqs = t[:, None] * inv_freq[None, :]
            freqs = jnp.concatenate([freqs, freqs], -1)
            base_scale = (half + 0.4 * DIM_HEAD) / (1.4 * DIM_HEAD)
            power = (t - n // 2) / (WINDOW // 2)
            scale = base_scale[None, :] ** power[:, None]
            scale = jnp.concatenate([scale, scale], -1)
            return (freqs, scale)

        def local_attention(q, k, v):
            b, h, n, d = q.shape
            w = WINDOW
            nw = n // w
            bq = q.reshape(b, h, nw, w, d)
            bk = k.reshape(b, h, nw, w, d)
            bv = v.reshape(b, h, nw, w, d)

            def look(t):
                p = jnp.pad(t, ((0, 0), (0, 0), (1, 0), (0, 0), (0, 0)))
                return jnp.concatenate([p[:, :, :nw], p[:, :, 1:]], axis=3)
            bk2, bv2 = (look(bk), look(bv))
            seq = jnp.arange(n).reshape(nw, w)
            seq_p = jnp.pad(seq, ((1, 0), (0, 0)), constant_values=-1)
            jt = jnp.concatenate([seq_p[:nw], seq_p[1:]], axis=1)
            it = seq[:, :, None]
            jb = jt[:, None, :]
            mask = (it < jb) | (it > jb + w) | (jb == -1)
            sim = jnp.einsum('bhwie,bhwje->bhwij', bq, bk2) * QK_SCALE
            sim = jnp.where(mask, -jnp.finfo(sim.dtype).max, sim)
            attn = jax.nn.softmax(sim, -1)
            out = jnp.einsum('bhwij,bhwje->bhwie', attn, bv2)
            return out.reshape(b, h, n, d)

        def attn_layer(x, Wqkv, qs, ksc, Wo):
            b, n, _ = x.shape
            qkv = x @ Wqkv
            q, k, v = jnp.split(qkv, 3, -1)
            sh = lambda t: t.reshape(b, n, HEADS, DIM_HEAD).transpose(0, 2, 1, 3)
            q, k, v = (sh(q), sh(k), sh(v))
            q = l2norm(q) * qs
            k = l2norm(k) * ksc
            freqs, scale = rotary_tables(n)
            cos, sin = (jnp.cos(freqs), jnp.sin(freqs))
            q = q * cos * scale + rotate_half(q) * sin * scale
            inv = 1.0 / scale
            k = k * cos * inv + rotate_half(k) * sin * inv
            out = local_attention(q, k, v)
            out = out.transpose(0, 2, 1, 3).reshape(b, n, INNER)
            return out @ Wo

        def ffn_layer(x, g, bln, W1, b1, W2, b2):
            mu = x.mean(-1, keepdims=True)
            var = ((x - mu) ** 2).mean(-1, keepdims=True)
            xn = (x - mu) / jnp.sqrt(var + 1e-05) * g + bln
            hg = xn @ W1 + b1
            a, gate = jnp.split(hg, 2, -1)
            return a * jax.nn.gelu(gate, approximate=False) @ W2 + b2
        for i in range(DEPTH):
            x = attn_layer(shift_tokens(x), Wqkv[i], q_scale[i], k_scale[i], Wo[i]) + x
            x = ffn_layer(shift_tokens(x), ln_g[i], ln_b[i], W1[i], b1[i], W2[i], b2[i]) + x
        return x
    x = L0_attn_x
    x = _layernorm(x + _L0_attn_ref(x, L0_attn_Wqa, L0_attn_Wqb, L0_attn_Wkva, L0_attn_Wkvb, L0_attn_Wout, L0_attn_bout), axis=-1)
    x = _layernorm(x + _L0_ffn_ref(x, L0_ffn_Wqkv, L0_ffn_q_scale, L0_ffn_k_scale, L0_ffn_Wo, L0_ffn_ln_g, L0_ffn_ln_b, L0_ffn_W1, L0_ffn_b1, L0_ffn_W2, L0_ffn_b2), axis=-1)
    return x

_drawn_inputs = setup_inputs


def setup_inputs(seed=0):
    import zlib

    import numpy as np

    out = dict(_drawn_inputs(seed))
    spreads = {'L0_ffn_q_scale': (1.0, 0.6),
     'L0_ffn_k_scale': (1.0, 0.6),
     'L0_ffn_ln_g': (1.0, 0.6),
     'L0_ffn_ln_b': (0.0, 0.8),
     'L0_ffn_b1': (0.0, 0.8),
     'L0_ffn_b2': (0.0, 0.1)}
    factors = {'L0_attn_Wqa': 8.0,
     'L0_attn_Wqb': 8.0,
     'L0_attn_Wkva': 8.0,
     'L0_attn_Wkvb': 8.0,
     'L0_attn_Wout': 8.0,
     'L0_ffn_W1': 3.675,
     'L0_ffn_W2': 3.612,
     'L0_attn_bout': 4.185}
    for name, (base, spread) in spreads.items():
        noise = np.random.default_rng([zlib.crc32(name.encode()), seed]).standard_normal(out[name].shape)
        drawn = base * np.exp(spread * noise) if base else spread * noise
        out[name] = jnp.asarray(drawn.astype(out[name].dtype))
    for name, factor in factors.items():
        out[name] = (out[name] * factor).astype(out[name].dtype)
    return out
```

```python
import concourse.bass as bass
from concourse import mybir
from contextlib import ExitStack

fp32 = mybir.dt.float32
bf16 = mybir.dt.bfloat16
i32 = mybir.dt.int32
ALU = mybir.AluOpType
ACT = mybir.ActivationFunctionType
AX = mybir.AxisListType

P = 128
BATCH, SEQ, DIM = 4, 1024, 128
MASKED = -1e30

DEPTH, HEADS, DH, WINDOW = 6, 16, 64, 32
INNER = HEADS * DH
FF = DIM * 4 * 2 // 3
FF_BLOCKS = [(0, 128), (128, 128), (256, FF - 256)]
QK_SCALE = 8.0
PAIR = 2 * P
POS = SEQ // PAIR
ROUNDS = DEPTH * BATCH
PAIRS = ROUNDS * POS
HP = HEADS // 2
RSQRT_MAGIC = 0x5F3759DF

SMALL = dict(g=0, b=1, b1a=2, b1g=5, b2=8)
N_SMALL = 9


class Ring:

    def __init__(self, stage_names):
        self.stage_names = stage_names
        self.full = len(stage_names)
        assert self.full % 3 == 0

    def names(self, t):
        return [s for s, lag in self.stage_names if not isinstance(t, int) or 0 <= t - lag < PAIRS]

    def before(self, t):
        early = [len(self.names(s)) for s in (-1, 0, 1)]
        if isinstance(t, int) and t < 2:
            return sum(early[:t + 1])
        if isinstance(t, int) and t > PAIRS:
            return self.before(t - 1) + len(self.names(t - 1))
        return self.full * t + (sum(early) - 2 * self.full)

    def at(self, step, name):
        early = sum(len(self.names(s)) for s in (-1, 0, 1))
        j = self.names(step.t).index(name)
        b = self.before(step.t)
        number = b + j
        slot = (number if isinstance(b, int) else early - 2 * self.full + j) % 3
        return slot, number


class Step:

    def __init__(self, f, p):
        self.f, self.p = f, p
        self.t = POS * f + p

    def pair(self, lag):
        return Pair(self, lag)


class Pair:

    def __init__(self, step, lag):
        q = step.p - lag
        self.p = q % POS
        self.f = step.f + q // POS
        self.n = step.t - lag
        self.par = self.p % 2
        self.k = 2 * self.f + self.p // 2
        self.exists = not isinstance(self.n, int) or 0 <= self.n < PAIRS


def layer_of(f):
    return (f // BATCH) % DEPTH


def dram_rows(region, f, row, count):
    return region[bass.ds(f, 1), row:row + count, :].rearrange("one t d -> (one t) d")


def local_layers(nc, x_dram, x1_dram, w):
    with ExitStack() as ctx:
        def sb(name, shape, dt=fp32):
            return ctx.enter_context(nc.sbuf_tensor(name, shape, dt))

        def sem(name):
            return ctx.enter_context(nc.semaphore(name))

        w_qkv = sb("w_qkv", [P, 3 * INNER])
        w_o = sb("w_o", [P, HP, DIM])
        w_1 = sb("w_1", [P, 2 * FF])
        w_2 = sb("w_2", [P, 3, DIM])
        small = sb("small", [P, N_SMALL])
        qk_row = sb("qk_row", [P, 4, DH])
        rotary = sb("rotary", [P, SEQ // P, 4, DH])
        table = sb("table", [P, SEQ // P, 4, DH])
        ident = sb("ident", [P, P])
        ident_b = sb("ident_b", [P, P], bf16)
        mask = sb("mask", [P, 2, 4, 2, 2 * WINDOW], bf16)
        xs = [sb(f"xs{i}", [P, 2, DIM]) for i in range(2)]
        xr = [sb(f"xr{i}", [P, 2, DIM]) for i in range(2)]
        xs1 = [sb(f"xs1{i}", [P, 2, DIM]) for i in range(2)]
        x1 = [sb(f"x1{i}", [P, 2, DIM]) for i in range(2)]
        x2 = [sb(f"x2{i}", [P, 2, DIM]) for i in range(2)]
        xT = sb("xT", [P, PAIR])
        sq = [sb(f"sq{i}", [P, 8, DH]) for i in range(2)]
        by_cos = sb("by_cos", [P, 2, 2 * INNER])
        by_sin = sb("by_sin", [P, 2, 2 * INNER])
        qk_rot = sb("qk_rot", [P, 2, 2 * INNER])
        ss = sb("ss", [P, 2, 2 * HEADS])
        rnorm = sb("rnorm", [P, 2, 2 * HEADS])
        newton = sb("newton", [P, 2, 2 * HEADS])
        v = [sb(f"v{i}", [P, 2, INNER]) for i in range(2)]
        v_back = [sb(f"v_back{i}", [P, 2, INNER]) for i in range(2)]
        qT = sb("qT", [P, HP, PAIR])
        kT = [sb(f"kT{i}", [P, HP, WINDOW + PAIR]) for i in range(2)]
        prob = [sb(f"prob{i}", [P, HEADS, 2 * WINDOW]) for i in range(2)]
        row_max = sb("row_max", [P, 2, HEADS])
        row_sum = sb("row_sum", [P, 2, HEADS])
        inv_sum = sb("inv_sum", [P, 2, HEADS])
        probT = [sb(f"probT{i}", [P, HP, P]) for i in range(2)]
        attn = sb("attn", [P, 2, INNER])
        attnT = sb("attnT", [P, HP, PAIR])
        yT = sb("yT", [P, PAIR])
        y2T = sb("y2T", [P, PAIR])
        stats = sb("stats", [P, 2, 6])
        mean_var = sb("mean_var", [P, 2, 2])
        var_eps = sb("var_eps", [P, 2])
        rstd = sb("rstd", [P, 2])
        nwt = sb("nwt", [P, 2])
        xn = sb("xn", [P, 2, DIM])
        xnT = sb("xnT", [P, PAIR])
        gate = sb("gate", [P, 3, PAIR])
        hidden = sb("hidden", [P, 3, PAIR])

        bank_d = [ctx.enter_context(nc.psum_tensor(f"bank_d{i}", [P, 512], fp32)) for i in range(3)]
        scores = ctx.enter_context(nc.psum_tensor("scores", [P, HP, 2, 2 * WINDOW], fp32))
        bank_a = [ctx.enter_context(nc.psum_tensor(f"bank_a{i}", [P, 512], fp32)) for i in range(3)]

        chunks = [(a, kind, c) for a in range(2) for kind in "qk" for c in range(2)]
        chunks += [(a, "v", c) for a in range(2) for c in range(2)]
        ring_d = Ring([(x, 0) for x in chunks]
                      + [("xn", 2), ("y", 1), ("aA", 2), ("aB", 2), ("xT", -1), ("y2", 2)])
        ring_a = Ring([(f"PT{i}", 1) for i in range(4)] + [(f"O{i}", 1) for i in range(4)]
                      + [(f"qk{i}", 0) for i in range(8)] + [(f"OT{i}", 1) for i in range(4)]
                      + [("yT", 1), ("gA", 2), ("gB", 2), ("y2T", 2)])

        s_init = sem("s_init")
        s_const = sem("s_const")
        s_zero = sem("s_zero")
        xs_in = [sem(f"xs_in{i}") for i in range(2)]
        xr_in = [sem(f"xr_in{i}") for i in range(2)]
        xs1_in = [sem(f"xs1_in{i}") for i in range(2)]
        v_back_in = [sem(f"v_back_in{i}") for i in range(2)]
        x1_out, x2_out = sem("x1_out"), sem("x2_out")
        wqkv_in, wo_in, wffn_in, qkrow_in = sem("wqkv_in"), sem("wo_in"), sem("wffn_in"), sem("qkrow_in")
        d_filled, d_free = sem("d_filled"), sem("d_free")
        a_filled, a_free = sem("a_filled"), sem("a_free")
        squared = sem("squared")
        norm_ready = sem("norm_ready")
        qk_ready = sem("qk_ready")
        table_ready = sem("table_ready")
        scores_ready, scores_used = sem("scores_ready"), sem("scores_used")
        exp_done, inv_ready, prob_ready = sem("exp_done"), sem("inv_ready"), sem("prob_ready")
        xn_ready = sem("xn_ready")
        v_link = sem("v_link")
        p_link = sem("p_link")

        INIT = 4
        block = ctx.enter_context(nc.Block())

        def rounds(eng, step_fn, last_fn=None):
            for p in range(POS):
                step_fn(Step(0, p))
            with eng.Fori(1, ROUNDS) as f:
                for p in range(POS):
                    step_fn(Step(f, p))
            for t in (PAIRS, PAIRS + 1):
                step_fn(Step(ROUNDS, t - PAIRS))

        def prev(s):
            return Step(s.f, s.p - 1) if s.p else Step(s.f - 1, POS - 1)

        def runs(pair):
            return pair.exists

        @block.sync
        def _(sp):
            def load_attention_weights(f):
                sp.dma_start(w_qkv[:, :], w["Wqkv"][bass.ds(layer_of(f), 1), :, :]
                             .rearrange("one k n -> (one k) n")).then_inc(wqkv_in, 16)
                sp.dma_start(qk_row[:, :, :], w["qk_rows"][bass.ds(layer_of(f), 1), :]
                             .rearrange("one (r d) -> one r d", d=DH).to_broadcast([P, 4, DH])).then_inc(qkrow_in, 16)

            def load_wo(f):
                sp.dma_start(w_o[:, :, :], w["Wo"][bass.ds(layer_of(f), 1), :, :]
                             .rearrange("one (c k) n -> k (one c) n", k=P)).then_inc(wo_in, 16)

            def load_ffn(f):
                layer = bass.ds(layer_of(f), 1)
                sp.dma_start(w_1[:, :], w["W1"][layer, :, :].rearrange("one k n -> (one k) n")).then_inc(wffn_in, 16)
                sp.dma_start(w_2[:, 0:2, :], w["W2"][layer, 0:2 * P, :]
                             .rearrange("one (c k) n -> k (one c) n", k=P)).then_inc(wffn_in, 16)
                sp.dma_start(w_2[0:FF - 2 * P, 2, :], w["W2"][layer, 2 * P:FF, :]
                             .rearrange("one k n -> (one k) n")).then_inc(wffn_in, 16)
                sp.dma_start(small[:, :], w["small"][layer, :, :].rearrange("one k n -> (one k) n")).then_inc(wffn_in, 16)

            def load_shifted(dst, region, f, p, s):
                row = 1 + PAIR * p
                lo = dram_rows(region, f, row, PAIR).rearrange("(a t) d -> t a d", a=2)
                hi = dram_rows(region, f, row - 1, PAIR).rearrange("(a t) d -> t a d", a=2)
                sp.dma_start(dst[:, :, 0:DIM // 2], lo[:, :, 0:DIM // 2]).then_inc(s, 16)
                sp.dma_start(dst[:, :, DIM // 2:DIM], hi[:, :, DIM // 2:DIM]).then_inc(s, 16)

            def load_xs(pair):
                load_shifted(xs[pair.par], x_dram, pair.f, pair.p, xs_in[pair.par])

            sp.dma_start(rotary[:, :, :, :], w["rotary"]).then_inc(s_const, 16)
            load_attention_weights(0)
            load_wo(0)
            load_ffn(0)
            load_xs(Step(0, 0).pair(0))

            def step(s):
                new, now, back1, back2 = (s.pair(lag) for lag in (-1, 0, 1, 2))
                if not isinstance(s.t, int) or s.t > 2:
                    sp.wait_ge(x2_out, 16 * (s.t - 2))
                if runs(now) and not (isinstance(s.t, int) and s.t == PAIRS):
                    load_xs(new)
                if runs(back1):
                    sp.dma_start(xr[back1.par][:, :, :], dram_rows(x_dram, back1.f, 1 + PAIR * back1.p, PAIR)
                                 .rearrange("(a t) d -> t a d", a=2)).then_inc(xr_in[back1.par], 16)
                if runs(now):
                    sp.wait_ge(d_free, ring_d.at(s, (1, "v", 1))[1] + 1)
                    q = WINDOW
                    src, old, dst = v[now.par], v[1 - now.par], v_back[now.par]
                    done = v_back_in[now.par]
                    sp.dma_start(dst[q:P, :, :], src[0:P - q, :, :]).then_inc(done, 16)
                    sp.dma_start(dst[0:q, 1, :], src[P - q:P, 0, :]).then_inc(done, 16)
                    sp.dma_start(dst[0:q, 0, :], old[P - q:P, 1, :]).then_inc(done, 16)
                    if s.p == POS - 1:
                        load_attention_weights(s.f + 1)
                if runs(back1) and s.p == 0 and not (isinstance(s.t, int) and s.t == PAIRS):
                    sp.wait_ge(a_filled, ring_a.at(s, "yT")[1] + 1)
                    load_wo(s.f)
                if runs(back1):
                    sp.wait_ge(d_free, ring_d.at(s, "y")[1] + 1)
                    sp.dma_start(x1_dram[1 + PAIR * back1.p:1 + PAIR * (back1.p + 1), :]
                                 .rearrange("(a t) d -> t a d", a=2), x1[back1.par][:, :, :]).then_inc(x1_out, 16)
                    sp.wait_ge(x1_out, 16 * (back1.n + 1))
                    if not isinstance(back1.n, int) or back1.n >= 2:
                        sp.wait_ge(xn_ready, back1.n - 1)
                    row = 1 + PAIR * back1.p
                    for lo, hi, r in ((0, DIM // 2, row), (DIM // 2, DIM, row - 1)):
                        sp.dma_start(xs1[back1.par][:, :, lo:hi], x1_dram[r:r + PAIR, lo:hi]
                                     .rearrange("(a t) d -> t a d", a=2)).then_inc(xs1_in[back1.par], 16)
                if runs(back2):
                    sp.wait_ge(d_free, ring_d.at(s, "y2")[1] + 1)
                    sp.dma_start(dram_rows(x_dram, back2.f + BATCH, 1 + PAIR * back2.p, PAIR)
                                 .rearrange("(a t) d -> t a d", a=2), x2[back2.par][:, :, :]).then_inc(x2_out, 16)
                    if s.p == 1 and not (isinstance(s.t, int) and s.t > PAIRS):
                        load_ffn(s.f)

            rounds(sp, step)
            sp.wait_ge(x2_out, 16 * PAIRS)

        @block.tensor
        def _(pe):
            def fill_d(s, name):
                slot, n = ring_d.at(s, name)
                if not isinstance(n, int) or n >= 3:
                    pe.wait_ge(d_free, n - 2)
                return bank_d[slot]

            def fill_a(s, name):
                slot, n = ring_a.at(s, name)
                if not isinstance(n, int) or n >= 3:
                    pe.wait_ge(a_free, n - 2)
                return bank_a[slot]

            def transpose_x(s):
                new = s.pair(-1)
                pe.wait_ge(xs_in[new.par], 32 * (new.k + 1))
                bank = fill_d(s, "xT")
                for a in range(2):
                    last = nc.tensor.transpose(bank[:, P * a:P * (a + 1)], xs[new.par][:, a, :], ident[:, :])
                last.then_inc(d_filled, 1)

            def project(s):
                if s.p == 0:
                    pe.wait_ge(wqkv_in, 16 * (s.f + 1))
                pe.wait_ge(d_free, ring_d.at(prev(s), "xT")[1] + 1)
                for a, kind, c in chunks:
                    bank = fill_d(s, (a, kind, c))
                    col = INNER * "qkv".index(kind) + 512 * c
                    nc.tensor.matmul(bank[:, :], xT[:, P * a:P * (a + 1)], w_qkv[:, col:col + 512],
                                     start=True, stop=True).then_inc(d_filled, 1)

            def transpose_probs(s, pair):
                for i in range(4):
                    ph, half = divmod(i, 2)
                    if half == 0:
                        pe.wait_ge(prob_ready, 2 * pair.n + ph + 1)
                    bank = fill_a(s, f"PT{i}")
                    for j in range(4):
                        hp = 4 * half + j
                        last = nc.tensor.transpose(
                            bank[:, P * j:P * (j + 1)],
                            prob[ph][:, 2 * hp:2 * hp + 2, :].rearrange("p u k -> p (u k)"), ident[:, :])
                    last.then_inc(a_filled, 1)

            def times_v(s, pair):
                pe.wait_ge(a_free, ring_a.at(s, "PT3")[1] + 1)
                pe.wait_ge(v_back_in[pair.par], 48 * (pair.k + 1))
                for i in range(4):
                    a, half = divmod(i, 2)
                    bank = fill_a(s, f"O{i}")
                    nc.tensor.matmul(bank[:, 0:2], ident_b[:, :], ident_b[:, 0:2], start=True, stop=True)
                    for hp in range(4 * half, 4 * half + 4):
                        for h2 in range(2):
                            h = 2 * hp + h2
                            for win in range(4):
                                u, ph = divmod(win, 2)
                                src = (v if ph else v_back)[pair.par]
                                last = nc.tensor.matmul(
                                    bank[32 * win:32 * win + 32, DH * (h - 8 * half):DH * (h - 8 * half + 1)],
                                    probT[ph][64 * u:64 * u + 64, hp, 32 * (2 * h2 + a):32 * (2 * h2 + a) + 32],
                                    src[64 * u:64 * u + 64, a, DH * h:DH * (h + 1)],
                                    start=True, stop=True)
                    last.then_inc(a_filled, 1)

            def transpose_qk(s):
                now = s.pair(0)
                for i in range(8):
                    a, kind, half = i // 4, (i // 2) % 2, i % 2
                    if i % 4 == 0:
                        pe.wait_ge(qk_ready, 2 * now.n + a + 1)
                    bank = fill_a(s, f"qk{i}")
                    for j in range(4):
                        col = INNER * kind + P * (4 * half + j)
                        last = nc.tensor.transpose(bank[:, P * j:P * (j + 1)], qk_rot[:, a, col:col + P], ident[:, :])
                    last.then_inc(a_filled, 1)

            def transpose_attn(s):
                for i in range(4):
                    a, half = divmod(i, 2)
                    pe.wait_ge(a_free, ring_a.at(s, f"O{2 * a + 1}")[1] + 1)
                    bank = fill_a(s, f"OT{i}")
                    for j in range(4):
                        hp = 4 * half + j
                        last = nc.tensor.transpose(bank[:, P * j:P * (j + 1)], attn[:, a, P * hp:P * (hp + 1)], ident[:, :])
                    last.then_inc(a_filled, 1)

            def score(s, ph, half):
                now = s.pair(0)
                if half == 0:
                    pe.wait_ge(a_free, ring_a.at(s, "qk7")[1] + 1)
                    n = 2 * now.n + ph
                    if not isinstance(n, int) or n >= 1:
                        pe.wait_ge(scores_used, n)
                first = now.p == 0 and ph == 0
                bank = scores[:, 4 * half:4 * half + 4, :, :]
                nc.tensor.matmul(bank, ident_b[:, :], mask[:, int(first), :, :, :], start=True, stop=False,
                                 skip_group_check=True)
                for hp in range(4 * half, 4 * half + 4):
                    for u in range(2):
                        for h2 in range(2):
                            for a in range(2):
                                win = 4 * a + 2 * u + ph
                                row = 32 * (2 * h2 + a)
                                last = nc.tensor.matmul(
                                    scores[row:row + 32, hp, u, :],
                                    qT[64 * h2:64 * h2 + 64, hp, 32 * win:32 * win + 32],
                                    kT[now.par][64 * h2:64 * h2 + 64, hp, 32 * win:32 * win + 64],
                                    start=False, stop=True, skip_group_check=True)
                if half:
                    last.then_inc(scores_ready, 1)

            def times_wo(s, pair):
                if s.p == 1:
                    pe.wait_ge(wo_in, 16 * (s.f + 1))
                pe.wait_ge(a_free, ring_a.at(s, "OT3")[1] + 1)
                bank = fill_a(s, "yT")
                for hp in range(HP):
                    last = nc.tensor.matmul(bank[:, 0:PAIR], w_o[:, hp, :], attnT[:, hp, :],
                                            start=(hp == 0), stop=(hp == HP - 1))
                last.then_inc(a_filled, 1)

            def transpose_pair(s, name, src):
                bank = fill_d(s, name)
                for a in range(2):
                    last = nc.tensor.transpose(bank[:, P * a:P * (a + 1)], src(a), ident[:, :])
                last.then_inc(d_filled, 1)

            def ffn_up(s, pair):
                if s.p == 2:
                    pe.wait_ge(wffn_in, 64 * (s.f + 1))
                pe.wait_ge(d_free, ring_d.at(s, "xn")[1] + 1)
                for name, group, lo in (("gA", (0, 1), FF), ("aA", (0, 1), 0), ("gB", (2,), FF), ("aB", (2,), 0)):
                    on_a = name[0] == "g"
                    bank = (fill_a if on_a else fill_d)(s, name)
                    for k in group:
                        first, width = FF_BLOCKS[k]
                        col = PAIR * (k - group[0])
                        last = nc.tensor.matmul(bank[0:width, col:col + PAIR], w_1[:, lo + first:lo + first + width],
                                                xnT[:, :], start=True, stop=True)
                    last.then_inc(a_filled if on_a else d_filled, 1)

            def ffn_down(s):
                pe.wait_ge(d_free, ring_d.at(s, "aB")[1] + 1)
                bank = fill_a(s, "y2T")
                for k, (first, width) in enumerate(FF_BLOCKS):
                    last = nc.tensor.matmul(bank[:, 0:PAIR], w_2[0:width, k, :], hidden[0:width, k, :],
                                            start=(k == 0), stop=(k == 2))
                last.then_inc(a_filled, 1)

            pe.wait_ge(s_init, INIT)
            transpose_x(Step(-1, POS - 1))

            def step(s):
                now, back1, back2 = s.pair(0), s.pair(1), s.pair(2)
                if runs(now):
                    project(s)
                if runs(back1):
                    transpose_probs(s, back1)
                    times_v(s, back1)
                if runs(now):
                    transpose_qk(s)
                if runs(back1):
                    transpose_attn(s)
                if runs(now):
                    score(s, 0, 0)
                    score(s, 0, 1)
                if runs(back1):
                    times_wo(s, back1)
                if runs(back2):
                    pe.wait_ge(xn_ready, back2.n + 1)
                    transpose_pair(s, "xn", lambda a: xn[:, a, :])
                if runs(back1):
                    pe.wait_ge(a_free, ring_a.at(s, "yT")[1] + 1)
                    transpose_pair(s, "y", lambda a: yT[:, P * a:P * (a + 1)])
                if runs(back2):
                    ffn_up(s, back2)
                if runs(now) and not (isinstance(s.t, int) and s.t >= PAIRS):
                    transpose_x(s)
                if runs(now):
                    score(s, 1, 0)
                if runs(back2):
                    ffn_down(s)
                if runs(now):
                    score(s, 1, 1)
                if runs(back2):
                    pe.wait_ge(a_free, ring_a.at(s, "y2T")[1] + 1)
                    transpose_pair(s, "y2", lambda a: y2T[:, P * a:P * (a + 1)])

            rounds(pe, step)

        @block.scalar
        def _(act):
            def filled(s, name):
                slot, n = ring_a.at(s, name)
                act.wait_ge(a_filled, n + 1)
                return bank_a[slot]

            def step(s):
                now, back1, back2 = s.pair(0), s.pair(1), s.pair(2)
                if runs(now):
                    for i, name in enumerate(chunks[:8]):
                        slot, n = ring_d.at(s, name)
                        act.wait_ge(d_filled, n + 1)
                        if not isinstance(now.n, int) or now.n > 0 or i >= 2:
                            m = ring_d.at(s, chunks[i - 2])[1] if i >= 2 else ring_d.at(prev(s), chunks[6 + i])[1]
                            act.wait_ge(d_free, m + 1)
                        nc.scalar.activation(sq[i % 2][:, :, :], bank_d[slot][:, :].rearrange("p (h d) -> p h d", d=DH),
                                             ACT.Square).then_inc(squared, 1)
                if runs(back1):
                    for i in range(4):
                        ph, half = divmod(i, 2)
                        bank = filled(s, f"PT{i}")
                        nc.scalar.activation(probT[ph][:, 4 * half:4 * half + 4, :], bank[:, :].rearrange("p (j t) -> p j t", t=P),
                                             ACT.Copy).then_inc(a_free, 1)
                    for i in range(4):
                        a, half = divmod(i, 2)
                        bank = filled(s, f"O{i}")
                        nc.scalar.activation(attn[:, a, 512 * half:512 * (half + 1)], bank[:, :], ACT.Copy).then_inc(a_free, 1)
                if runs(now):
                    for i in range(8):
                        a, kind, half = i // 4, (i // 2) % 2, i % 2
                        bank = filled(s, f"qk{i}")[:, :].rearrange("p (j t) -> p j t", t=P)
                        hps = slice(4 * half, 4 * half + 4)
                        if kind == 0:
                            out = qT[:, hps, P * a:P * (a + 1)]
                        else:
                            out = kT[now.par][:, hps, WINDOW + P * a:WINDOW + P * (a + 1)]
                            if a == 1:
                                nxt = kT[1 - now.par][:, hps, 0:WINDOW]
                                nc.scalar.activation(nxt, bank[:, :, P - WINDOW:P], ACT.Copy,
                                                     scale=0.0 if now.p == POS - 1 else 1.0)
                        nc.scalar.activation(out, bank, ACT.Copy).then_inc(a_free, 1)
                if runs(back1):
                    for i in range(4):
                        a, half = divmod(i, 2)
                        bank = filled(s, f"OT{i}")
                        nc.scalar.activation(attnT[:, 4 * half:4 * half + 4, P * a:P * (a + 1)],
                                             bank[:, :].rearrange("p (j t) -> p j t", t=P), ACT.Copy).then_inc(a_free, 1)
                if runs(now):
                    act.wait_ge(scores_used, 2 * now.n + 1)
                    nc.scalar.activation(prob[0][:, :, :], prob[0][:, :, :], ACT.Exp).then_inc(exp_done, 1)
                if runs(back1):
                    bank = filled(s, "yT")
                    nc.scalar.activation(yT[:, :], bank[:, 0:PAIR], ACT.Copy).then_inc(a_free, 1)
                if runs(back2):
                    if s.p == 2:
                        act.wait_ge(wffn_in, 64 * (s.f + 1))
                    for name, group in (("gA", (0, 1)), ("gB", (2,))):
                        bank = filled(s, name)
                        for k in group:
                            width = FF_BLOCKS[k][1]
                            last = nc.scalar.activation(gate[0:width, k, :], bank[0:width, PAIR * (k - group[0]):PAIR * (k - group[0] + 1)],
                                                        ACT.Gelu, bias=small[0:width, SMALL["b1g"] + k:SMALL["b1g"] + k + 1])
                        last.then_inc(a_free, 1)
                    bank = filled(s, "y2T")
                    nc.scalar.activation(y2T[:, :], bank[:, 0:PAIR], ACT.Identity,
                                         bias=small[:, SMALL["b2"]:SMALL["b2"] + 1]).then_inc(a_free, 1)
                if runs(now):
                    act.wait_ge(scores_used, 2 * now.n + 2)
                    nc.scalar.activation(prob[1][:, :, :], prob[1][:, :, :], ACT.Exp).then_inc(exp_done, 1)

            act.wait_ge(s_init, INIT)
            rounds(act, step)

        @block.vector
        def _(dve):
            links = [0]

            def link(ins):
                links[0] += 1
                ins.then_inc(v_link, 1)
                dve.wait_ge(v_link, links[0])

            def filled(s, name):
                slot, n = ring_d.at(s, name)
                dve.wait_ge(d_filled, n + 1)
                return bank_d[slot]

            def rsqrt(out, x, tmp, done):
                link(nc.vector.tensor_scalar(out.bitcast(i32), x.bitcast(i32), 1, None, ALU.logical_shift_right))
                link(nc.vector.tensor_scalar(out.bitcast(i32), out.bitcast(i32), -1.0, float(RSQRT_MAGIC), ALU.mult, ALU.add))
                for k in range(3):
                    link(nc.vector.tensor_tensor(tmp, out, out, ALU.mult))
                    link(nc.vector.scalar_tensor_tensor(tmp, tmp, -0.5, x, ALU.mult, ALU.mult))
                    ins = nc.vector.scalar_tensor_tensor(out, tmp, 1.5, out, ALU.add, ALU.mult)
                    done(ins) if k == 2 else link(ins)

            def softmax_shift(s, ph):
                n = 2 * s.pair(0).n + ph
                dve.wait_ge(scores_ready, n + 1)
                sc = scores[:, :, :, :].rearrange("p h u k -> p (h u) k")
                link(nc.vector.tensor_reduce(row_max[:, ph, :], sc, AX.X, ALU.max))
                if not isinstance(n, int) or n >= 2:
                    dve.wait_ge(a_filled, ring_a.at(s, f"PT{2 * ph + 1}")[1] + 1)
                nc.vector.tensor_tensor(prob[ph][:, :, :], sc,
                                        row_max[:, ph, :].unsqueeze(2).to_broadcast([P, HEADS, 2 * WINDOW]),
                                        ALU.subtract).then_inc(scores_used, 1)

            def softmax_sum(s, ph):
                n = 2 * s.pair(0).n + ph
                dve.wait_ge(exp_done, n + 1)
                link(nc.vector.tensor_reduce(row_sum[:, ph, :], prob[ph][:, :, :], AX.X, ALU.add))
                nc.vector.reciprocal(inv_sum[:, ph, :], row_sum[:, ph, :]).then_inc(inv_ready, 1)

            def step(s):
                now, back1, back2 = s.pair(0), s.pair(1), s.pair(2)
                if runs(now):
                    if s.p == 0:
                        dve.wait_ge(table_ready, s.f + 1)
                    for i, name in enumerate(chunks[:8]):
                        a, kind, c = name
                        bank = filled(s, name)
                        t4 = table[:, 2 * now.p + a, :, :]
                        kq = "qk".index(kind)
                        col = INNER * kq + 512 * c
                        dve.wait_ge(squared, 8 * now.n + i + 1)
                        link(nc.vector.tensor_reduce(ss[:, a, HEADS * kq + 8 * c:HEADS * kq + 8 * c + 8], sq[i % 2][:, :, :], AX.X, ALU.add))
                        if i % 4 == 0 and (not isinstance(now.n, int) or now.n > 0):
                            dve.wait_ge(qk_ready, 2 * now.n + a - 1)
                        cos = t4[:, 2 * kq, :].unsqueeze(1).to_broadcast([P, 8, DH])
                        nc.vector.tensor_tensor(by_cos[:, a, col:col + 512].rearrange("p (h d) -> p h d", d=DH),
                                                bank[:, :].rearrange("p (h d) -> p h d", d=DH), cos, ALU.mult)
                        sin = t4[:, 2 * kq + 1, :].rearrange("p (r d) -> p r d", r=2).unsqueeze(1).to_broadcast([P, 8, 2, DH // 2])
                        swapped = bank[:, :].rearrange("p (h r d) -> p h r d", r=2, d=DH // 2)[:, :, ::-1, :]
                        nc.vector.tensor_tensor(by_sin[:, a, col:col + 512].rearrange("p (h r d) -> p h r d", r=2, d=DH // 2),
                                                swapped, sin, ALU.mult).then_inc(d_free, 1)
                    if not isinstance(now.n, int) or now.n > 0:
                        dve.wait_ge(qk_ready, 2 * now.n)
                    flat = lambda z: z[:, :, :].rearrange("p a h -> p (a h)")
                    link(nc.vector.tensor_scalar(flat(ss), flat(ss), 1e-24, None, ALU.max))
                    rsqrt(flat(rnorm), flat(ss), flat(newton), lambda ins: ins.then_inc(norm_ready, 1))
                    for a, _, c in chunks[8:]:
                        bank = filled(s, (a, "v", c))
                        if (a, c) == (0, 0) and (not isinstance(now.n, int) or now.n >= 1):
                            dve.wait_ge(v_back_in[1 - now.par], 48 * (prev(s).pair(0).k + 1))
                            if not isinstance(now.n, int) or now.n >= 2:
                                dve.wait_ge(a_filled, ring_a.at(prev(s), "O3")[1] + 1)
                        nc.vector.tensor_copy(v[now.par][:, a, 512 * c:512 * (c + 1)], bank[:, :]).then_inc(d_free, 1)
                if runs(back2):
                    dve.wait_ge(xs1_in[back2.par], 32 * (back2.k + 1))
                    src = xs1[back2.par]
                    for a in range(2):
                        last = nc.vector.bn_stats(stats[:, a, :], src[:, a, :])
                    link(last)
                    for a in range(2):
                        last = nc.vector.bn_aggr(mean_var[:, a, :], stats[:, a, :])
                    link(last)
                    link(nc.vector.tensor_scalar(var_eps[:, :], mean_var[:, :, 1], 1e-5, None, ALU.add))
                    rsqrt(rstd[:, :], var_eps[:, :], nwt[:, :], link)
                    for a in range(2):
                        last = nc.vector.tensor_scalar(xn[:, a, :], src[:, a, :], mean_var[:, a, 0:1], rstd[:, a:a + 1],
                                                       ALU.subtract, ALU.mult)
                    last.then_inc(xn_ready, 1)
                if runs(now):
                    softmax_shift(s, 0)
                if runs(back2):
                    if s.p == 2:
                        dve.wait_ge(wffn_in, 64 * (s.f + 1))
                    bank = filled(s, "xn")
                    nc.vector.tensor_scalar(xnT[:, :], bank[:, 0:PAIR], small[:, SMALL["g"]:SMALL["g"] + 1],
                                            small[:, SMALL["b"]:SMALL["b"] + 1], ALU.mult, ALU.add).then_inc(d_free, 1)
                if runs(now):
                    softmax_sum(s, 0)
                if runs(back1):
                    bank = filled(s, "y")
                    dve.wait_ge(xr_in[back1.par], 16 * (back1.k + 1))
                    if not isinstance(back1.n, int) or back1.n >= 2:
                        dve.wait_ge(x1_out, 16 * (back1.n - 1))
                    nc.vector.tensor_tensor(x1[back1.par][:, :, :], bank[:, 0:PAIR].rearrange("p (a d) -> p a d", a=2),
                                            xr[back1.par][:, :, :], ALU.add).then_inc(d_free, 1)
                if runs(back2):
                    for name, group in (("aA", (0, 1)), ("aB", (2,))):
                        bank = filled(s, name)
                        dve.wait_ge(a_free, ring_a.at(s, "g" + name[1])[1] + 1)
                        for k in group:
                            width = FF_BLOCKS[k][1]
                            last = nc.vector.scalar_tensor_tensor(
                                hidden[0:width, k, :], bank[0:width, PAIR * (k - group[0]):PAIR * (k - group[0] + 1)],
                                small[0:width, SMALL["b1a"] + k:SMALL["b1a"] + k + 1], gate[0:width, k, :], ALU.add, ALU.mult)
                        last.then_inc(d_free, 1)
                if runs(now):
                    bank = filled(s, "xT")
                    nc.vector.tensor_copy(xT[:, :], bank[:, 0:PAIR]).then_inc(d_free, 1)
                    softmax_shift(s, 1)
                if runs(back2):
                    bank = filled(s, "y2")
                    if not isinstance(back2.n, int) or back2.n >= 2:
                        dve.wait_ge(x2_out, 16 * (back2.n - 1))
                    nc.vector.tensor_tensor(x2[back2.par][:, :, :], bank[:, 0:PAIR].rearrange("p (a d) -> p a d", a=2),
                                            x1[back2.par][:, :, :], ALU.add).then_inc(d_free, 1)
                if runs(now):
                    softmax_sum(s, 1)
                if s.p == POS - 1:
                    nc.vector.sem_clear(v_link)
                    links[0] = 0

            nc.vector.memset(v[1][:, :, :], 0.0)
            dve.wait_ge(s_zero, 3)
            nc.vector.tensor_copy(ident_b[:, :], ident[:, :]).then_inc(s_init, 1)
            nc.vector.memset(kT[0][:, :, 0:WINDOW], 0.0).then_inc(s_init, 1)
            bank = bank_d[0]
            dve.wait_ge(d_filled, 1)
            nc.vector.tensor_copy(xT[:, :], bank[:, 0:PAIR]).then_inc(d_free, 1)
            rounds(dve, step)


        @block.gpsimd
        def _(pool):
            links = [0]

            def link(ins):
                links[0] += 1
                ins.then_inc(p_link, 1)
                pool.wait_ge(p_link, links[0])

            nc.gpsimd.memset(ident[:, :], 0.0).then_inc(s_zero, 1)
            nc.gpsimd.memset(mask[:, :, :, :, :], 0.0).then_inc(s_zero, 1)
            pool.wait_ge(s_zero, 2)
            nc.gpsimd.affine_select(out=ident[:, :], in_=ident[:, :], compare_op=ALU.not_equal, fill=1.0, base=0,
                                    pattern=[[-1, P]], channel_multiplier=1).then_inc(s_zero, 1)
            for q in range(4):
                rows = mask[32 * q:32 * q + 32, :, :, :, :].rearrange("p m h u k -> p (m h u) k")
                for own, sign in ((0, 1), (1, -1)):
                    part = rows[:, :, WINDOW * own:WINDOW * (own + 1)]
                    link(nc.gpsimd.affine_select(out=part, in_=part, compare_op=ALU.is_ge, fill=MASKED, base=0,
                                                 pattern=[[0, 16], [sign, WINDOW]], channel_multiplier=-sign))
            for q in (0, 2):
                nc.gpsimd.memset(mask[32 * q:32 * q + 32, 1, :, 0, 0:WINDOW], MASKED).then_inc(s_init, 1)
            pool.wait_ge(s_init, INIT)

            def make_table(f):
                pool.wait_ge(qkrow_in, 16 * (f + 1))
                nc.gpsimd.tensor_tensor(table[:, :, :, :].rearrange("p t r d -> p t (r d)"),
                                        rotary[:, :, :, :].rearrange("p t r d -> p t (r d)"),
                                        qk_row[:, :, :].rearrange("p r d -> p (r d)").unsqueeze(1).to_broadcast([P, SEQ // P, 4 * DH]),
                                        ALU.mult).then_inc(table_ready, 1)

            pool.wait_ge(s_const, 16)
            make_table(0)
            def step(s):
                now = s.pair(0)
                if not runs(now):
                    return
                pool.wait_ge(norm_ready, now.n + 1)
                for a in range(2):
                    link(nc.gpsimd.tensor_tensor(by_cos[:, a, :], by_cos[:, a, :], by_sin[:, a, :], ALU.add))
                    if a == 0 and (not isinstance(now.n, int) or now.n > 0):
                        pool.wait_ge(scores_ready, 2 * now.n - 1)
                    nc.gpsimd.tensor_tensor(qk_rot[:, a, :].rearrange("p (h d) -> p h d", d=DH),
                                            by_cos[:, a, :].rearrange("p (h d) -> p h d", d=DH),
                                            rnorm[:, a, :].unsqueeze(2).to_broadcast([P, 2 * HEADS, DH]),
                                            ALU.mult).then_inc(qk_ready, 1)
                if s.p == POS - 1:
                    nf = s.f + 1
                    pool.wait_ge(qkrow_in, 16 * (nf + 1))
                    make_table(nf)
                for ph in range(2):
                    pool.wait_ge(inv_ready, 2 * now.n + ph + 1)
                    nc.gpsimd.tensor_tensor(prob[ph][:, :, :], prob[ph][:, :, :],
                                            inv_sum[:, ph, :].unsqueeze(2).to_broadcast([P, HEADS, 2 * WINDOW]),
                                            ALU.mult).then_inc(prob_ready, 1)
                if s.p == POS - 1:
                    nc.gpsimd.sem_clear(p_link)
                    links[0] = 0

            rounds(pool, step)


A_HEADS, A_KV, A_DH = 16, 4, 8
Q_RANK, KV_RANK = 64, 32
TILES = SEQ // P
HALF = SEQ // 2
PARTS = 6
SPLIT = PARTS * A_DH
Q_PART, K_PART = (0, 0, 1, 0, 1, 2), (0, 1, 0, 2, 1, 0)
NEG_UNIT, FIRST_MAX = 17, 3
MAX_UNITS = [(i, half) for i in range(TILES) for half in range(1 + (i >= 4))]
UNITS = [(qb, hpl, kt) for qb in range(2) for hpl in range(2) for kt in range(4 * qb + 4)]


def rsqrt(nc, link, out, x, tmp, last):
    link(nc.vector.tensor_scalar(out.bitcast(i32), x.bitcast(i32), 1, None, ALU.logical_shift_right))
    link(nc.vector.tensor_scalar(out.bitcast(i32), out.bitcast(i32), -1.0, float(RSQRT_MAGIC), ALU.mult, ALU.add))
    for k in range(3):
        link(nc.vector.tensor_tensor(tmp, out, out, ALU.mult))
        link(nc.vector.scalar_tensor_tensor(tmp, tmp, -0.5, x, ALU.mult, ALU.mult))
        (last if k == 2 else link)(nc.vector.scalar_tensor_tensor(out, tmp, 1.5, out, ALU.add, ALU.mult))


def maxima_at(u):
    per = 48 // (NEG_UNIT - 2 - FIRST_MAX)
    return range(48)[per * (u - FIRST_MAX):per * (u - FIRST_MAX + 1)] if u >= FIRST_MAX else range(0)


class MiscFills:

    def __init__(self):
        prep = ["xT0", "xT1", "pr0", "pr1", "kv0", "kv1", "kv2", "kv3", "tq0", "tq1", "tk", "nm"]
        self.names = [(-1, name) for name in prep]
        for g in range(A_KV):
            for u in range(len(UNITS)):
                self.names += [(g, name) for name in self.at_unit(g, u)]
            self.names.append((g, "oa1"))
        self.names += [(A_KV, name) for name in ("ao0", "ao1", "y0", "y1")]

    @staticmethod
    def at_unit(g, u):
        at = {11: "oa0"}
        if g < A_KV - 1:
            at |= {0: "tq0", 1: "tq1", 2: "tk", NEG_UNIT: "nm"}
        return [at[u]] if u in at else []

    def number(self, b, g, name):
        return len(self.names) * b + self.names.index((g, name))


def mla_attention(nc, x_in, x_dram, neg_dram, w):
    with ExitStack() as ctx:
        def sb(name, shape, dt=fp32):
            return ctx.enter_context(nc.sbuf_tensor(name, shape, dt))

        def sem(name):
            return ctx.enter_context(nc.semaphore(name))

        def psum(name, shape):
            return ctx.enter_context(nc.psum_tensor(name, shape, fp32))

        w_a = sb("w_a", [P, Q_RANK + KV_RANK])
        w_b = sb("w_b", [Q_RANK + KV_RANK, DIM + 2 * A_KV * A_DH])
        w_out = sb("w_out", [P, DIM])
        b_out = sb("b_out", [P, DIM])
        rope_q = sb("rope_q", [P, TILES, 2, DIM])
        rope_k = sb("rope_k", [P, TILES, 2, A_KV * A_DH])
        ident = sb("a_ident", [P, P])
        ident_b = sb("a_ident_b", [P, P], bf16)
        mask_q = sb("mask_q", [P, P], bf16)
        mask_k = sb("mask_k", [P, P], bf16)
        x = sb("a_x", [P, TILES, DIM])
        xr = sb("a_xr", [P, TILES, DIM])
        xT = sb("a_xT", [P, SEQ])
        latent = sb("latent", [Q_RANK + KV_RANK, SEQ])
        qkv = sb("qkv", [P, TILES, DIM + 2 * A_KV * A_DH])
        t_cos, t_sin = sb("t_cos", [P, TILES, DIM]), sb("t_sin", [P, TILES, DIM])
        q_rot = sb("q_rot", [P, TILES, DIM])
        k_cos, k_sin = sb("k_cos", [P, TILES, A_KV * A_DH]), sb("k_sin", [P, TILES, A_KV * A_DH])
        k_rot = sb("k_rot", [P, TILES, A_KV * A_DH])
        q_split = sb("q_split", [P, TILES, A_HEADS, 64], bf16)
        k_split = sb("k_split", [P, TILES, A_KV, 2, 64], bf16)
        qx = [sb(f"qx{g}", [P, 2, SEQ], bf16) for g in range(A_KV)]
        kx = [sb(f"kx{g}", [P, SEQ], bf16) for g in range(A_KV)]
        vx = [sb(f"vx{g}", [P, TILES, 32]) for g in range(A_KV)]
        part_max = sb("part_max", [P, 4, 12])
        neg = sb("neg", [P, 4, TILES])
        neg_split = sb("neg_split", [P, 2, 3, 2, TILES], bf16)
        negT = sb("negT", [96, P], bf16)
        probT = [sb(f"a_probT{i}", [P, 2, HALF]) for i in range(3)]
        accT = [sb(f"accT{i}", [P, HALF]) for i in range(2)]
        recip = sb("recip", [P, 4, 4])
        attn = sb("a_attn", [P, TILES, DIM])
        attnT = sb("a_attnT", [P, SEQ])
        z = sb("z", [P, TILES, DIM])
        stats = sb("a_stats", [P, TILES, 6])
        mean_var = sb("a_mean_var", [P, TILES, 2])
        var_eps, rstd, nwt = sb("a_var_eps", [P, TILES]), sb("a_rstd", [P, TILES]), sb("a_nwt", [P, TILES])
        y = sb("a_y", [P, TILES, DIM])

        s_max = [psum(f"s_max{i}", [P, 512]) for i in range(2)]
        s_T = [psum(f"s_T{i}", [P, 2, HALF]) for i in range(2)]
        acc = psum("acc", [P, HALF])
        misc = psum("misc", [P, 512])
        misc_b = misc[:, :].bitcast(bf16)
        fills = MiscFills()

        w_in, x_load, xr_in, y_out = sem("a_w_in"), sem("a_x_load"), sem("a_xr_in"), sem("a_y_out")
        zeroed, masked, ready = sem("a_zeroed"), sem("a_masked"), sem("a_ready")
        m_filled, m_free = sem("m_filled"), sem("m_free")
        max_filled, max_free = sem("max_filled"), sem("max_free")
        st_filled, exp_done, av_done, acc_free = sem("st_filled"), sem("a_exp_done"), sem("av_done"), sem("acc_free")
        split_ready, neg_ready = sem("split_ready"), sem("neg_ready")
        neg_out, neg_in = sem("neg_out"), sem("neg_in")
        y_ready = sem("a_y_ready")
        v_link = sem("a_v_link")
        READY = 3

        block = ctx.enter_context(nc.Block())

        def batches(eng, body):
            body(0)
            with eng.Fori(1, BATCH) as b:
                body(b)

        def later(b):
            return not isinstance(b, int) or b > 0

        @block.sync
        def _(sp):
            def load_x(b):
                sp.dma_start(x[:, :, :], x_in[bass.ds(b, 1), :, :].rearrange("one (t p) d -> p (one t) d", p=P)).then_inc(x_load, 16)

            load_x(0)
            sp.dma_start(w_a[:, 0:Q_RANK], w["Wqa"]).then_inc(w_in, 16)
            sp.dma_start(w_a[:, Q_RANK:], w["Wkva"]).then_inc(w_in, 16)
            sp.wait_ge(zeroed, 1)
            sp.dma_start(w_b[0:Q_RANK, 0:DIM], w["Wqb"]).then_inc(w_in, 16)
            sp.dma_start(w_b[Q_RANK:, DIM:], w["Wkvb"]).then_inc(w_in, 16)
            sp.dma_start(rope_q[:, :, :, :], w["rope_q"]).then_inc(w_in, 16)
            sp.dma_start(rope_k[:, :, :, :], w["rope_k"]).then_inc(w_in, 16)
            sp.dma_start(w_out[:, :], w["Wout"]).then_inc(w_in, 16)
            sp.dma_start(b_out[:, :], w["bout"].rearrange("(one d) -> one d", one=1).to_broadcast([P, DIM])).then_inc(w_in, 16)

            def neg_rows(g, G, number):
                sp.wait_ge(m_free, number + 1)
                sp.dma_start(neg_dram, negT[:, :]).then_inc(neg_out, 16)
                sp.wait_ge(neg_out, 16 * (G + 1))
                for h2 in range(2):
                    row = 64 * h2 + SPLIT
                    sp.dma_start(qx[g][row:row + 3, :, :].rearrange("r j q -> r (j q)"),
                                 neg_dram[48 * h2:48 * h2 + 48, :].rearrange("(r c) q -> r (c q)", r=3)).then_inc(neg_in, 16)

            def body(b):
                if later(b):
                    sp.wait_ge(y_ready, b)
                sp.dma_start(xr[:, :, :], x_in[bass.ds(b, 1), :, :].rearrange("one (t p) d -> p (one t) d", p=P)).then_inc(xr_in, 16)
                sp.wait_ge(m_free, fills.number(b, -1, "xT1") + 1)
                load_x((b + 1) % BATCH)
                for g in range(A_KV):
                    neg_rows(g, A_KV * b + g, fills.number(b, g - 1, "nm"))
                sp.wait_ge(y_ready, b + 1)
                sp.dma_start(x_dram[bass.ds(b, 1), 1:1 + SEQ, :].rearrange("one (t p) d -> p (one t) d", p=P), y[:, :, :]).then_inc(y_out, 16)

            batches(sp, body)
            sp.wait_ge(y_out, 16 * BATCH)
            sp.wait_ge(x_load, 16 * (BATCH + 1))

        @block.tensor
        def _(pe):
            def fill(number):
                if not isinstance(number, int) or number >= 1:
                    pe.wait_ge(m_free, number)

            def prep(num, name):
                n = num(name)
                k = int(name[-1])
                if name[:2] == "xT":
                    fill(n)
                    for t in range(4):
                        last = nc.tensor.transpose(misc[:, P * t:P * (t + 1)], x[:, 4 * k + t, :], ident[:, :])
                elif name[:2] == "pr":
                    fill(n)
                    last = nc.tensor.matmul(misc[0:Q_RANK + KV_RANK, :], w_a[:, :], xT[:, HALF * k:HALF * (k + 1)], start=True, stop=True)
                else:
                    fill(n)
                    for t in range(2):
                        tile = 2 * k + t
                        last = nc.tensor.matmul(misc[:, 192 * t:192 * (t + 1)], latent[:, P * tile:P * (tile + 1)], w_b[:, :],
                                                start=True, stop=True)
                last.then_inc(m_filled, 1)

            def transpose_split(n, g, name):
                fill(n)
                for t in range(TILES):
                    if name == "tk":
                        src = k_split[:, t, g, :, :]
                    else:
                        h = 4 * g + 2 * int(name[-1])
                        src = q_split[:, t, h:h + 2, :]
                    last = nc.tensor.transpose(misc_b[:, P * t:P * (t + 1)], src.rearrange("p a c -> p (a c)"), ident_b[:, :])
                last.then_inc(m_filled, 1)

            def max_unit(g, G, m):
                head, (i, half) = m // 12, MAX_UNITS[m % 12]
                hpl, h2 = divmod(head, 2)
                n = 48 * G + m
                if not isinstance(n, int) or n >= 2:
                    pe.wait_ge(max_free, n - 1)
                bank = s_max[m % 2]
                width = min(512, P * (i + 1) - 512 * half)
                diagonal = P * i // 512 == half
                rows = slice(64 * h2, 64 * h2 + SPLIT)
                last = nc.tensor.matmul(bank[:, 0:width], qx[g][rows, hpl, P * i:P * (i + 1)],
                                        kx[g][rows, 512 * half:512 * half + width],
                                        start=True, stop=not diagonal, skip_group_check=True)
                if diagonal:
                    last = nc.tensor.matmul(bank[:, width - P:width], ident_b[:, :], mask_q[:, :], start=False, stop=True,
                                            skip_group_check=True)
                last.then_inc(max_filled, 1)

            def transposed_scores(g, G, u):
                qb, hpl, kt = UNITS[u]
                n = 24 * G + u
                if not isinstance(n, int) or n >= 2:
                    pe.wait_ge(exp_done, n - 1)
                lo = max(0, P * (kt - 4 * qb))
                diagonal = kt >= 4 * qb
                for h2 in range(2):
                    bank = s_T[u % 2][:, h2, :]
                    rows = slice(64 * h2, 64 * h2 + SPLIT + 3)
                    last = nc.tensor.matmul(bank[:, lo:HALF], kx[g][rows, P * kt:P * (kt + 1)],
                                            qx[g][rows, hpl, HALF * qb + lo:HALF * (qb + 1)],
                                            start=True, stop=not diagonal, skip_group_check=True)
                    if diagonal:
                        last = nc.tensor.matmul(bank[:, lo:lo + P], ident_b[:, :], mask_k[:, :], start=False, stop=True,
                                                skip_group_check=True)
                last.then_inc(st_filled, 1)

            def times_v(g, G, u):
                qb, hpl, kt = UNITS[u]
                pe.wait_ge(exp_done, 24 * G + u + 1)
                if kt == 0 and hpl == 0:
                    n = 2 * G + qb
                    if not isinstance(n, int) or n >= 1:
                        pe.wait_ge(acc_free, n)
                lo = max(0, P * (kt - 4 * qb))
                for h2 in range(2):
                    q = 32 * (2 * hpl + h2)
                    last = nc.tensor.matmul(acc[q:q + 32, lo:HALF], vx[g][:, kt, :], probT[u % 3][:, h2, lo:HALF],
                                            start=(kt == 0), stop=(kt == 4 * qb + 3), skip_group_check=True)
                last.then_inc(av_done, 1)

            def transpose_max(n):
                fill(n)
                nc.tensor.transpose(misc_b[0:96, 0:P], neg_split[:, :, :, :, :].rearrange("p a r j i -> p (a r j i)"),
                                    ident_b[:, :]).then_inc(m_filled, 1)

            def transpose_acc(n, qb):
                fill(n)
                for t in range(4):
                    last = nc.tensor.transpose(misc[:, P * t:P * (t + 1)], accT[qb][:, P * t:P * (t + 1)], ident[:, :])
                last.then_inc(m_filled, 1)

            pe.wait_ge(ready, READY)
            pe.wait_ge(w_in, 16 * 8)

            def body(b):
                num = lambda name: fills.number(b, -1, name)
                pe.wait_ge(x_load, 16 * (b + 1))
                for name in ("xT0", "xT1", "pr0", "pr1", "kv0", "kv1", "kv2", "kv3"):
                    prep(num, name)
                pe.wait_ge(split_ready, b + 1)
                for name in ("tq0", "tq1", "tk"):
                    transpose_split(num(name), 0, name)
                pe.wait_ge(m_free, num("tk") + 1)
                for m in range(48):
                    max_unit(0, A_KV * b, m)
                pe.wait_ge(neg_ready, A_KV * b + 1)
                transpose_max(num("nm"))
                for g in range(A_KV):
                    attend(b, g)
                num = lambda name: fills.number(b, A_KV, name)
                for k in range(2):
                    fill(num(f"ao{k}"))
                    for t in range(4):
                        last_t = nc.tensor.transpose(misc[:, P * t:P * (t + 1)], attn[:, 4 * k + t, :], ident[:, :])
                    last_t.then_inc(m_filled, 1)
                for k in range(2):
                    fill(num(f"y{k}"))
                    for t in range(4):
                        tile = 4 * k + t
                        last_t = nc.tensor.matmul(misc[:, P * t:P * (t + 1)], attnT[:, P * tile:P * (tile + 1)], w_out[:, :],
                                                  start=True, stop=True)
                    last_t.then_inc(m_filled, 1)

            def attend(b, g):
                G = A_KV * b + g
                num = lambda name: fills.number(b, g, name)
                pe.wait_ge(neg_in, 32 * (G + 1))
                transposed_scores(g, G, 0)
                m = 0
                for u in range(len(UNITS)):
                    if u + 1 < len(UNITS):
                        transposed_scores(g, G, u + 1)
                    for name in fills.at_unit(g, u):
                        if name == "oa0":
                            pe.wait_ge(acc_free, 2 * G + 1)
                            transpose_acc(num(name), 0)
                        elif name == "nm":
                            pe.wait_ge(neg_ready, G + 2)
                            transpose_max(num(name))
                        else:
                            transpose_split(num(name), g + 1, name)
                    if g < A_KV - 1 and u >= FIRST_MAX:
                        if u == FIRST_MAX:
                            pe.wait_ge(m_free, num("tk") + 1)
                        for m in maxima_at(u):
                            max_unit(g + 1, G + 1, m)
                    times_v(g, G, u)
                pe.wait_ge(acc_free, 2 * G + 2)
                transpose_acc(num("oa1"), 1)

            batches(pe, body)

        @block.scalar
        def _(act):
            def filled(n):
                act.wait_ge(m_filled, n + 1)

            def prep(num, name):
                filled(num(name))
                k = int(name[-1])
                if name[:2] == "xT":
                    nc.scalar.activation(xT[:, HALF * k:HALF * (k + 1)], misc[:, :], ACT.Copy).then_inc(m_free, 1)
                elif name[:2] == "pr":
                    r = Q_RANK + KV_RANK
                    nc.scalar.activation(latent[:, HALF * k:HALF * (k + 1)], misc[0:r, :], ACT.Copy).then_inc(m_free, 1)
                else:
                    nc.scalar.activation(qkv[:, 2 * k:2 * k + 2, :], misc[:, 0:384].rearrange("p (t c) -> p t c", t=2),
                                         ACT.Copy).then_inc(m_free, 1)

            def split_out(n, g, name):
                filled(n)
                out = kx[g][:, :] if name == "tk" else qx[g][:, int(name[-1]), :]
                nc.scalar.activation(out, misc_b, ACT.Copy).then_inc(m_free, 1)

            def neg_evacuate(n):
                filled(n)
                nc.scalar.activation(negT[:, :], misc_b[0:96, 0:P], ACT.Copy).then_inc(m_free, 1)

            def body(b):
                num = lambda name: fills.number(b, -1, name)
                for name in ("xT0", "xT1", "pr0", "pr1", "kv0", "kv1", "kv2", "kv3"):
                    prep(num, name)
                for name in ("tq0", "tq1", "tk"):
                    split_out(num(name), 0, name)
                neg_evacuate(num("nm"))
                for g in range(A_KV):
                    G = A_KV * b + g
                    num = lambda name: fills.number(b, g, name)
                    for u, (qb, hpl, kt) in enumerate(UNITS):
                        n = 24 * G + u
                        act.wait_ge(st_filled, n + 1)
                        if not isinstance(n, int) or n >= 3:
                            act.wait_ge(av_done, n - 2)
                        lo = max(0, P * (kt - 4 * qb))
                        nc.scalar.activation(probT[u % 3][:, :, lo:HALF], s_T[u % 2][:, :, lo:HALF], ACT.Exp).then_inc(exp_done, 1)
                        if u == 8:
                            evacuate(G, 0)
                        for name in fills.at_unit(g, u):
                            if name == "nm":
                                neg_evacuate(num(name))
                            elif name != "oa0":
                                split_out(num(name), g + 1, name)
                    evacuate(G, 1)
                for k in range(2):
                    filled(fills.number(b, A_KV, f"ao{k}"))
                    nc.scalar.activation(attnT[:, HALF * k:HALF * (k + 1)], misc[:, :], ACT.Copy).then_inc(m_free, 1)

            def evacuate(G, qb):
                act.wait_ge(av_done, 24 * G + (24 if qb else 8))
                nc.scalar.activation(accT[qb][:, :], acc[:, :], ACT.Copy).then_inc(acc_free, 1)

            batches(act, body)

        @block.vector
        def _(dve):
            links = [0]

            def link(ins):
                links[0] += 1
                ins.then_inc(v_link, 1)
                dve.wait_ge(v_link, links[0])

            def rope():
                q_in = qkv[:, :, 0:DIM]
                nc.vector.tensor_tensor(t_cos[:, :, :], q_in, rope_q[:, :, 0, :], ALU.mult)
                nc.vector.tensor_tensor(t_sin[:, :, :].rearrange("p t (c r) -> p t c r", r=2),
                                        q_in.rearrange("p t (c r) -> p t c r", r=2)[:, :, :, ::-1],
                                        rope_q[:, :, 1, :].rearrange("p t (c r) -> p t c r", r=2), ALU.mult)
                k_in = qkv[:, :, DIM:].rearrange("p t (c r v) -> p t c r v", r=2, v=2)[:, :, :, :, 0]
                nc.vector.tensor_tensor(k_cos[:, :, :].rearrange("p t (c r) -> p t c r", r=2), k_in,
                                        rope_k[:, :, 0, :].rearrange("p t (c r) -> p t c r", r=2), ALU.mult)
                link(nc.vector.tensor_tensor(k_sin[:, :, :].rearrange("p t (c r) -> p t c r", r=2), k_in[:, :, :, ::-1],
                                             rope_k[:, :, 1, :].rearrange("p t (c r) -> p t c r", r=2), ALU.mult))
                nc.vector.tensor_tensor(q_rot[:, :, :], t_cos[:, :, :], t_sin[:, :, :], ALU.add)
                link(nc.vector.tensor_tensor(k_rot[:, :, :], k_cos[:, :, :], k_sin[:, :, :], ALU.add))

            def split():
                qs = [q_split[:, :, :, A_DH * j:A_DH * (j + 1)] for j in range(PARTS)]
                ks = [[k_split[:, :, :, d, A_DH * j:A_DH * (j + 1)] for d in range(2)] for j in range(PARTS)]
                q_f = q_rot[:, :, :].rearrange("p t (h d) -> p t h d", d=A_DH)
                k_f = k_rot[:, :, :].rearrange("p t (h d) -> p t h d", d=A_DH)
                for part in range(3):
                    mine_q = [j for j in range(PARTS) if Q_PART[j] == part]
                    mine_k = [j for j in range(PARTS) if K_PART[j] == part]
                    nc.vector.tensor_copy(qs[mine_q[0]], q_f)
                    link(nc.vector.tensor_copy(ks[mine_k[0]][0], k_f))
                    if part < 2:
                        nc.vector.tensor_tensor(q_f, q_f, qs[mine_q[0]], ALU.subtract)
                        nc.vector.tensor_tensor(k_f, k_f, ks[mine_k[0]][0], ALU.subtract)
                    for j in mine_q[1:]:
                        nc.vector.tensor_copy(qs[j], qs[mine_q[0]])
                    for j in mine_k:
                        for d in range(2):
                            if (j, d) != (mine_k[0], 0):
                                last = nc.vector.tensor_copy(ks[j][d], ks[mine_k[0]][0])
                    if part < 2:
                        link(last)
                last.then_inc(split_ready, 1)

            def copy_v(g):
                v_in = qkv[:, :, DIM + 16 * g:DIM + 16 * (g + 1)].rearrange("p t (d v) -> p t d v", v=2)[:, :, :, 1]
                nc.vector.tensor_copy(vx[g][:, :, 0:A_DH], v_in)

            def reduce_unit(G, m):
                head, (i, half) = m // 12, MAX_UNITS[m % 12]
                n = 48 * G + m
                dve.wait_ge(max_filled, n + 1)
                width = min(512, P * (i + 1) - 512 * half)
                col = i + 4 * half
                nc.vector.tensor_reduce(part_max[:, head, col:col + 1], s_max[m % 2][:, 0:width], AX.X, ALU.max).then_inc(max_free, 1)

            def split_max(G):
                dve.wait_ge(max_free, 48 * (G + 1))
                link(nc.vector.tensor_tensor(part_max[:, :, 4:8], part_max[:, :, 4:8], part_max[:, :, 8:12], ALU.max))
                link(nc.vector.tensor_scalar(neg[:, :, :], part_max[:, :, 0:8], -1.0, None, ALU.mult))
                rest = neg[:, :, :].rearrange("p (j a) i -> p j a i", a=2)
                for r in range(3):
                    part = neg_split[:, :, r, :, :].rearrange("p a j i -> p j a i")
                    ins = nc.vector.tensor_copy(part, rest)
                    if r == 2:
                        ins.then_inc(neg_ready, 1)
                    else:
                        link(ins)
                        link(nc.vector.tensor_tensor(rest, rest, part, ALU.subtract))

            def normalise(g, qb, n):
                dve.wait_ge(m_filled, n + 1)
                heads = misc[:, :].rearrange("p (t h c) -> p t h c", t=4, c=32)
                link(nc.vector.reciprocal(recip[:, :, :], heads[:, :, :, A_DH]))
                nc.vector.tensor_tensor(
                    attn[:, 4 * qb:4 * qb + 4, 32 * g:32 * (g + 1)].rearrange("p t (h d) -> p t h d", d=A_DH),
                    heads[:, :, :, 0:A_DH], recip[:, :, :].unsqueeze(3).to_broadcast([P, 4, 4, A_DH]), ALU.mult).then_inc(m_free, 1)

            nc.vector.memset(w_b[:, :], 0.0).then_inc(zeroed, 1)
            nc.vector.memset(q_split[:, :, :, :], 0.0)
            nc.vector.memset(k_split[:, :, :, :, :], 0.0)
            for g in range(A_KV):
                nc.vector.memset(vx[g][:, :, :], 0.0)
            link(nc.vector.memset(recip[:, :, :], 0.0))
            for g in range(A_KV):
                nc.vector.memset(vx[g][:, :, A_DH:A_DH + 1], 1.0)
            nc.vector.memset(k_split[:, :, :, :, SPLIT:SPLIT + 3], 1.0).then_inc(ready, 1)
            dve.wait_ge(masked, 3)
            link(nc.vector.tensor_copy(ident_b[:, :], ident[:, :]))
            nc.vector.memset(recip[:, :, :], 0.0).then_inc(ready, 1)

            dve.wait_ge(w_in, 16 * 8)

            def body(b):
                dve.wait_ge(m_free, fills.number(b, -1, "kv3") + 1)
                rope()
                for g in range(A_KV):
                    copy_v(g)
                split()
                for m in range(48):
                    reduce_unit(A_KV * b, m)
                split_max(A_KV * b)
                for g in range(A_KV):
                    G = A_KV * b + g
                    for u in range(len(UNITS)):
                        if u == 11:
                            normalise(g, 0, fills.number(b, g, "oa0"))
                        if g < A_KV - 1:
                            for m in maxima_at(u):
                                reduce_unit(G + 1, m)
                                if m == 47:
                                    split_max(G + 1)
                    normalise(g, 1, fills.number(b, g, "oa1"))
                dve.wait_ge(xr_in, 16 * (b + 1))
                for k in range(2):
                    dve.wait_ge(m_filled, fills.number(b, A_KV, f"y{k}") + 1)
                    nc.vector.tensor_tensor(z[:, 4 * k:4 * k + 4, :], misc[:, :].rearrange("p (t d) -> p t d", t=4),
                                            xr[:, 4 * k:4 * k + 4, :], ALU.add).then_inc(m_free, 1)
                dve.wait_ge(m_free, fills.number(b, A_KV, "y1") + 1)
                link(nc.vector.tensor_tensor(z[:, :, :], z[:, :, :], b_out[:, :].unsqueeze(1).to_broadcast([P, TILES, DIM]), ALU.add))
                if later(b):
                    dve.wait_ge(y_out, 16 * b)
                layer_norm(nc, link, z, y, TILES, stats, mean_var, var_eps, rstd, nwt, lambda ins: ins.then_inc(y_ready, 1))
                nc.vector.sem_clear(v_link)
                links[0] = 0

            nc.vector.sem_clear(v_link)
            links[0] = 0
            batches(dve, body)

        @block.gpsimd
        def _(pool):
            nc.gpsimd.memset(ident[:, :], 0.0).then_inc(masked, 1)
            nc.gpsimd.memset(mask_q[:, :], 0.0).then_inc(masked, 1)
            pool.wait_ge(masked, 2)
            nc.gpsimd.affine_select(out=ident[:, :], in_=ident[:, :], compare_op=ALU.not_equal, fill=1.0, base=0,
                                    pattern=[[-1, P]], channel_multiplier=1).then_inc(masked, 1)
            nc.gpsimd.affine_select(out=mask_k[:, :], in_=mask_q[:, :], compare_op=ALU.is_ge, fill=MASKED, base=0,
                                    pattern=[[1, P]], channel_multiplier=-1).then_inc(masked, 1)
            pool.wait_ge(masked, 4)
            nc.gpsimd.affine_select(out=mask_q[:, :], in_=mask_q[:, :], compare_op=ALU.is_ge, fill=MASKED, base=0,
                                    pattern=[[-1, P]], channel_multiplier=1).then_inc(ready, 1)


def layer_norm(nc, link, src, out, tiles, stats, mean_var, var_eps, rstd, tmp, last):
    for t in range(tiles):
        ins = nc.vector.bn_stats(stats[:, t, :], src[:, t, :])
    link(ins)
    for t in range(tiles):
        ins = nc.vector.bn_aggr(mean_var[:, t, :], stats[:, t, :])
    link(ins)
    link(nc.vector.tensor_scalar(var_eps[:, 0:tiles], mean_var[:, 0:tiles, 1], 1e-5, None, ALU.add))
    rsqrt(nc, link, rstd[:, 0:tiles], var_eps[:, 0:tiles], tmp[:, 0:tiles], link)
    for t in range(tiles):
        ins = nc.vector.tensor_scalar(out[:, t, :], src[:, t, :], mean_var[:, t, 0:1], rstd[:, t:t + 1], ALU.subtract, ALU.mult)
    last(ins)


def closing_norm(nc, x_dram, out):
    with ExitStack() as ctx:
        def sb(name, shape, dt=fp32):
            return ctx.enter_context(nc.sbuf_tensor(name, shape, dt))

        def sem(name):
            return ctx.enter_context(nc.semaphore(name))

        x_first = [sb(f"x_first{b}", [P, TILES, DIM]) for b in range(BATCH)]
        x_last = [sb(f"x_last{b}", [P, TILES, DIM]) for b in range(BATCH)]
        normed = [sb(f"normed{b}", [P, TILES, DIM]) for b in range(BATCH)]
        stats = sb("c_stats", [P, TILES, 6])
        mean_var = sb("c_mean_var", [P, TILES, 2])
        var_eps, rstd, nwt = (sb(f"c_{n}", [P, TILES]) for n in ("var_eps", "rstd", "nwt"))
        loaded = [sem(f"c_loaded{b}") for b in range(BATCH)]
        norm_done, stored, v_link = sem("c_norm_done"), sem("c_stored"), sem("c_v_link")
        block = ctx.enter_context(nc.Block())

        def tiled(rows):
            return rows.rearrange("(t p) d -> p t d", p=P)

        @block.sync
        def _(sp):
            for b in range(BATCH):
                sp.dma_start(x_first[b][:, :, :], tiled(x_dram[b, 1:1 + SEQ, :])).then_inc(loaded[b], 16)
                sp.dma_start(x_last[b][:, :, :], tiled(x_dram[ROUNDS + b, 1:1 + SEQ, :])).then_inc(loaded[b], 16)
            for b in range(BATCH):
                sp.wait_ge(norm_done, b + 1)
                sp.dma_start(tiled(out[b, :, :]), normed[b][:, :, :]).then_inc(stored, 16)
            sp.wait_ge(stored, 16 * BATCH)

        @block.vector
        def _(dve):
            links = [0]

            def link(ins):
                links[0] += 1
                ins.then_inc(v_link, 1)
                dve.wait_ge(v_link, links[0])

            for b in range(BATCH):
                dve.wait_ge(loaded[b], 32)
                link(nc.vector.tensor_tensor(x_first[b][:, :, :], x_first[b][:, :, :], x_last[b][:, :, :], ALU.add))
                layer_norm(nc, link, x_first[b], normed[b], TILES, stats, mean_var, var_eps, rstd, nwt,
                           lambda ins: ins.then_inc(norm_done, 1))


def clear_first_rows(nc, x_dram, x1_dram):
    with ExitStack() as ctx:
        zeros = ctx.enter_context(nc.sbuf_tensor("zeros", [P, DIM], fp32))
        zeroed, rows_out = ctx.enter_context(nc.semaphore("zeroed")), ctx.enter_context(nc.semaphore("rows_out"))
        block = ctx.enter_context(nc.Block())

        @block.vector
        def _(dve):
            nc.vector.memset(zeros[:, :], 0.0).then_inc(zeroed, 1)

        @block.sync
        def _(sp):
            sp.wait_ge(zeroed, 1)
            sp.dma_start(x_dram[:, 0, :], zeros[0:ROUNDS + BATCH, :]).then_inc(rows_out, 16)
            sp.dma_start(x1_dram[0:1, :], zeros[0:1, :]).then_inc(rows_out, 16)
            sp.wait_ge(rows_out, 32)


def build(nc, w, out):
    x_dram = nc.dram_tensor("x_layers", [ROUNDS + BATCH, 1 + SEQ, DIM], fp32, kind="Internal").ap()
    x1_dram = nc.dram_tensor("x1", [1 + SEQ, DIM], fp32, kind="Internal").ap()
    neg_dram = nc.dram_tensor("neg_max", [96, P], bf16, kind="Internal").ap()
    clear_first_rows(nc, x_dram, x1_dram)
    mla_attention(nc, w["x"], x_dram, neg_dram, w)
    local_layers(nc, x_dram, x1_dram, w)
    closing_norm(nc, x_dram, out)



def rope_tables(np):
    D = A_DH
    inv_freq = 1.0 / 10000.0 ** (np.arange(0, D, 2, dtype=np.float32) / np.float32(D))
    freqs = (np.arange(SEQ, dtype=np.float32)[:, None] * inv_freq.astype(np.float32)[None, :]).astype(np.float64)
    cos = np.repeat(np.cos(freqs), 2, axis=1)
    sin = np.repeat(np.sin(freqs), 2, axis=1) * np.where(np.arange(D) % 2, 1.0, -1.0)
    tables = []
    for heads, scale in ((A_HEADS, D ** -0.5), (A_KV, 1.0)):
        both = np.stack([np.tile(cos, (1, heads)), np.tile(sin, (1, heads))], 1) * scale
        both = both.reshape(TILES, P, 2, heads * D).transpose(1, 0, 2, 3)
        tables.append(np.ascontiguousarray(both.astype(np.float32)))
    return tables


def rotary_table(np):
    half = np.arange(0, DH, 2, dtype=np.float32)
    inv_freq = (1.0 / np.power(np.float32(10000.0), half / np.float32(DH))).astype(np.float32)
    t = np.arange(SEQ, dtype=np.float32)
    freqs = (t[:, None] * inv_freq[None, :]).astype(np.float64)
    freqs = np.concatenate([freqs, freqs], -1)
    base_scale = ((half + np.float32(0.4 * DH)) / np.float32(1.4 * DH)).astype(np.float64)
    power = ((t - SEQ // 2) / (WINDOW // 2)).astype(np.float64)
    scale = base_scale[None, :] ** power[:, None]
    scale = np.concatenate([scale, scale], -1)
    cos, sin = np.cos(freqs), np.sin(freqs) * np.where(np.arange(DH) < DH // 2, -1.0, 1.0)
    rows = np.stack([cos * scale * QK_SCALE, sin * scale * QK_SCALE, cos / scale, sin / scale], 1)
    return np.ascontiguousarray(rows.reshape(TILES, P, 4, DH).transpose(1, 0, 2, 3).astype(np.float32))


def pack_vectors(np, a):
    def swap(v):
        return np.concatenate([v[:, DH // 2:], v[:, :DH // 2]], 1)

    qs, ks = a["L0_ffn_q_scale"], a["L0_ffn_k_scale"]
    qk_rows = np.concatenate([qs, swap(qs), ks, swap(ks)], 1)
    small = np.zeros((DEPTH, P, N_SMALL), np.float32)
    small[:, :, SMALL["g"]], small[:, :, SMALL["b"]] = a["L0_ffn_ln_g"], a["L0_ffn_ln_b"]
    for k, (first, width) in enumerate(FF_BLOCKS):
        small[:, :width, SMALL["b1a"] + k] = a["L0_ffn_b1"][:, first:first + width]
        small[:, :width, SMALL["b1g"] + k] = a["L0_ffn_b1"][:, FF + first:FF + first + width]
    small[:, :, SMALL["b2"]] = a["L0_ffn_b2"]
    return np.ascontiguousarray(qk_rows), small


def kernel(**inputs):
    import numpy as np
    import concourse.bacc as bacc
    from concourse.bass_utils import run_bass_kernel_spmd

    nc = bacc.Bacc("TRN2", target_bir_lowering=False, num_devices=1)
    a = {name: np.ascontiguousarray(value) for name, value in inputs.items()}
    rope_q, rope_k = rope_tables(np)
    qk_rows, small = pack_vectors(np, a)
    tensors = dict(x=a["L0_attn_x"], Wqa=a["L0_attn_Wqa"], Wqb=a["L0_attn_Wqb"], Wkva=a["L0_attn_Wkva"],
                   Wkvb=a["L0_attn_Wkvb"], Wout=a["L0_attn_Wout"], bout=a["L0_attn_bout"], rope_q=rope_q, rope_k=rope_k,
                   Wqkv=a["L0_ffn_Wqkv"], Wo=a["L0_ffn_Wo"], W1=a["L0_ffn_W1"], W2=a["L0_ffn_W2"],
                   qk_rows=qk_rows, small=small, rotary=rotary_table(np))
    arrays = {f"in_{name}_dram": value for name, value in tensors.items()}
    w = {name: nc.dram_tensor(f"in_{name}_dram", value.shape, fp32, kind="ExternalInput").ap()
         for name, value in tensors.items()}
    out = nc.dram_tensor("out_dram", (BATCH, SEQ, DIM), fp32, kind="ExternalOutput").ap()
    build(nc, w, out)
    return run_bass_kernel_spmd(nc, [arrays], core_ids=[0]).results[0]["out_dram"]
```

```python
import concourse.bass as bass
from concourse import mybir
from contextlib import ExitStack

fp32 = mybir.dt.float32
bf16 = mybir.dt.bfloat16
i32 = mybir.dt.int32
ALU = mybir.AluOpType
ACT = mybir.ActivationFunctionType
AX = mybir.AxisListType

P = 128
BATCH, SEQ, DIM = 4, 1024, 128
MASKED = -1e30

DEPTH, HEADS, DH, WINDOW = 6, 16, 64, 32
INNER = HEADS * DH
FF = DIM * 4 * 2 // 3
FF_BLOCKS = [(0, 128), (128, 128), (256, FF - 256)]
QK_SCALE = 8.0
PAIR = 2 * P
POS = SEQ // PAIR
ROUNDS = DEPTH * BATCH
PAIRS = ROUNDS * POS
HP = HEADS // 2
RSQRT_MAGIC = 0x5F3759DF

SMALL = dict(g=0, b=1, b1a=2, b1g=5, b2=8)
N_SMALL = 9


class Ring:

    def __init__(self, stage_names):
        self.stage_names = stage_names
        self.full = len(stage_names)
        assert self.full % 3 == 0

    def names(self, t):
        return [s for s, lag in self.stage_names if not isinstance(t, int) or 0 <= t - lag < PAIRS]

    def before(self, t):
        early = [len(self.names(s)) for s in (-1, 0, 1)]
        if isinstance(t, int) and t < 2:
            return sum(early[:t + 1])
        if isinstance(t, int) and t > PAIRS:
            return self.before(t - 1) + len(self.names(t - 1))
        return self.full * t + (sum(early) - 2 * self.full)

    def at(self, step, name):
        early = sum(len(self.names(s)) for s in (-1, 0, 1))
        j = self.names(step.t).index(name)
        b = self.before(step.t)
        number = b + j
        slot = (number if isinstance(b, int) else early - 2 * self.full + j) % 3
        return slot, number


class Step:

    def __init__(self, f, p):
        self.f, self.p = f, p
        self.t = POS * f + p

    def pair(self, lag):
        return Pair(self, lag)


class Pair:

    def __init__(self, step, lag):
        self.step, self.lag = step, lag
        q = step.p - lag
        self.p = q % POS
        self.f = step.f + q // POS
        self.n = step.t - lag
        self.par = self.p % 2
        self.k = 2 * self.f + self.p // 2
        self.exists = not isinstance(self.n, int) or 0 <= self.n < PAIRS


def layer_of(f):
    return (f // BATCH) % DEPTH


def dram_rows(region, f, row, count):
    return region[bass.ds(f, 1), row:row + count, :].rearrange("one t d -> (one t) d")


def local_layers(nc, x_dram, x1_dram, w):
    with ExitStack() as ctx:
        def sb(name, shape, dt=fp32):
            return ctx.enter_context(nc.sbuf_tensor(name, shape, dt))

        def sem(name):
            return ctx.enter_context(nc.semaphore(name))

        w_qkv = sb("w_qkv", [P, 3 * INNER])
        w_o = sb("w_o", [P, HP, DIM])
        w_1 = sb("w_1", [P, 2 * FF])
        w_2 = sb("w_2", [P, 3, DIM])
        small = sb("small", [P, N_SMALL])
        qk_row = sb("qk_row", [P, 4, DH])
        rotary = sb("rotary", [P, SEQ // P, 4, DH])
        table = sb("table", [P, SEQ // P, 4, DH])
        ident = sb("ident", [P, P])
        ident_b = sb("ident_b", [P, P], bf16)
        mask = sb("mask", [P, 2, 4, 2, 2 * WINDOW], bf16)
        xs = [sb(f"xs{i}", [P, 2, DIM]) for i in range(2)]
        xr = [sb(f"xr{i}", [P, 2, DIM]) for i in range(2)]
        xs1 = [sb(f"xs1{i}", [P, 2, DIM]) for i in range(2)]
        x1 = [sb(f"x1{i}", [P, 2, DIM]) for i in range(2)]
        x2 = [sb(f"x2{i}", [P, 2, DIM]) for i in range(2)]
        xT = sb("xT", [P, PAIR])
        sq = [sb(f"sq{i}", [P, 8, DH]) for i in range(2)]
        by_cos = sb("by_cos", [P, 2, 2 * INNER])
        by_sin = sb("by_sin", [P, 2, 2 * INNER])
        qk_rot = sb("qk_rot", [P, 2, 2 * INNER])
        ss = sb("ss", [P, 2, 2 * HEADS + 2])
        rnorm = sb("rnorm", [P, 2, 2 * HEADS + 2])
        newton = sb("newton", [P, 2 * HEADS + 2])
        v = [sb(f"v{i}", [P, 2, INNER]) for i in range(2)]
        v_back = [sb(f"v_back{i}", [P, 2, INNER]) for i in range(2)]
        qT = sb("qT", [P, HP, PAIR])
        kT = [sb(f"kT{i}", [P, HP, WINDOW + PAIR]) for i in range(2)]
        prob = [sb(f"prob{i}", [P, HEADS, 2 * WINDOW]) for i in range(2)]
        row_max = sb("row_max", [P, 2, HEADS])
        row_sum = sb("row_sum", [P, 2, HEADS])
        inv_sum = sb("inv_sum", [P, 2, HEADS])
        probT = [sb(f"probT{i}", [P, HP, P]) for i in range(2)]
        attn = sb("attn", [P, 2, INNER])
        attnT = sb("attnT", [P, HP, PAIR])
        yT = sb("yT", [P, PAIR])
        y2T = sb("y2T", [P, PAIR])
        stats = sb("stats", [P, 2, 6])
        mean_var = sb("mean_var", [P, 2, 2])
        xn = sb("xn", [P, 2, DIM])
        xnT = sb("xnT", [P, PAIR])
        gate = sb("gate", [P, 3, PAIR])
        hidden = sb("hidden", [P, 3, PAIR])

        bank_d = [ctx.enter_context(nc.psum_tensor(f"bank_d{i}", [P, 512], fp32)) for i in range(3)]
        scores = ctx.enter_context(nc.psum_tensor("scores", [P, HP, 2, 2 * WINDOW], fp32))
        bank_a = [ctx.enter_context(nc.psum_tensor(f"bank_a{i}", [P, 512], fp32)) for i in range(3)]

        chunks = [(a, kind, c) for a in range(2) for kind in "qk" for c in range(2)]
        chunks += [(a, "v", c) for a in range(2) for c in range(2)]
        qk_chunks, v_chunks = chunks[:8], chunks[8:]
        EARLY = 3
        early, late = [(x, -1) for x in qk_chunks[:EARLY]], [(x, 0) for x in qk_chunks[EARLY:]]
        ring_d = Ring(late + [("xn", 2), (v_chunks[0], 0), ("aA", 2), ("aB", 2)] + [(x, 0) for x in v_chunks[1:]]
                      + [("xT", -1)] + early + [("y2", 2), ("y", 1)])
        ring_a = Ring([(f"qk{i}", 1) for i in range(8)]
                      + [("PT0", 1), ("PT1", 1), ("gA", 2), ("gB", 2), ("PT2", 1), ("PT3", 1)]
                      + [("O0", 1), ("O2", 1), ("O1", 1), ("OT0", 1), ("O3", 1), ("OT2", 1), ("y2T", 2)]
                      + [("OT1", 1), ("OT3", 1), ("yT", 1)])

        s_init = sem("s_init")
        s_const = sem("s_const")
        s_zero = sem("s_zero")
        xs_in = [sem(f"xs_in{i}") for i in range(2)]
        xr_in = [sem(f"xr_in{i}") for i in range(2)]
        xs1_in = [sem(f"xs1_in{i}") for i in range(2)]
        v_back_in = [sem(f"v_back_in{i}") for i in range(2)]
        x1_out, x2_out = sem("x1_out"), sem("x2_out")
        wqk_in, wv_in, wo_in, wffn_in, qkrow_in = sem("wqk_in"), sem("wv_in"), sem("wo_in"), sem("wffn_in"), sem("qkrow_in")
        d_filled, d_free = sem("d_filled"), sem("d_free")
        a_filled, a_free = sem("a_filled"), sem("a_free")
        squared = sem("squared")
        norm_ready = sem("norm_ready")
        qk_ready = sem("qk_ready")
        table_ready = sem("table_ready")
        scores_ready, scores_used = sem("scores_ready"), sem("scores_used")
        maximum = sem("maximum")
        exp_done, inv_ready, prob_ready = sem("exp_done"), sem("inv_ready"), sem("prob_ready")
        xn_ready = sem("xn_ready")
        v_link = sem("v_link")
        p_link = sem("p_link")

        INIT = 4
        block = ctx.enter_context(nc.Block())

        def rounds(eng, step_fn, last_fn=None):
            for p in range(POS):
                step_fn(Step(0, p))
            with eng.Fori(1, ROUNDS) as f:
                for p in range(POS):
                    step_fn(Step(f, p))
            for t in (PAIRS, PAIRS + 1):
                step_fn(Step(ROUNDS, t - PAIRS))

        def prev(s):
            return Step(s.f, s.p - 1) if s.p else Step(s.f - 1, POS - 1)

        def chunk_at(pair, i):
            s = pair.step
            if i < EARLY and pair.lag == 0:
                s = prev(s)
            return ring_d.at(s, chunks[i])

        def runs(pair):
            return pair.exists

        @block.sync
        def _(sp):
            def load_w_qkv(f, lo, hi, done):
                sp.dma_start(w_qkv[:, lo:hi], w["Wqkv"][bass.ds(layer_of(f), 1), :, lo:hi]
                             .rearrange("one k n -> (one k) n")).then_inc(done, 16)

            def load_qk_rows(f):
                sp.dma_start(qk_row[:, :, :], w["qk_rows"][bass.ds(layer_of(f), 1), :]
                             .rearrange("one (r d) -> one r d", d=DH).to_broadcast([P, 4, DH])).then_inc(qkrow_in, 16)

            def load_wo(f):
                sp.dma_start(w_o[:, :, :], w["Wo"][bass.ds(layer_of(f), 1), :, :]
                             .rearrange("one (c k) n -> k (one c) n", k=P)).then_inc(wo_in, 16)

            def load_ffn(f):
                layer = bass.ds(layer_of(f), 1)
                sp.dma_start(w_1[:, :], w["W1"][layer, :, :].rearrange("one k n -> (one k) n")).then_inc(wffn_in, 16)
                sp.dma_start(w_2[:, 0:2, :], w["W2"][layer, 0:2 * P, :]
                             .rearrange("one (c k) n -> k (one c) n", k=P)).then_inc(wffn_in, 16)
                sp.dma_start(w_2[0:FF - 2 * P, 2, :], w["W2"][layer, 2 * P:FF, :]
                             .rearrange("one k n -> (one k) n")).then_inc(wffn_in, 16)
                sp.dma_start(small[:, :], w["small"][layer, :, :].rearrange("one k n -> (one k) n")).then_inc(wffn_in, 16)

            def load_shifted(dst, region, f, p, s):
                row = 1 + PAIR * p
                lo = dram_rows(region, f, row, PAIR).rearrange("(a t) d -> t a d", a=2)
                hi = dram_rows(region, f, row - 1, PAIR).rearrange("(a t) d -> t a d", a=2)
                sp.dma_start(dst[:, :, 0:DIM // 2], lo[:, :, 0:DIM // 2]).then_inc(s, 16)
                sp.dma_start(dst[:, :, DIM // 2:DIM], hi[:, :, DIM // 2:DIM]).then_inc(s, 16)

            def load_xs(pair):
                load_shifted(xs[pair.par], x_dram, pair.f, pair.p, xs_in[pair.par])

            sp.dma_start(rotary[:, :, :, :], w["rotary"]).then_inc(s_const, 16)
            load_xs(Step(0, 0).pair(0))
            load_w_qkv(0, 0, 2 * INNER, wqk_in)
            load_qk_rows(0)
            load_w_qkv(0, 2 * INNER, 3 * INNER, wv_in)
            load_wo(0)
            load_ffn(0)

            def step(s):
                new, now, back1, back2 = (s.pair(lag) for lag in (-1, 0, 1, 2))
                if not isinstance(s.t, int) or s.t > 2:
                    sp.wait_ge(x2_out, 16 * (s.t - 2))
                if runs(now) and not (isinstance(s.t, int) and s.t == PAIRS):
                    load_xs(new)
                if runs(back1):
                    sp.dma_start(xr[back1.par][:, :, :], dram_rows(x_dram, back1.f, 1 + PAIR * back1.p, PAIR)
                                 .rearrange("(a t) d -> t a d", a=2)).then_inc(xr_in[back1.par], 16)
                if runs(now) and s.p == 0:
                    sp.wait_ge(table_ready, s.f + 1)
                    load_qk_rows(s.f + 1)
                if runs(now) and s.p == POS - 1:
                    sp.wait_ge(d_filled, chunk_at(now, 7)[1] + 1)
                    load_w_qkv(s.f + 1, 0, 2 * INNER, wqk_in)
                if runs(now):
                    sp.wait_ge(d_free, ring_d.at(s, (1, "v", 1))[1] + 1)
                    q = WINDOW
                    src, old, dst = v[now.par], v[1 - now.par], v_back[now.par]
                    done = v_back_in[now.par]
                    sp.dma_start(dst[q:P, :, :], src[0:P - q, :, :]).then_inc(done, 16)
                    sp.dma_start(dst[0:q, 1, :], src[P - q:P, 0, :]).then_inc(done, 16)
                    sp.dma_start(dst[0:q, 0, :], old[P - q:P, 1, :]).then_inc(done, 16)
                    if s.p == POS - 1:
                        load_w_qkv(s.f + 1, 2 * INNER, 3 * INNER, wv_in)
                if runs(back2):
                    sp.wait_ge(d_free, ring_d.at(s, "y2")[1] + 1)
                    sp.dma_start(dram_rows(x_dram, back2.f + BATCH, 1 + PAIR * back2.p, PAIR)
                                 .rearrange("(a t) d -> t a d", a=2), x2[back2.par][:, :, :]).then_inc(x2_out, 16)
                    if s.p == 1 and not (isinstance(s.t, int) and s.t > PAIRS):
                        load_ffn(s.f)
                if runs(back1):
                    sp.wait_ge(d_free, ring_d.at(s, "y")[1] + 1)
                    sp.dma_start(x1_dram[1 + PAIR * back1.p:1 + PAIR * (back1.p + 1), :]
                                 .rearrange("(a t) d -> t a d", a=2), x1[back1.par][:, :, :]).then_inc(x1_out, 16)
                    sp.wait_ge(x1_out, 16 * (back1.n + 1))
                    if not isinstance(back1.n, int) or back1.n >= 2:
                        sp.wait_ge(xn_ready, back1.n - 1)
                    row = 1 + PAIR * back1.p
                    for lo, hi, r in ((0, DIM // 2, row), (DIM // 2, DIM, row - 1)):
                        sp.dma_start(xs1[back1.par][:, :, lo:hi], x1_dram[r:r + PAIR, lo:hi]
                                     .rearrange("(a t) d -> t a d", a=2)).then_inc(xs1_in[back1.par], 16)
                if runs(back1) and s.p == 0 and not (isinstance(s.t, int) and s.t == PAIRS):
                    sp.wait_ge(a_filled, ring_a.at(s, "yT")[1] + 1)
                    load_wo(s.f)

            rounds(sp, step)
            sp.wait_ge(x2_out, 16 * PAIRS)

        @block.tensor
        def _(pe):
            def fill_d(s, name):
                slot, n = ring_d.at(s, name)
                if not isinstance(n, int) or n >= 3:
                    pe.wait_ge(d_free, n - 2)
                return bank_d[slot]

            def fill_a(s, name, after=None):
                slot, n = ring_a.at(s, name)
                order = ring_a.names(s.t)
                if after and order.index(after) + 1 >= order.index(name) - 2:
                    pe.wait_ge(a_free, ring_a.at(s, after)[1] + 1)
                elif not isinstance(n, int) or n >= 3:
                    pe.wait_ge(a_free, n - 2)
                return bank_a[slot]

            def transpose_x(s):
                new = s.pair(-1)
                pe.wait_ge(xs_in[new.par], 32 * (new.k + 1))
                bank = fill_d(s, "xT")
                for a in range(2):
                    last = nc.tensor.transpose(bank[:, P * a:P * (a + 1)], xs[new.par][:, a, :], ident[:, :])
                last.then_inc(d_filled, 1)

            def project(s, i):
                a, kind, c = chunks[i]
                if i == 0:
                    if s.p == POS - 1:
                        pe.wait_ge(wqk_in, 16 * (s.f + 2))
                    pe.wait_ge(d_free, ring_d.at(s, "xT")[1] + 1)
                if i == 8 and s.p == 0:
                    pe.wait_ge(wv_in, 16 * (s.f + 1))
                bank = fill_d(s, chunks[i])
                col = INNER * "qkv".index(kind) + 512 * c
                nc.tensor.matmul(bank[:, :], xT[:, P * a:P * (a + 1)], w_qkv[:, col:col + 512],
                                 start=True, stop=True).then_inc(d_filled, 1)

            def transpose_probs(s, pair, ph):
                pe.wait_ge(prob_ready, 2 * pair.n + ph + 1)
                for half in range(2):
                    i = 2 * ph + half
                    bank = fill_a(s, f"PT{i}")
                    for j in range(4):
                        hp = 4 * half + j
                        last = nc.tensor.transpose(
                            bank[:, P * j:P * (j + 1)],
                            prob[ph][:, 2 * hp:2 * hp + 2, :].rearrange("p u k -> p (u k)"), ident[:, :])
                    last.then_inc(a_filled, 1)

            def times_v(s, pair, i):
                a, half = divmod(i, 2)
                if i == 0:
                    pe.wait_ge(v_back_in[pair.par], 48 * (pair.k + 1))
                bank = fill_a(s, f"O{i}", after="PT3")
                nc.tensor.matmul(bank[:, 0:2], ident_b[:, :], ident_b[:, 0:2], start=True, stop=True)
                for hp in range(4 * half, 4 * half + 4):
                    for h2 in range(2):
                        h = 2 * hp + h2
                        for win in range(4):
                            u, ph = divmod(win, 2)
                            src = (v if ph else v_back)[pair.par]
                            last = nc.tensor.matmul(
                                bank[32 * win:32 * win + 32, DH * (h - 8 * half):DH * (h - 8 * half + 1)],
                                probT[ph][64 * u:64 * u + 64, hp, 32 * (2 * h2 + a):32 * (2 * h2 + a) + 32],
                                src[64 * u:64 * u + 64, a, DH * h:DH * (h + 1)],
                                start=True, stop=True)
                last.then_inc(a_filled, 1)

            def transpose_qk(s, pair, i):
                a, kind, half = i // 4, (i // 2) % 2, i % 2
                if i % 4 == 0:
                    pe.wait_ge(qk_ready, 2 * pair.n + a + 1)
                bank = fill_a(s, f"qk{i}")
                for j in range(4):
                    col = INNER * kind + P * (4 * half + j)
                    last = nc.tensor.transpose(bank[:, P * j:P * (j + 1)], qk_rot[:, a, col:col + P], ident[:, :])
                last.then_inc(a_filled, 1)

            def transpose_attn(s, i):
                a, half = divmod(i, 2)
                bank = fill_a(s, f"OT{i}", after=f"O{i}")
                for j in range(4):
                    hp = 4 * half + j
                    last = nc.tensor.transpose(bank[:, P * j:P * (j + 1)], attn[:, a, P * hp:P * (hp + 1)], ident[:, :])
                last.then_inc(a_filled, 1)

            def score(s, pair, ph, half):
                if half == 0:
                    pe.wait_ge(a_free, ring_a.at(s, "qk7")[1] + 1)
                    n = 2 * pair.n + ph
                    if not isinstance(n, int) or n >= 1:
                        pe.wait_ge(scores_used, n)
                first = pair.p == 0 and ph == 0
                bank = scores[:, 4 * half:4 * half + 4, :, :]
                nc.tensor.matmul(bank, ident_b[:, :], mask[:, int(first), :, :, :], start=True, stop=False,
                                 skip_group_check=True)
                for hp in range(4 * half, 4 * half + 4):
                    for u in range(2):
                        for h2 in range(2):
                            for a in range(2):
                                win = 4 * a + 2 * u + ph
                                row = 32 * (2 * h2 + a)
                                last = nc.tensor.matmul(
                                    scores[row:row + 32, hp, u, :],
                                    qT[64 * h2:64 * h2 + 64, hp, 32 * win:32 * win + 32],
                                    kT[pair.par][64 * h2:64 * h2 + 64, hp, 32 * win:32 * win + 64],
                                    start=False, stop=True, skip_group_check=True)
                if half:
                    last.then_inc(scores_ready, 1)

            def times_wo(s, pair):
                if s.p == 1:
                    pe.wait_ge(wo_in, 16 * (s.f + 1))
                bank = fill_a(s, "yT", after="OT2")
                for hp in range(HP):
                    if hp == HP // 2:
                        pe.wait_ge(a_free, ring_a.at(s, "OT3")[1] + 1)
                    last = nc.tensor.matmul(bank[:, 0:PAIR], w_o[:, hp, :], attnT[:, hp, :],
                                            start=(hp == 0), stop=(hp == HP - 1))
                last.then_inc(a_filled, 1)

            def transpose_pair(s, name, src):
                bank = fill_d(s, name)
                for a in range(2):
                    last = nc.tensor.transpose(bank[:, P * a:P * (a + 1)], src(a), ident[:, :])
                last.then_inc(d_filled, 1)

            def ffn_up(s, pair):
                if s.p == 2:
                    pe.wait_ge(wffn_in, 64 * (s.f + 1))
                pe.wait_ge(d_free, ring_d.at(s, "xn")[1] + 1)
                for name, group, lo in (("gA", (0, 1), FF), ("aA", (0, 1), 0), ("gB", (2,), FF), ("aB", (2,), 0)):
                    on_a = name[0] == "g"
                    bank = (fill_a if on_a else fill_d)(s, name)
                    for k in group:
                        first, width = FF_BLOCKS[k]
                        col = PAIR * (k - group[0])
                        last = nc.tensor.matmul(bank[0:width, col:col + PAIR], w_1[:, lo + first:lo + first + width],
                                                xnT[:, :], start=True, stop=True)
                    last.then_inc(a_filled if on_a else d_filled, 1)

            def ffn_down(s):
                pe.wait_ge(d_free, ring_d.at(s, "aB")[1] + 1)
                bank = fill_a(s, "y2T")
                for k, (first, width) in enumerate(FF_BLOCKS):
                    last = nc.tensor.matmul(bank[:, 0:PAIR], w_2[0:width, k, :], hidden[0:width, k, :],
                                            start=(k == 0), stop=(k == 2))
                last.then_inc(a_filled, 1)

            pe.wait_ge(s_init, INIT)
            transpose_x(Step(-1, POS - 1))
            for i in range(EARLY):
                project(Step(-1, POS - 1), i)

            def step(s):
                now, back1, back2 = s.pair(0), s.pair(1), s.pair(2)

                def project_now(*which):
                    if runs(now):
                        for i in which:
                            project(s, i)

                def project_next(i):
                    if s.pair(-1).exists:
                        project(s, i)

                for i in range(4):
                    if runs(back1):
                        transpose_qk(s, back1, 2 * i)
                        transpose_qk(s, back1, 2 * i + 1)
                    if i < 3:
                        project_now(EARLY + i)
                if runs(back1):
                    score(s, back1, 0, 0)
                    score(s, back1, 0, 1)
                project_now(6, 7)
                if runs(back1):
                    score(s, back1, 1, 0)
                    score(s, back1, 1, 1)
                if runs(back2):
                    pe.wait_ge(xn_ready, back2.n + 1)
                    transpose_pair(s, "xn", lambda a: xn[:, a, :])
                project_now(8)
                if runs(back1):
                    transpose_probs(s, back1, 0)
                if runs(back2):
                    ffn_up(s, back2)
                project_now(9)
                if runs(back1):
                    transpose_probs(s, back1, 1)
                project_now(10)
                if runs(back1):
                    times_v(s, back1, 0)
                    times_v(s, back1, 2)
                project_now(11)
                if s.pair(-1).exists:
                    transpose_x(s)
                if runs(back1):
                    times_v(s, back1, 1)
                    transpose_attn(s, 0)
                    times_v(s, back1, 3)
                    transpose_attn(s, 2)
                if runs(back2):
                    ffn_down(s)
                project_next(0)
                if runs(back1):
                    transpose_attn(s, 1)
                    transpose_attn(s, 3)
                project_next(1)
                project_next(2)
                if runs(back2):
                    pe.wait_ge(a_free, ring_a.at(s, "y2T")[1] + 1)
                    transpose_pair(s, "y2", lambda a: y2T[:, P * a:P * (a + 1)])
                if runs(back1):
                    times_wo(s, back1)
                if runs(back1):
                    pe.wait_ge(a_free, ring_a.at(s, "yT")[1] + 1)
                    transpose_pair(s, "y", lambda a: yT[:, P * a:P * (a + 1)])

            rounds(pe, step)

        @block.scalar
        def _(act):
            def filled(s, name):
                slot, n = ring_a.at(s, name)
                act.wait_ge(a_filled, n + 1)
                return bank_a[slot]

            def square(pair, i):
                if not runs(pair):
                    return
                slot, n = chunk_at(pair, i)
                act.wait_ge(d_filled, n + 1)
                if i >= 2 or not isinstance(pair.n, int) or pair.n > 0:
                    m = chunk_at(pair, i - 2)[1] if i >= 2 else chunk_at(pair.step.pair(pair.lag + 1), 6 + i)[1]
                    act.wait_ge(d_free, m + 1)
                nc.scalar.activation(sq[i % 2][:, :, :], bank_d[slot][:, :].rearrange("p (h d) -> p h d", d=DH),
                                     ACT.Square).then_inc(squared, 1)

            def copy_qk(s, pair, i):
                a, kind, half = i // 4, (i // 2) % 2, i % 2
                bank = filled(s, f"qk{i}")[:, :].rearrange("p (j t) -> p j t", t=P)
                hps = slice(4 * half, 4 * half + 4)
                if kind == 0:
                    out = qT[:, hps, P * a:P * (a + 1)]
                else:
                    out = kT[pair.par][:, hps, WINDOW + P * a:WINDOW + P * (a + 1)]
                    if a == 1:
                        nxt = kT[1 - pair.par][:, hps, 0:WINDOW]
                        nc.scalar.activation(nxt, bank[:, :, P - WINDOW:P], ACT.Copy,
                                             scale=0.0 if pair.p == POS - 1 else 1.0)
                nc.scalar.activation(out, bank, ACT.Copy).then_inc(a_free, 1)

            def exponentials(pair, ph):
                act.wait_ge(scores_used, 2 * pair.n + ph + 1)
                nc.scalar.activation(prob[ph][:, :, :], prob[ph][:, :, :], ACT.Exp).then_inc(exp_done, 1)

            def copy_probs(s, ph):
                for half in range(2):
                    bank = filled(s, f"PT{2 * ph + half}")
                    nc.scalar.activation(probT[ph][:, 4 * half:4 * half + 4, :], bank[:, :].rearrange("p (j t) -> p j t", t=P),
                                         ACT.Copy).then_inc(a_free, 1)

            def copy_attn(s, i):
                a, half = divmod(i, 2)
                bank = filled(s, f"O{i}")
                nc.scalar.activation(attn[:, a, 512 * half:512 * (half + 1)], bank[:, :], ACT.Copy).then_inc(a_free, 1)

            def copy_attnT(s, i):
                a, half = divmod(i, 2)
                bank = filled(s, f"OT{i}")
                nc.scalar.activation(attnT[:, 4 * half:4 * half + 4, P * a:P * (a + 1)],
                                     bank[:, :].rearrange("p (j t) -> p j t", t=P), ACT.Copy).then_inc(a_free, 1)

            def gates(s):
                if s.p == 2:
                    act.wait_ge(wffn_in, 64 * (s.f + 1))
                for name, group in (("gA", (0, 1)), ("gB", (2,))):
                    bank = filled(s, name)
                    for k in group:
                        width = FF_BLOCKS[k][1]
                        last = nc.scalar.activation(gate[0:width, k, :], bank[0:width, PAIR * (k - group[0]):PAIR * (k - group[0] + 1)],
                                                    ACT.Gelu, bias=small[0:width, SMALL["b1g"] + k:SMALL["b1g"] + k + 1])
                    last.then_inc(a_free, 1)

            def step(s):
                new, now, back1, back2 = (s.pair(lag) for lag in (-1, 0, 1, 2))
                for i in range(4):
                    if runs(back1):
                        copy_qk(s, back1, 2 * i)
                        copy_qk(s, back1, 2 * i + 1)
                    if i < 3:
                        square(now, EARLY + i)
                square(now, 6)
                if runs(back1):
                    exponentials(back1, 0)
                square(now, 7)
                if runs(back1):
                    exponentials(back1, 1)
                    copy_probs(s, 0)
                if runs(back2):
                    gates(s)
                if runs(back1):
                    copy_probs(s, 1)
                    copy_attn(s, 0)
                    copy_attn(s, 2)
                    copy_attn(s, 1)
                    copy_attnT(s, 0)
                    copy_attn(s, 3)
                    copy_attnT(s, 2)
                if runs(back2):
                    bank = filled(s, "y2T")
                    nc.scalar.activation(y2T[:, :], bank[:, 0:PAIR], ACT.Identity,
                                         bias=small[:, SMALL["b2"]:SMALL["b2"] + 1]).then_inc(a_free, 1)
                square(new, 0)
                if runs(back1):
                    copy_attnT(s, 1)
                    copy_attnT(s, 3)
                square(new, 1)
                square(new, 2)
                if runs(back1):
                    bank = filled(s, "yT")
                    nc.scalar.activation(yT[:, :], bank[:, 0:PAIR], ACT.Copy).then_inc(a_free, 1)

            act.wait_ge(s_init, INIT)
            for i in range(EARLY):
                square(Step(-1, POS - 1).pair(-1), i)
            rounds(act, step)

        @block.vector
        def _(dve):
            links, chain = [0], [0]

            def link(ins):
                links[0] += 1
                ins.then_inc(v_link, 1)
                dve.wait_ge(v_link, links[0])

            def filled(s, name):
                slot, n = ring_d.at(s, name)
                dve.wait_ge(d_filled, n + 1)
                return bank_d[slot]

            def rsqrt_step(out, x, tmp, k):
                if k == 0:
                    return nc.vector.tensor_scalar(out.bitcast(i32), x.bitcast(i32), 1, None, ALU.logical_shift_right)
                if k == 1:
                    return nc.vector.tensor_scalar(out.bitcast(i32), out.bitcast(i32), -1.0, float(RSQRT_MAGIC), ALU.mult, ALU.add)
                if k % 3 == 2:
                    return nc.vector.tensor_tensor(tmp, out, out, ALU.mult)
                if k % 3 == 0:
                    return nc.vector.scalar_tensor_tensor(tmp, tmp, -0.5, x, ALU.mult, ALU.mult)
                return nc.vector.scalar_tensor_tensor(out, tmp, 1.5, out, ALU.add, ALU.mult)

            def softmax_shift(s, ph):
                if not runs(s.pair(1)):
                    return
                n = 2 * s.pair(1).n + ph
                dve.wait_ge(scores_ready, n + 1)
                sc = scores[:, :, :, :].rearrange("p h u k -> p (h u) k")
                ins = nc.vector.tensor_reduce(row_max[:, ph, :], sc, AX.X, ALU.max)
                if ph == 0:
                    ins.then_inc(maximum, 1)
                    first_norm(s, 1)
                    dve.wait_ge(maximum, s.pair(1).n + 1)
                else:
                    link(ins)
                if not isinstance(n, int) or n >= 2:
                    dve.wait_ge(a_filled, ring_a.at(prev(s), f"PT{2 * ph + 1}")[1] + 1)
                nc.vector.tensor_tensor(prob[ph][:, :, :], sc,
                                        row_max[:, ph, :].unsqueeze(2).to_broadcast([P, HEADS, 2 * WINDOW]),
                                        ALU.subtract).then_inc(scores_used, 1)

            def softmax_sum(s, ph):
                if not runs(s.pair(1)):
                    return
                n = 2 * s.pair(1).n + ph
                dve.wait_ge(exp_done, n + 1)
                link(nc.vector.tensor_reduce(row_sum[:, ph, :], prob[ph][:, :, :], AX.X, ALU.add))
                nc.vector.reciprocal(inv_sum[:, ph, :], row_sum[:, ph, :]).then_inc(inv_ready, 1)

            def rotate(s, pair, i, norm_step=None):
                if not runs(pair):
                    return
                a, kind, c = chunks[i]
                if i == 0 and pair.p == 0:
                    dve.wait_ge(table_ready, pair.f + 1)
                slot, n = chunk_at(pair, i)
                bank = bank_d[slot]
                t4 = table[:, 2 * pair.p + a, :, :]
                kq = "qk".index(kind)
                col = INNER * kq + 512 * c
                if i % 4 == 0 and (not isinstance(pair.n, int) or pair.n > 0):
                    dve.wait_ge(qk_ready, 2 * pair.n + a - 1)
                if norm_step is not None:
                    first_norm(s, norm_step)
                dve.wait_ge(squared, 8 * pair.n + i + 1)
                cos = t4[:, 2 * kq, :].unsqueeze(1).to_broadcast([P, 8, DH])
                nc.vector.tensor_tensor(by_cos[:, a, col:col + 512].rearrange("p (h d) -> p h d", d=DH),
                                        bank[:, :].rearrange("p (h d) -> p h d", d=DH), cos, ALU.mult)
                if norm_step is not None:
                    first_norm(s, norm_step + 1)
                nc.vector.tensor_reduce(ss[:, a, HEADS * kq + 8 * c:HEADS * kq + 8 * c + 8], sq[i % 2][:, :, :], AX.X, ALU.add)
                if norm_step is not None:
                    first_norm(s, norm_step + 2)
                sin = t4[:, 2 * kq + 1, :].rearrange("p (r d) -> p r d", r=2).unsqueeze(1).to_broadcast([P, 8, 2, DH // 2])
                swapped = bank[:, :].rearrange("p (h r d) -> p h r d", r=2, d=DH // 2)[:, :, ::-1, :]
                nc.vector.tensor_tensor(by_sin[:, a, col:col + 512].rearrange("p (h r d) -> p h r d", r=2, d=DH // 2),
                                        swapped, sin, ALU.mult).then_inc(d_free, 1)
                if norm_step is not None:
                    first_norm(s, norm_step + 3)
                if i % 4 == 3:
                    dve.wait_ge(d_free, n + 1)

            def copy_x(s):
                bank = filled(s, "xT")
                nc.vector.tensor_copy(xT[:, :], bank[:, 0:PAIR]).then_inc(d_free, 1)

            def variances(s):
                back2 = s.pair(2)
                dve.wait_ge(xs1_in[back2.par], 32 * (back2.k + 1))
                for a in range(2):
                    last = nc.vector.bn_stats(stats[:, a, :], xs1[back2.par][:, a, :])
                link(last)
                for a in range(2):
                    last = nc.vector.bn_aggr(mean_var[:, a, :], stats[:, a, :])
                link(last)
                link(nc.vector.tensor_scalar(ss[:, 0, 2 * HEADS:], mean_var[:, :, 1], 1e-5, None, ALU.add))

            def first_norm(s, step):
                now, back2 = s.pair(0), s.pair(2)
                lo = 0 if runs(now) else 2 * HEADS
                hi = 2 * HEADS + 2 if runs(back2) else 2 * HEADS
                if lo == hi:
                    return
                x, out, tmp = ss[:, 0, lo:hi], rnorm[:, 0, lo:hi], newton[:, lo:hi]
                if step > 0 and chain[0]:
                    dve.wait_ge(v_link, chain[0])
                if step == 0:
                    chain[0] = 0
                    if not runs(now):
                        return
                    ins = nc.vector.tensor_scalar(ss[:, 0, 0:2 * HEADS], ss[:, 0, 0:2 * HEADS], 1e-24, None, ALU.max)
                else:
                    ins = rsqrt_step(out, x, tmp, step - 1)
                if step == 11 and runs(now):
                    ins.then_inc(norm_ready, 1)
                    return
                ins.then_inc(v_link, 1)
                links[0] += 1
                chain[0] = links[0]

            def second_norm(s):
                link(nc.vector.tensor_scalar(ss[:, 1, 0:2 * HEADS], ss[:, 1, 0:2 * HEADS], 1e-24, None, ALU.max))
                for k in range(11):
                    ins = rsqrt_step(rnorm[:, 1, 0:2 * HEADS], ss[:, 1, 0:2 * HEADS], newton[:, 0:2 * HEADS], k)
                    if k < 10:
                        link(ins)
                    else:
                        ins.then_inc(norm_ready, 1)

            def normalise(s):
                now, back2 = s.pair(0), s.pair(2)
                if runs(now):
                    dve.wait_ge(norm_ready, 2 * now.n + 1)
                else:
                    dve.wait_ge(v_link, chain[0])
                for a in range(2):
                    last = nc.vector.tensor_scalar(xn[:, a, :], xs1[back2.par][:, a, :], mean_var[:, a, 0:1],
                                                   rnorm[:, 0, 2 * HEADS + a:2 * HEADS + a + 1], ALU.subtract, ALU.mult)
                last.then_inc(xn_ready, 1)

            def copy_v(s, i):
                now = s.pair(0)
                if not runs(now):
                    return
                a, _, c = chunks[i]
                bank = filled(s, chunks[i])
                if i == 8 and (not isinstance(now.n, int) or now.n >= 1):
                    dve.wait_ge(v_back_in[1 - now.par], 48 * (prev(s).pair(0).k + 1))
                    if not isinstance(now.n, int) or now.n >= 2:
                        dve.wait_ge(a_filled, ring_a.at(prev(s), "O3")[1] + 1)
                nc.vector.tensor_copy(v[now.par][:, a, 512 * c:512 * (c + 1)], bank[:, :]).then_inc(d_free, 1)

            def hidden_units(s):
                for name, group in (("aA", (0, 1)), ("aB", (2,))):
                    bank = filled(s, name)
                    dve.wait_ge(a_free, ring_a.at(s, "g" + name[1])[1] + 1)
                    for k in group:
                        width = FF_BLOCKS[k][1]
                        last = nc.vector.scalar_tensor_tensor(
                            hidden[0:width, k, :], bank[0:width, PAIR * (k - group[0]):PAIR * (k - group[0] + 1)],
                            small[0:width, SMALL["b1a"] + k:SMALL["b1a"] + k + 1], gate[0:width, k, :], ALU.add, ALU.mult)
                    last.then_inc(d_free, 1)

            def step(s):
                new, now, back1, back2 = (s.pair(lag) for lag in (-1, 0, 1, 2))
                rotate(s, now, 3)
                rotate(s, now, 4)
                rotate(s, now, 5)
                if runs(back2):
                    variances(s)
                first_norm(s, 0)
                if runs(back1):
                    softmax_shift(s, 0)
                else:
                    first_norm(s, 1)
                first_norm(s, 2)
                first_norm(s, 3)
                if runs(now):
                    rotate(s, now, 6, norm_step=4)
                else:
                    for k in range(4, 8):
                        first_norm(s, k)
                for k in range(8, 12):
                    first_norm(s, k)
                if runs(back2):
                    normalise(s)
                softmax_sum(s, 0)
                softmax_shift(s, 1)
                rotate(s, now, 7)
                if runs(back2):
                    if s.p == 2:
                        dve.wait_ge(wffn_in, 64 * (s.f + 1))
                    bank = filled(s, "xn")
                    nc.vector.tensor_scalar(xnT[:, :], bank[:, 0:PAIR], small[:, SMALL["g"]:SMALL["g"] + 1],
                                            small[:, SMALL["b"]:SMALL["b"] + 1], ALU.mult, ALU.add).then_inc(d_free, 1)
                copy_v(s, 8)
                softmax_sum(s, 1)
                if runs(back2):
                    hidden_units(s)
                if runs(now):
                    second_norm(s)
                for i in (9, 10, 11):
                    copy_v(s, i)
                if new.exists:
                    copy_x(s)
                rotate(s, new, 0)
                rotate(s, new, 1)
                rotate(s, new, 2)
                if runs(back2):
                    bank = filled(s, "y2")
                    if not isinstance(back2.n, int) or back2.n >= 2:
                        dve.wait_ge(x2_out, 16 * (back2.n - 1))
                    nc.vector.tensor_tensor(x2[back2.par][:, :, :], bank[:, 0:PAIR].rearrange("p (a d) -> p a d", a=2),
                                            x1[back2.par][:, :, :], ALU.add).then_inc(d_free, 1)
                if runs(back1):
                    bank = filled(s, "y")
                    dve.wait_ge(xr_in[back1.par], 16 * (back1.k + 1))
                    if not isinstance(back1.n, int) or back1.n >= 2:
                        dve.wait_ge(x1_out, 16 * (back1.n - 1))
                    nc.vector.tensor_tensor(x1[back1.par][:, :, :], bank[:, 0:PAIR].rearrange("p (a d) -> p a d", a=2),
                                            xr[back1.par][:, :, :], ALU.add).then_inc(d_free, 1)
                if s.p == POS - 1:
                    nc.vector.sem_clear(v_link)
                    links[0] = 0

            nc.vector.memset(v[1][:, :, :], 0.0)
            dve.wait_ge(s_zero, 3)
            nc.vector.tensor_copy(ident_b[:, :], ident[:, :]).then_inc(s_init, 1)
            nc.vector.memset(kT[0][:, :, 0:WINDOW], 0.0).then_inc(s_init, 1)
            copy_x(Step(-1, POS - 1))
            for i in range(EARLY):
                rotate(None, Step(-1, POS - 1).pair(-1), i)
            rounds(dve, step)


        @block.gpsimd
        def _(pool):
            links = [0]

            def link(ins):
                links[0] += 1
                ins.then_inc(p_link, 1)
                pool.wait_ge(p_link, links[0])

            nc.gpsimd.memset(ident[:, :], 0.0).then_inc(s_zero, 1)
            nc.gpsimd.memset(mask[:, :, :, :, :], 0.0).then_inc(s_zero, 1)
            pool.wait_ge(s_zero, 2)
            nc.gpsimd.affine_select(out=ident[:, :], in_=ident[:, :], compare_op=ALU.not_equal, fill=1.0, base=0,
                                    pattern=[[-1, P]], channel_multiplier=1).then_inc(s_zero, 1)
            for q in range(4):
                rows = mask[32 * q:32 * q + 32, :, :, :, :].rearrange("p m h u k -> p (m h u) k")
                for own, sign in ((0, 1), (1, -1)):
                    part = rows[:, :, WINDOW * own:WINDOW * (own + 1)]
                    link(nc.gpsimd.affine_select(out=part, in_=part, compare_op=ALU.is_ge, fill=MASKED, base=0,
                                                 pattern=[[0, 16], [sign, WINDOW]], channel_multiplier=-sign))
            for q in (0, 2):
                nc.gpsimd.memset(mask[32 * q:32 * q + 32, 1, :, 0, 0:WINDOW], MASKED).then_inc(s_init, 1)
            pool.wait_ge(s_init, INIT)

            def make_table(f):
                pool.wait_ge(qkrow_in, 16 * (f + 1))
                nc.gpsimd.tensor_tensor(table[:, :, :, :].rearrange("p t r d -> p t (r d)"),
                                        rotary[:, :, :, :].rearrange("p t r d -> p t (r d)"),
                                        qk_row[:, :, :].rearrange("p r d -> p (r d)").unsqueeze(1).to_broadcast([P, SEQ // P, 4 * DH]),
                                        ALU.mult).then_inc(table_ready, 1)

            pool.wait_ge(s_const, 16)
            make_table(0)
            def add_products(s, a):
                link(nc.gpsimd.tensor_tensor(by_cos[:, a, :], by_cos[:, a, :], by_sin[:, a, :], ALU.add))

            def norm_qk(s, a):
                now, back1 = s.pair(0), s.pair(1)
                pool.wait_ge(norm_ready, 2 * now.n + a + 1)
                if runs(back1):
                    pool.wait_ge(a_filled, ring_a.at(s, f"qk{4 * a + 3}")[1] + 1)
                nc.gpsimd.tensor_tensor(qk_rot[:, a, :].rearrange("p (h d) -> p h d", d=DH),
                                        by_cos[:, a, :].rearrange("p (h d) -> p h d", d=DH),
                                        rnorm[:, a, 0:2 * HEADS].unsqueeze(2).to_broadcast([P, 2 * HEADS, DH]),
                                        ALU.mult).then_inc(qk_ready, 1)

            def normalise(pair, ph):
                pool.wait_ge(inv_ready, 2 * pair.n + ph + 1)
                nc.gpsimd.tensor_tensor(prob[ph][:, :, :], prob[ph][:, :, :],
                                        inv_sum[:, ph, :].unsqueeze(2).to_broadcast([P, HEADS, 2 * WINDOW]),
                                        ALU.mult).then_inc(prob_ready, 1)

            def step(s):
                now, back1 = s.pair(0), s.pair(1)
                if runs(now):
                    pool.wait_ge(d_free, chunk_at(now, 3)[1] + 1)
                    add_products(s, 0)
                if runs(back1):
                    normalise(back1, 0)
                if runs(now):
                    norm_qk(s, 0)
                if runs(back1):
                    normalise(back1, 1)
                if runs(now):
                    pool.wait_ge(d_free, chunk_at(now, 7)[1] + 1)
                    if s.p == POS - 1:
                        make_table(s.f + 1)
                    add_products(s, 1)
                    norm_qk(s, 1)
                if s.p == POS - 1:
                    nc.gpsimd.sem_clear(p_link)
                    links[0] = 0

            rounds(pool, step)


A_HEADS, A_KV, A_DH = 16, 4, 8
Q_RANK, KV_RANK = 64, 32
TILES = SEQ // P
HALF = SEQ // 2
PARTS = 6
SPLIT = PARTS * A_DH
Q_PART, K_PART = (0, 0, 1, 0, 1, 2), (0, 1, 0, 2, 1, 0)
NEG_UNIT, FIRST_MAX = 17, 3
MAX_UNITS = [(i, half) for i in range(TILES) for half in range(1 + (i >= 4))]
UNITS = [(qb, hpl, kt) for qb in range(2) for hpl in range(2) for kt in range(4 * qb + 4)]


def rsqrt(nc, link, out, x, tmp, last):
    link(nc.vector.tensor_scalar(out.bitcast(i32), x.bitcast(i32), 1, None, ALU.logical_shift_right))
    link(nc.vector.tensor_scalar(out.bitcast(i32), out.bitcast(i32), -1.0, float(RSQRT_MAGIC), ALU.mult, ALU.add))
    for k in range(3):
        link(nc.vector.tensor_tensor(tmp, out, out, ALU.mult))
        link(nc.vector.scalar_tensor_tensor(tmp, tmp, -0.5, x, ALU.mult, ALU.mult))
        (last if k == 2 else link)(nc.vector.scalar_tensor_tensor(out, tmp, 1.5, out, ALU.add, ALU.mult))


def maxima_at(u):
    per = 48 // (NEG_UNIT - 2 - FIRST_MAX)
    return range(48)[per * (u - FIRST_MAX):per * (u - FIRST_MAX + 1)] if u >= FIRST_MAX else range(0)


class MiscFills:

    def __init__(self):
        prep = ["xT0", "xT1", "pr0", "pr1", "kv0", "kv1", "kv2", "kv3", "tq0", "tq1", "tk", "nm"]
        self.names = [(-1, name) for name in prep]
        for g in range(A_KV):
            for u in range(len(UNITS)):
                self.names += [(g, name) for name in self.at_unit(g, u)]
            self.names.append((g, "oa1"))
        self.names += [(A_KV, name) for name in ("ao0", "ao1", "y0", "y1")]

    @staticmethod
    def at_unit(g, u):
        at = {11: "oa0"}
        if g < A_KV - 1:
            at |= {0: "tq0", 1: "tq1", 2: "tk", NEG_UNIT: "nm"}
        return [at[u]] if u in at else []

    def number(self, b, g, name):
        return len(self.names) * b + self.names.index((g, name))


def mla_attention(nc, x_in, x_dram, neg_dram, w):
    with ExitStack() as ctx:
        def sb(name, shape, dt=fp32):
            return ctx.enter_context(nc.sbuf_tensor(name, shape, dt))

        def sem(name):
            return ctx.enter_context(nc.semaphore(name))

        def psum(name, shape):
            return ctx.enter_context(nc.psum_tensor(name, shape, fp32))

        w_a = sb("w_a", [P, Q_RANK + KV_RANK])
        w_b = sb("w_b", [Q_RANK + KV_RANK, DIM + 2 * A_KV * A_DH])
        w_out = sb("w_out", [P, DIM])
        b_out = sb("b_out", [P, DIM])
        rope_q = sb("rope_q", [P, TILES, 2, DIM])
        rope_k = sb("rope_k", [P, TILES, 2, A_KV * A_DH])
        ident = sb("a_ident", [P, P])
        ident_b = sb("a_ident_b", [P, P], bf16)
        mask_q = sb("mask_q", [P, P], bf16)
        mask_k = sb("mask_k", [P, P], bf16)
        x = sb("a_x", [P, TILES, DIM])
        xr = sb("a_xr", [P, TILES, DIM])
        xT = sb("a_xT", [P, SEQ])
        latent = sb("latent", [Q_RANK + KV_RANK, SEQ])
        qkv = sb("qkv", [P, TILES, DIM + 2 * A_KV * A_DH])
        t_cos, t_sin = sb("t_cos", [P, TILES, DIM]), sb("t_sin", [P, TILES, DIM])
        q_rot = sb("q_rot", [P, TILES, DIM])
        k_cos, k_sin = sb("k_cos", [P, TILES, A_KV * A_DH]), sb("k_sin", [P, TILES, A_KV * A_DH])
        k_rot = sb("k_rot", [P, TILES, A_KV * A_DH])
        q_split = sb("q_split", [P, TILES, A_HEADS, 64], bf16)
        k_split = sb("k_split", [P, TILES, A_KV, 2, 64], bf16)
        qx = [sb(f"qx{g}", [P, 2, SEQ], bf16) for g in range(A_KV)]
        kx = [sb(f"kx{g}", [P, SEQ], bf16) for g in range(A_KV)]
        vx = [sb(f"vx{g}", [P, TILES, 32]) for g in range(A_KV)]
        part_max = sb("part_max", [P, 4, 12])
        neg = sb("neg", [P, 4, TILES])
        neg_split = sb("neg_split", [P, 2, 3, 2, TILES], bf16)
        negT = sb("negT", [96, P], bf16)
        probT = [sb(f"a_probT{i}", [P, 2, HALF]) for i in range(3)]
        accT = [sb(f"accT{i}", [P, HALF]) for i in range(2)]
        recip = sb("recip", [P, 4, 4])
        attn = sb("a_attn", [P, TILES, DIM])
        attnT = sb("a_attnT", [P, SEQ])
        z = sb("z", [P, TILES, DIM])
        stats = sb("a_stats", [P, TILES, 6])
        mean_var = sb("a_mean_var", [P, TILES, 2])
        var_eps, rstd, nwt = sb("a_var_eps", [P, TILES]), sb("a_rstd", [P, TILES]), sb("a_nwt", [P, TILES])
        y = sb("a_y", [P, TILES, DIM])

        s_max = [psum(f"s_max{i}", [P, 512]) for i in range(2)]
        s_T = [psum(f"s_T{i}", [P, 2, HALF]) for i in range(2)]
        acc = psum("acc", [P, HALF])
        misc = psum("misc", [P, 512])
        misc_b = misc[:, :].bitcast(bf16)
        fills = MiscFills()

        w_in, x_load, xr_in, y_out = sem("a_w_in"), sem("a_x_load"), sem("a_xr_in"), sem("a_y_out")
        zeroed, masked, ready = sem("a_zeroed"), sem("a_masked"), sem("a_ready")
        m_filled, m_free = sem("m_filled"), sem("m_free")
        max_filled, max_free = sem("max_filled"), sem("max_free")
        st_filled, exp_done, av_done, acc_free = sem("st_filled"), sem("a_exp_done"), sem("av_done"), sem("acc_free")
        split_ready, neg_ready = sem("split_ready"), sem("neg_ready")
        neg_out, neg_in = sem("neg_out"), sem("neg_in")
        y_ready = sem("a_y_ready")
        v_link = sem("a_v_link")
        READY = 3

        block = ctx.enter_context(nc.Block())

        def batches(eng, body):
            body(0)
            with eng.Fori(1, BATCH) as b:
                body(b)

        def later(b):
            return not isinstance(b, int) or b > 0

        @block.sync
        def _(sp):
            def load_x(b):
                sp.dma_start(x[:, :, :], x_in[bass.ds(b, 1), :, :].rearrange("one (t p) d -> p (one t) d", p=P)).then_inc(x_load, 16)

            load_x(0)
            sp.dma_start(w_a[:, 0:Q_RANK], w["Wqa"]).then_inc(w_in, 16)
            sp.dma_start(w_a[:, Q_RANK:], w["Wkva"]).then_inc(w_in, 16)
            sp.wait_ge(zeroed, 1)
            sp.dma_start(w_b[0:Q_RANK, 0:DIM], w["Wqb"]).then_inc(w_in, 16)
            sp.dma_start(w_b[Q_RANK:, DIM:], w["Wkvb"]).then_inc(w_in, 16)
            sp.dma_start(rope_q[:, :, :, :], w["rope_q"]).then_inc(w_in, 16)
            sp.dma_start(rope_k[:, :, :, :], w["rope_k"]).then_inc(w_in, 16)
            sp.dma_start(w_out[:, :], w["Wout"]).then_inc(w_in, 16)
            sp.dma_start(b_out[:, :], w["bout"].rearrange("(one d) -> one d", one=1).to_broadcast([P, DIM])).then_inc(w_in, 16)

            def neg_rows(g, G, number):
                sp.wait_ge(m_free, number + 1)
                sp.dma_start(neg_dram, negT[:, :]).then_inc(neg_out, 16)
                sp.wait_ge(neg_out, 16 * (G + 1))
                for h2 in range(2):
                    row = 64 * h2 + SPLIT
                    sp.dma_start(qx[g][row:row + 3, :, :].rearrange("r j q -> r (j q)"),
                                 neg_dram[48 * h2:48 * h2 + 48, :].rearrange("(r c) q -> r (c q)", r=3)).then_inc(neg_in, 16)

            def body(b):
                if later(b):
                    sp.wait_ge(y_ready, b)
                sp.dma_start(xr[:, :, :], x_in[bass.ds(b, 1), :, :].rearrange("one (t p) d -> p (one t) d", p=P)).then_inc(xr_in, 16)
                sp.wait_ge(m_free, fills.number(b, -1, "xT1") + 1)
                load_x((b + 1) % BATCH)
                for g in range(A_KV):
                    neg_rows(g, A_KV * b + g, fills.number(b, g - 1, "nm"))
                sp.wait_ge(y_ready, b + 1)
                sp.dma_start(x_dram[bass.ds(b, 1), 1:1 + SEQ, :].rearrange("one (t p) d -> p (one t) d", p=P), y[:, :, :]).then_inc(y_out, 16)

            batches(sp, body)
            sp.wait_ge(y_out, 16 * BATCH)
            sp.wait_ge(x_load, 16 * (BATCH + 1))

        @block.tensor
        def _(pe):
            def fill(number):
                if not isinstance(number, int) or number >= 1:
                    pe.wait_ge(m_free, number)

            def prep(num, name):
                n = num(name)
                k = int(name[-1])
                if name[:2] == "xT":
                    fill(n)
                    for t in range(4):
                        last = nc.tensor.transpose(misc[:, P * t:P * (t + 1)], x[:, 4 * k + t, :], ident[:, :])
                elif name[:2] == "pr":
                    fill(n)
                    last = nc.tensor.matmul(misc[0:Q_RANK + KV_RANK, :], w_a[:, :], xT[:, HALF * k:HALF * (k + 1)], start=True, stop=True)
                else:
                    fill(n)
                    for t in range(2):
                        tile = 2 * k + t
                        last = nc.tensor.matmul(misc[:, 192 * t:192 * (t + 1)], latent[:, P * tile:P * (tile + 1)], w_b[:, :],
                                                start=True, stop=True)
                last.then_inc(m_filled, 1)

            def transpose_split(n, g, name):
                fill(n)
                for t in range(TILES):
                    if name == "tk":
                        src = k_split[:, t, g, :, :]
                    else:
                        h = 4 * g + 2 * int(name[-1])
                        src = q_split[:, t, h:h + 2, :]
                    last = nc.tensor.transpose(misc_b[:, P * t:P * (t + 1)], src.rearrange("p a c -> p (a c)"), ident_b[:, :])
                last.then_inc(m_filled, 1)

            def max_unit(g, G, m):
                head, (i, half) = m // 12, MAX_UNITS[m % 12]
                hpl, h2 = divmod(head, 2)
                n = 48 * G + m
                if not isinstance(n, int) or n >= 2:
                    pe.wait_ge(max_free, n - 1)
                bank = s_max[m % 2]
                width = min(512, P * (i + 1) - 512 * half)
                diagonal = P * i // 512 == half
                rows = slice(64 * h2, 64 * h2 + SPLIT)
                last = nc.tensor.matmul(bank[:, 0:width], qx[g][rows, hpl, P * i:P * (i + 1)],
                                        kx[g][rows, 512 * half:512 * half + width],
                                        start=True, stop=not diagonal, skip_group_check=True)
                if diagonal:
                    last = nc.tensor.matmul(bank[:, width - P:width], ident_b[:, :], mask_q[:, :], start=False, stop=True,
                                            skip_group_check=True)
                last.then_inc(max_filled, 1)

            def transposed_scores(g, G, u):
                qb, hpl, kt = UNITS[u]
                n = 24 * G + u
                if not isinstance(n, int) or n >= 2:
                    pe.wait_ge(exp_done, n - 1)
                lo = max(0, P * (kt - 4 * qb))
                diagonal = kt >= 4 * qb
                for h2 in range(2):
                    bank = s_T[u % 2][:, h2, :]
                    rows = slice(64 * h2, 64 * h2 + SPLIT + 3)
                    last = nc.tensor.matmul(bank[:, lo:HALF], kx[g][rows, P * kt:P * (kt + 1)],
                                            qx[g][rows, hpl, HALF * qb + lo:HALF * (qb + 1)],
                                            start=True, stop=not diagonal, skip_group_check=True)
                    if diagonal:
                        last = nc.tensor.matmul(bank[:, lo:lo + P], ident_b[:, :], mask_k[:, :], start=False, stop=True,
                                                skip_group_check=True)
                last.then_inc(st_filled, 1)

            def times_v(g, G, u):
                qb, hpl, kt = UNITS[u]
                pe.wait_ge(exp_done, 24 * G + u + 1)
                if kt == 0 and hpl == 0:
                    n = 2 * G + qb
                    if not isinstance(n, int) or n >= 1:
                        pe.wait_ge(acc_free, n)
                lo = max(0, P * (kt - 4 * qb))
                for h2 in range(2):
                    q = 32 * (2 * hpl + h2)
                    last = nc.tensor.matmul(acc[q:q + 32, lo:HALF], vx[g][:, kt, :], probT[u % 3][:, h2, lo:HALF],
                                            start=(kt == 0), stop=(kt == 4 * qb + 3), skip_group_check=True)
                last.then_inc(av_done, 1)

            def transpose_max(n):
                fill(n)
                nc.tensor.transpose(misc_b[0:96, 0:P], neg_split[:, :, :, :, :].rearrange("p a r j i -> p (a r j i)"),
                                    ident_b[:, :]).then_inc(m_filled, 1)

            def transpose_acc(n, qb):
                fill(n)
                for t in range(4):
                    last = nc.tensor.transpose(misc[:, P * t:P * (t + 1)], accT[qb][:, P * t:P * (t + 1)], ident[:, :])
                last.then_inc(m_filled, 1)

            pe.wait_ge(ready, READY)
            pe.wait_ge(w_in, 16 * 8)

            def body(b):
                num = lambda name: fills.number(b, -1, name)
                pe.wait_ge(x_load, 16 * (b + 1))
                for name in ("xT0", "xT1", "pr0", "pr1", "kv0", "kv1", "kv2", "kv3"):
                    prep(num, name)
                pe.wait_ge(split_ready, b + 1)
                for name in ("tq0", "tq1", "tk"):
                    transpose_split(num(name), 0, name)
                pe.wait_ge(m_free, num("tk") + 1)
                for m in range(48):
                    max_unit(0, A_KV * b, m)
                pe.wait_ge(neg_ready, A_KV * b + 1)
                transpose_max(num("nm"))
                for g in range(A_KV):
                    attend(b, g)
                num = lambda name: fills.number(b, A_KV, name)
                for k in range(2):
                    fill(num(f"ao{k}"))
                    for t in range(4):
                        last_t = nc.tensor.transpose(misc[:, P * t:P * (t + 1)], attn[:, 4 * k + t, :], ident[:, :])
                    last_t.then_inc(m_filled, 1)
                for k in range(2):
                    fill(num(f"y{k}"))
                    for t in range(4):
                        tile = 4 * k + t
                        last_t = nc.tensor.matmul(misc[:, P * t:P * (t + 1)], attnT[:, P * tile:P * (tile + 1)], w_out[:, :],
                                                  start=True, stop=True)
                    last_t.then_inc(m_filled, 1)

            def attend(b, g):
                G = A_KV * b + g
                num = lambda name: fills.number(b, g, name)
                pe.wait_ge(neg_in, 32 * (G + 1))
                transposed_scores(g, G, 0)
                m = 0
                for u in range(len(UNITS)):
                    if u + 1 < len(UNITS):
                        transposed_scores(g, G, u + 1)
                    for name in fills.at_unit(g, u):
                        if name == "oa0":
                            pe.wait_ge(acc_free, 2 * G + 1)
                            transpose_acc(num(name), 0)
                        elif name == "nm":
                            pe.wait_ge(neg_ready, G + 2)
                            transpose_max(num(name))
                        else:
                            transpose_split(num(name), g + 1, name)
                    if g < A_KV - 1 and u >= FIRST_MAX:
                        if u == FIRST_MAX:
                            pe.wait_ge(m_free, num("tk") + 1)
                        for m in maxima_at(u):
                            max_unit(g + 1, G + 1, m)
                    times_v(g, G, u)
                pe.wait_ge(acc_free, 2 * G + 2)
                transpose_acc(num("oa1"), 1)

            batches(pe, body)

        @block.scalar
        def _(act):
            def filled(n):
                act.wait_ge(m_filled, n + 1)

            def prep(num, name):
                filled(num(name))
                k = int(name[-1])
                if name[:2] == "xT":
                    nc.scalar.activation(xT[:, HALF * k:HALF * (k + 1)], misc[:, :], ACT.Copy).then_inc(m_free, 1)
                elif name[:2] == "pr":
                    r = Q_RANK + KV_RANK
                    nc.scalar.activation(latent[:, HALF * k:HALF * (k + 1)], misc[0:r, :], ACT.Copy).then_inc(m_free, 1)
                else:
                    nc.scalar.activation(qkv[:, 2 * k:2 * k + 2, :], misc[:, 0:384].rearrange("p (t c) -> p t c", t=2),
                                         ACT.Copy).then_inc(m_free, 1)

            def split_out(n, g, name):
                filled(n)
                out = kx[g][:, :] if name == "tk" else qx[g][:, int(name[-1]), :]
                nc.scalar.activation(out, misc_b, ACT.Copy).then_inc(m_free, 1)

            def neg_evacuate(n):
                filled(n)
                nc.scalar.activation(negT[:, :], misc_b[0:96, 0:P], ACT.Copy).then_inc(m_free, 1)

            def body(b):
                num = lambda name: fills.number(b, -1, name)
                for name in ("xT0", "xT1", "pr0", "pr1", "kv0", "kv1", "kv2", "kv3"):
                    prep(num, name)
                for name in ("tq0", "tq1", "tk"):
                    split_out(num(name), 0, name)
                neg_evacuate(num("nm"))
                for g in range(A_KV):
                    G = A_KV * b + g
                    num = lambda name: fills.number(b, g, name)
                    for u, (qb, hpl, kt) in enumerate(UNITS):
                        n = 24 * G + u
                        act.wait_ge(st_filled, n + 1)
                        if not isinstance(n, int) or n >= 3:
                            act.wait_ge(av_done, n - 2)
                        lo = max(0, P * (kt - 4 * qb))
                        nc.scalar.activation(probT[u % 3][:, :, lo:HALF], s_T[u % 2][:, :, lo:HALF], ACT.Exp).then_inc(exp_done, 1)
                        if u == 8:
                            evacuate(G, 0)
                        for name in fills.at_unit(g, u):
                            if name == "nm":
                                neg_evacuate(num(name))
                            elif name != "oa0":
                                split_out(num(name), g + 1, name)
                    evacuate(G, 1)
                for k in range(2):
                    filled(fills.number(b, A_KV, f"ao{k}"))
                    nc.scalar.activation(attnT[:, HALF * k:HALF * (k + 1)], misc[:, :], ACT.Copy).then_inc(m_free, 1)

            def evacuate(G, qb):
                act.wait_ge(av_done, 24 * G + (24 if qb else 8))
                nc.scalar.activation(accT[qb][:, :], acc[:, :], ACT.Copy).then_inc(acc_free, 1)

            batches(act, body)

        @block.vector
        def _(dve):
            links = [0]

            def link(ins):
                links[0] += 1
                ins.then_inc(v_link, 1)
                dve.wait_ge(v_link, links[0])

            def rope():
                q_in = qkv[:, :, 0:DIM]
                nc.vector.tensor_tensor(t_cos[:, :, :], q_in, rope_q[:, :, 0, :], ALU.mult)
                nc.vector.tensor_tensor(t_sin[:, :, :].rearrange("p t (c r) -> p t c r", r=2),
                                        q_in.rearrange("p t (c r) -> p t c r", r=2)[:, :, :, ::-1],
                                        rope_q[:, :, 1, :].rearrange("p t (c r) -> p t c r", r=2), ALU.mult)
                k_in = qkv[:, :, DIM:].rearrange("p t (c r v) -> p t c r v", r=2, v=2)[:, :, :, :, 0]
                nc.vector.tensor_tensor(k_cos[:, :, :].rearrange("p t (c r) -> p t c r", r=2), k_in,
                                        rope_k[:, :, 0, :].rearrange("p t (c r) -> p t c r", r=2), ALU.mult)
                link(nc.vector.tensor_tensor(k_sin[:, :, :].rearrange("p t (c r) -> p t c r", r=2), k_in[:, :, :, ::-1],
                                             rope_k[:, :, 1, :].rearrange("p t (c r) -> p t c r", r=2), ALU.mult))
                nc.vector.tensor_tensor(q_rot[:, :, :], t_cos[:, :, :], t_sin[:, :, :], ALU.add)
                link(nc.vector.tensor_tensor(k_rot[:, :, :], k_cos[:, :, :], k_sin[:, :, :], ALU.add))

            def split():
                qs = [q_split[:, :, :, A_DH * j:A_DH * (j + 1)] for j in range(PARTS)]
                ks = [[k_split[:, :, :, d, A_DH * j:A_DH * (j + 1)] for d in range(2)] for j in range(PARTS)]
                q_f = q_rot[:, :, :].rearrange("p t (h d) -> p t h d", d=A_DH)
                k_f = k_rot[:, :, :].rearrange("p t (h d) -> p t h d", d=A_DH)
                for part in range(3):
                    mine_q = [j for j in range(PARTS) if Q_PART[j] == part]
                    mine_k = [j for j in range(PARTS) if K_PART[j] == part]
                    nc.vector.tensor_copy(qs[mine_q[0]], q_f)
                    link(nc.vector.tensor_copy(ks[mine_k[0]][0], k_f))
                    if part < 2:
                        nc.vector.tensor_tensor(q_f, q_f, qs[mine_q[0]], ALU.subtract)
                        nc.vector.tensor_tensor(k_f, k_f, ks[mine_k[0]][0], ALU.subtract)
                    for j in mine_q[1:]:
                        nc.vector.tensor_copy(qs[j], qs[mine_q[0]])
                    for j in mine_k:
                        for d in range(2):
                            if (j, d) != (mine_k[0], 0):
                                last = nc.vector.tensor_copy(ks[j][d], ks[mine_k[0]][0])
                    if part < 2:
                        link(last)
                last.then_inc(split_ready, 1)

            def copy_v(g):
                v_in = qkv[:, :, DIM + 16 * g:DIM + 16 * (g + 1)].rearrange("p t (d v) -> p t d v", v=2)[:, :, :, 1]
                nc.vector.tensor_copy(vx[g][:, :, 0:A_DH], v_in)

            def reduce_unit(G, m):
                head, (i, half) = m // 12, MAX_UNITS[m % 12]
                n = 48 * G + m
                dve.wait_ge(max_filled, n + 1)
                width = min(512, P * (i + 1) - 512 * half)
                col = i + 4 * half
                nc.vector.tensor_reduce(part_max[:, head, col:col + 1], s_max[m % 2][:, 0:width], AX.X, ALU.max).then_inc(max_free, 1)

            def split_max(G):
                dve.wait_ge(max_free, 48 * (G + 1))
                link(nc.vector.tensor_tensor(part_max[:, :, 4:8], part_max[:, :, 4:8], part_max[:, :, 8:12], ALU.max))
                link(nc.vector.tensor_scalar(neg[:, :, :], part_max[:, :, 0:8], -1.0, None, ALU.mult))
                rest = neg[:, :, :].rearrange("p (j a) i -> p j a i", a=2)
                for r in range(3):
                    part = neg_split[:, :, r, :, :].rearrange("p a j i -> p j a i")
                    ins = nc.vector.tensor_copy(part, rest)
                    if r == 2:
                        ins.then_inc(neg_ready, 1)
                    else:
                        link(ins)
                        link(nc.vector.tensor_tensor(rest, rest, part, ALU.subtract))

            def normalise(g, qb, n):
                dve.wait_ge(m_filled, n + 1)
                heads = misc[:, :].rearrange("p (t h c) -> p t h c", t=4, c=32)
                link(nc.vector.reciprocal(recip[:, :, :], heads[:, :, :, A_DH]))
                nc.vector.tensor_tensor(
                    attn[:, 4 * qb:4 * qb + 4, 32 * g:32 * (g + 1)].rearrange("p t (h d) -> p t h d", d=A_DH),
                    heads[:, :, :, 0:A_DH], recip[:, :, :].unsqueeze(3).to_broadcast([P, 4, 4, A_DH]), ALU.mult).then_inc(m_free, 1)

            nc.vector.memset(w_b[:, :], 0.0).then_inc(zeroed, 1)
            nc.vector.memset(q_split[:, :, :, :], 0.0)
            nc.vector.memset(k_split[:, :, :, :, :], 0.0)
            for g in range(A_KV):
                nc.vector.memset(vx[g][:, :, :], 0.0)
            link(nc.vector.memset(recip[:, :, :], 0.0))
            for g in range(A_KV):
                nc.vector.memset(vx[g][:, :, A_DH:A_DH + 1], 1.0)
            nc.vector.memset(k_split[:, :, :, :, SPLIT:SPLIT + 3], 1.0).then_inc(ready, 1)
            dve.wait_ge(masked, 3)
            link(nc.vector.tensor_copy(ident_b[:, :], ident[:, :]))
            nc.vector.memset(recip[:, :, :], 0.0).then_inc(ready, 1)

            dve.wait_ge(w_in, 16 * 8)

            def body(b):
                dve.wait_ge(m_free, fills.number(b, -1, "kv3") + 1)
                rope()
                for g in range(A_KV):
                    copy_v(g)
                split()
                for m in range(48):
                    reduce_unit(A_KV * b, m)
                split_max(A_KV * b)
                for g in range(A_KV):
                    G = A_KV * b + g
                    for u in range(len(UNITS)):
                        if u == 11:
                            normalise(g, 0, fills.number(b, g, "oa0"))
                        if g < A_KV - 1:
                            for m in maxima_at(u):
                                reduce_unit(G + 1, m)
                                if m == 47:
                                    split_max(G + 1)
                    normalise(g, 1, fills.number(b, g, "oa1"))
                dve.wait_ge(xr_in, 16 * (b + 1))
                for k in range(2):
                    dve.wait_ge(m_filled, fills.number(b, A_KV, f"y{k}") + 1)
                    nc.vector.tensor_tensor(z[:, 4 * k:4 * k + 4, :], misc[:, :].rearrange("p (t d) -> p t d", t=4),
                                            xr[:, 4 * k:4 * k + 4, :], ALU.add).then_inc(m_free, 1)
                dve.wait_ge(m_free, fills.number(b, A_KV, "y1") + 1)
                link(nc.vector.tensor_tensor(z[:, :, :], z[:, :, :], b_out[:, :].unsqueeze(1).to_broadcast([P, TILES, DIM]), ALU.add))
                if later(b):
                    dve.wait_ge(y_out, 16 * b)
                layer_norm(nc, link, z, y, TILES, stats, mean_var, var_eps, rstd, nwt, lambda ins: ins.then_inc(y_ready, 1))
                nc.vector.sem_clear(v_link)
                links[0] = 0

            nc.vector.sem_clear(v_link)
            links[0] = 0
            batches(dve, body)

        @block.gpsimd
        def _(pool):
            nc.gpsimd.memset(ident[:, :], 0.0).then_inc(masked, 1)
            nc.gpsimd.memset(mask_q[:, :], 0.0).then_inc(masked, 1)
            pool.wait_ge(masked, 2)
            nc.gpsimd.affine_select(out=ident[:, :], in_=ident[:, :], compare_op=ALU.not_equal, fill=1.0, base=0,
                                    pattern=[[-1, P]], channel_multiplier=1).then_inc(masked, 1)
            nc.gpsimd.affine_select(out=mask_k[:, :], in_=mask_q[:, :], compare_op=ALU.is_ge, fill=MASKED, base=0,
                                    pattern=[[1, P]], channel_multiplier=-1).then_inc(masked, 1)
            pool.wait_ge(masked, 4)
            nc.gpsimd.affine_select(out=mask_q[:, :], in_=mask_q[:, :], compare_op=ALU.is_ge, fill=MASKED, base=0,
                                    pattern=[[-1, P]], channel_multiplier=1).then_inc(ready, 1)


def layer_norm(nc, link, src, out, tiles, stats, mean_var, var_eps, rstd, tmp, last):
    for t in range(tiles):
        ins = nc.vector.bn_stats(stats[:, t, :], src[:, t, :])
    link(ins)
    for t in range(tiles):
        ins = nc.vector.bn_aggr(mean_var[:, t, :], stats[:, t, :])
    link(ins)
    link(nc.vector.tensor_scalar(var_eps[:, 0:tiles], mean_var[:, 0:tiles, 1], 1e-5, None, ALU.add))
    rsqrt(nc, link, rstd[:, 0:tiles], var_eps[:, 0:tiles], tmp[:, 0:tiles], link)
    for t in range(tiles):
        ins = nc.vector.tensor_scalar(out[:, t, :], src[:, t, :], mean_var[:, t, 0:1], rstd[:, t:t + 1], ALU.subtract, ALU.mult)
    last(ins)


def closing_norm(nc, x_dram, out):
    with ExitStack() as ctx:
        def sb(name, shape, dt=fp32):
            return ctx.enter_context(nc.sbuf_tensor(name, shape, dt))

        def sem(name):
            return ctx.enter_context(nc.semaphore(name))

        x_first = [sb(f"x_first{b}", [P, TILES, DIM]) for b in range(BATCH)]
        x_last = [sb(f"x_last{b}", [P, TILES, DIM]) for b in range(BATCH)]
        normed = [sb(f"normed{b}", [P, TILES, DIM]) for b in range(BATCH)]
        stats = sb("c_stats", [P, TILES, 6])
        mean_var = sb("c_mean_var", [P, TILES, 2])
        var_eps, rstd, nwt = (sb(f"c_{n}", [P, TILES]) for n in ("var_eps", "rstd", "nwt"))
        loaded = [sem(f"c_loaded{b}") for b in range(BATCH)]
        norm_done, stored, v_link = sem("c_norm_done"), sem("c_stored"), sem("c_v_link")
        block = ctx.enter_context(nc.Block())

        def tiled(rows):
            return rows.rearrange("(t p) d -> p t d", p=P)

        @block.sync
        def _(sp):
            for b in range(BATCH):
                sp.dma_start(x_first[b][:, :, :], tiled(x_dram[b, 1:1 + SEQ, :])).then_inc(loaded[b], 16)
                sp.dma_start(x_last[b][:, :, :], tiled(x_dram[ROUNDS + b, 1:1 + SEQ, :])).then_inc(loaded[b], 16)
            for b in range(BATCH):
                sp.wait_ge(norm_done, b + 1)
                sp.dma_start(tiled(out[b, :, :]), normed[b][:, :, :]).then_inc(stored, 16)
            sp.wait_ge(stored, 16 * BATCH)

        @block.vector
        def _(dve):
            links = [0]

            def link(ins):
                links[0] += 1
                ins.then_inc(v_link, 1)
                dve.wait_ge(v_link, links[0])

            for b in range(BATCH):
                dve.wait_ge(loaded[b], 32)
                link(nc.vector.tensor_tensor(x_first[b][:, :, :], x_first[b][:, :, :], x_last[b][:, :, :], ALU.add))
                layer_norm(nc, link, x_first[b], normed[b], TILES, stats, mean_var, var_eps, rstd, nwt,
                           lambda ins: ins.then_inc(norm_done, 1))


def clear_first_rows(nc, x_dram, x1_dram):
    with ExitStack() as ctx:
        zeros = ctx.enter_context(nc.sbuf_tensor("zeros", [P, DIM], fp32))
        zeroed, rows_out = ctx.enter_context(nc.semaphore("zeroed")), ctx.enter_context(nc.semaphore("rows_out"))
        block = ctx.enter_context(nc.Block())

        @block.vector
        def _(dve):
            nc.vector.memset(zeros[:, :], 0.0).then_inc(zeroed, 1)

        @block.sync
        def _(sp):
            sp.wait_ge(zeroed, 1)
            sp.dma_start(x_dram[:, 0, :], zeros[0:ROUNDS + BATCH, :]).then_inc(rows_out, 16)
            sp.dma_start(x1_dram[0:1, :], zeros[0:1, :]).then_inc(rows_out, 16)
            sp.wait_ge(rows_out, 32)


def build(nc, w, out):
    x_dram = nc.dram_tensor("x_layers", [ROUNDS + BATCH, 1 + SEQ, DIM], fp32, kind="Internal").ap()
    x1_dram = nc.dram_tensor("x1", [1 + SEQ, DIM], fp32, kind="Internal").ap()
    neg_dram = nc.dram_tensor("neg_max", [96, P], bf16, kind="Internal").ap()
    clear_first_rows(nc, x_dram, x1_dram)
    mla_attention(nc, w["x"], x_dram, neg_dram, w)
    local_layers(nc, x_dram, x1_dram, w)
    closing_norm(nc, x_dram, out)



def rope_tables(np):
    D = A_DH
    inv_freq = 1.0 / 10000.0 ** (np.arange(0, D, 2, dtype=np.float32) / np.float32(D))
    freqs = (np.arange(SEQ, dtype=np.float32)[:, None] * inv_freq.astype(np.float32)[None, :]).astype(np.float64)
    cos = np.repeat(np.cos(freqs), 2, axis=1)
    sin = np.repeat(np.sin(freqs), 2, axis=1) * np.where(np.arange(D) % 2, 1.0, -1.0)
    tables = []
    for heads, scale in ((A_HEADS, D ** -0.5), (A_KV, 1.0)):
        both = np.stack([np.tile(cos, (1, heads)), np.tile(sin, (1, heads))], 1) * scale
        both = both.reshape(TILES, P, 2, heads * D).transpose(1, 0, 2, 3)
        tables.append(np.ascontiguousarray(both.astype(np.float32)))
    return tables


def rotary_table(np):
    half = np.arange(0, DH, 2, dtype=np.float32)
    inv_freq = (1.0 / np.power(np.float32(10000.0), half / np.float32(DH))).astype(np.float32)
    t = np.arange(SEQ, dtype=np.float32)
    freqs = (t[:, None] * inv_freq[None, :]).astype(np.float64)
    freqs = np.concatenate([freqs, freqs], -1)
    base_scale = ((half + np.float32(0.4 * DH)) / np.float32(1.4 * DH)).astype(np.float64)
    power = ((t - SEQ // 2) / (WINDOW // 2)).astype(np.float64)
    scale = base_scale[None, :] ** power[:, None]
    scale = np.concatenate([scale, scale], -1)
    cos, sin = np.cos(freqs), np.sin(freqs) * np.where(np.arange(DH) < DH // 2, -1.0, 1.0)
    rows = np.stack([cos * scale * QK_SCALE, sin * scale * QK_SCALE, cos / scale, sin / scale], 1)
    return np.ascontiguousarray(rows.reshape(TILES, P, 4, DH).transpose(1, 0, 2, 3).astype(np.float32))


def pack_vectors(np, a):
    def swap(v):
        return np.concatenate([v[:, DH // 2:], v[:, :DH // 2]], 1)

    qs, ks = a["L0_ffn_q_scale"], a["L0_ffn_k_scale"]
    qk_rows = np.concatenate([qs, swap(qs), ks, swap(ks)], 1)
    small = np.zeros((DEPTH, P, N_SMALL), np.float32)
    small[:, :, SMALL["g"]], small[:, :, SMALL["b"]] = a["L0_ffn_ln_g"], a["L0_ffn_ln_b"]
    for k, (first, width) in enumerate(FF_BLOCKS):
        small[:, :width, SMALL["b1a"] + k] = a["L0_ffn_b1"][:, first:first + width]
        small[:, :width, SMALL["b1g"] + k] = a["L0_ffn_b1"][:, FF + first:FF + first + width]
    small[:, :, SMALL["b2"]] = a["L0_ffn_b2"]
    return np.ascontiguousarray(qk_rows), small


def kernel(**inputs):
    import numpy as np
    import concourse.bacc as bacc
    from concourse.bass_utils import run_bass_kernel_spmd

    nc = bacc.Bacc("TRN2", target_bir_lowering=False, num_devices=1)
    a = {name: np.ascontiguousarray(value) for name, value in inputs.items()}
    rope_q, rope_k = rope_tables(np)
    qk_rows, small = pack_vectors(np, a)
    tensors = dict(x=a["L0_attn_x"], Wqa=a["L0_attn_Wqa"], Wqb=a["L0_attn_Wqb"], Wkva=a["L0_attn_Wkva"],
                   Wkvb=a["L0_attn_Wkvb"], Wout=a["L0_attn_Wout"], bout=a["L0_attn_bout"], rope_q=rope_q, rope_k=rope_k,
                   Wqkv=a["L0_ffn_Wqkv"], Wo=a["L0_ffn_Wo"], W1=a["L0_ffn_W1"], W2=a["L0_ffn_W2"],
                   qk_rows=qk_rows, small=small, rotary=rotary_table(np))
    arrays = {f"in_{name}_dram": value for name, value in tensors.items()}
    w = {name: nc.dram_tensor(f"in_{name}_dram", value.shape, fp32, kind="ExternalInput").ap()
         for name, value in tensors.items()}
    out = nc.dram_tensor("out_dram", (BATCH, SEQ, DIM), fp32, kind="ExternalOutput").ap()
    build(nc, w, out)
    return run_bass_kernel_spmd(nc, [arrays], core_ids=[0]).results[0]["out_dram"]
```

```python
import concourse.bass as bass
from concourse import mybir
from contextlib import ExitStack

fp32 = mybir.dt.float32
bf16 = mybir.dt.bfloat16
i32 = mybir.dt.int32
ALU = mybir.AluOpType
ACT = mybir.ActivationFunctionType
AX = mybir.AxisListType

P = 128
BATCH, SEQ, DIM = 4, 1024, 128
MASKED = -1e30

DEPTH, HEADS, DH, WINDOW = 6, 16, 64, 32
INNER = HEADS * DH
FF = DIM * 4 * 2 // 3
FF_BLOCKS = [(0, 128), (128, 128), (256, FF - 256)]
QK_SCALE = 8.0
PAIR = 2 * P
POS = SEQ // PAIR
ROUNDS = DEPTH * BATCH
PAIRS = ROUNDS * POS
MAX_LAG = 3
HP = HEADS // 2
RSQRT_MAGIC = 0x5F3759DF

SMALL = dict(g=0, b=1, b1a=2, b1g=5, b2=8)
N_SMALL = 9


class Ring:

    def __init__(self, stage_names):
        self.stage_names = stage_names
        self.full = len(stage_names)
        assert self.full % 3 == 0

    def names(self, t):
        return [s for s, lag in self.stage_names if not isinstance(t, int) or 0 <= t - lag < PAIRS]

    def before(self, t):
        if isinstance(t, int) and t < MAX_LAG:
            return sum(len(self.names(s)) for s in range(-1, t))
        if isinstance(t, int) and t > PAIRS:
            return self.before(t - 1) + len(self.names(t - 1))
        return self.full * (t - MAX_LAG) + self.before_full()

    def before_full(self):
        return sum(len(self.names(s)) for s in range(-1, MAX_LAG))

    def at(self, step, name):
        j = self.names(step.t).index(name)
        before = self.before(step.t)
        slot = ((before if isinstance(before, int) else self.before_full()) + j) % 3
        return slot, before + j


class Step:

    def __init__(self, f, p):
        self.f, self.p = f, p
        self.t = POS * f + p

    def pair(self, lag):
        return Pair(self, lag)


class Pair:

    def __init__(self, step, lag):
        self.step, self.lag = step, lag
        q = step.p - lag
        self.p = q % POS
        self.f = step.f + q // POS
        self.n = step.t - lag
        self.par = self.p % 2
        self.k = 2 * self.f + self.p // 2
        self.exists = not isinstance(self.n, int) or 0 <= self.n < PAIRS


def layer_of(f):
    return (f // BATCH) % DEPTH


def dram_rows(region, f, row, count):
    return region[bass.ds(f, 1), row:row + count, :].rearrange("one t d -> (one t) d")


def local_layers(nc, x_dram, x1_dram, w):
    with ExitStack() as ctx:
        def sb(name, shape, dt=fp32):
            return ctx.enter_context(nc.sbuf_tensor(name, shape, dt))

        def sem(name):
            return ctx.enter_context(nc.semaphore(name))

        w_qkv = sb("w_qkv", [P, 3 * INNER])
        w_o = sb("w_o", [P, HP, DIM])
        w_1 = sb("w_1", [P, 2 * FF])
        w_2 = sb("w_2", [P, 3, DIM])
        small = sb("small", [P, N_SMALL])
        qk_row = sb("qk_row", [P, 4, DH])
        rotary = sb("rotary", [P, SEQ // P, 4, DH])
        table = sb("table", [P, SEQ // P, 4, DH])
        ident = sb("ident", [P, P])
        ident_b = sb("ident_b", [P, P], bf16)
        mask = sb("mask", [P, 2, 4, 2, 2 * WINDOW], bf16)
        xs = [sb(f"xs{i}", [P, 2, DIM]) for i in range(2)]
        xr = [sb(f"xr{i}", [P, 2, DIM]) for i in range(2)]
        xs1 = [sb(f"xs1{i}", [P, 2, DIM]) for i in range(2)]
        x1 = [sb(f"x1{i}", [P, 2, DIM]) for i in range(2)]
        x2 = [sb(f"x2{i}", [P, 2, DIM]) for i in range(2)]
        xT = sb("xT", [P, PAIR])
        sq = [sb(f"sq{i}", [P, 8, DH]) for i in range(2)]
        by_cos = sb("by_cos", [P, 2, 2 * INNER])
        by_sin = sb("by_sin", [P, 2, 2 * INNER])
        qk_rot = sb("qk_rot", [P, 2, 2 * INNER])
        ss = sb("ss", [P, 2, 2 * HEADS + 2])
        rnorm = sb("rnorm", [P, 2, 2 * HEADS + 2])
        newton = sb("newton", [P, 2 * HEADS + 2])
        v = [sb(f"v{i}", [P, 2, INNER]) for i in range(2)]
        v_back = [sb(f"v_back{i}", [P, 2, INNER]) for i in range(2)]
        qT = sb("qT", [P, HP, PAIR])
        kT = [sb(f"kT{i}", [P, HP, WINDOW + PAIR]) for i in range(2)]
        prob = [sb(f"prob{i}", [P, HEADS, 2 * WINDOW]) for i in range(2)]
        row_max = sb("row_max", [P, 2, HEADS])
        row_sum = sb("row_sum", [P, 2, HEADS])
        inv_sum = sb("inv_sum", [P, 2, HEADS])
        probT = [sb(f"probT{i}", [P, HP, P]) for i in range(2)]
        attn = sb("attn", [P, 2, INNER])
        attnT = sb("attnT", [P, HP, PAIR])
        yT = sb("yT", [P, PAIR])
        y2T = sb("y2T", [P, PAIR])
        stats = sb("stats", [P, 2, 6])
        mean_var = sb("mean_var", [P, 2, 2])
        xn = sb("xn", [P, 2, DIM])
        xnT = sb("xnT", [P, PAIR])
        gate = sb("gate", [P, 3, PAIR])
        hidden = sb("hidden", [P, 3, PAIR])

        bank_d = [ctx.enter_context(nc.psum_tensor(f"bank_d{i}", [P, 512], fp32)) for i in range(3)]
        scores = ctx.enter_context(nc.psum_tensor("scores", [P, HP, 2, 2 * WINDOW], fp32))
        bank_a = [ctx.enter_context(nc.psum_tensor(f"bank_a{i}", [P, 512], fp32)) for i in range(3)]

        chunks = [(a, kind, c) for a in range(2) for kind in "qk" for c in range(2)]
        chunks += [(a, "v", c) for a in range(2) for c in range(2)]
        qk_chunks, v_chunks = chunks[:8], chunks[8:]
        EARLY = 4
        early, late = [(x, -1) for x in qk_chunks[:EARLY]], [(x, 0) for x in qk_chunks[EARLY:]]
        v0, v1, v2, v3 = ((x, 0) for x in v_chunks)
        ring_d = Ring(late + [v0, ("yT", 2), ("aA", 3), v1, ("aB", 3), v2, ("y", 2), v3]
                      + [("xT", -1)] + early + [("y2", 3)])
        ring_a = Ring([(f"qk{i}", 1) for i in range(8)]
                      + [("xn", 3), ("gA", 3), ("PT0", 1), ("PT1", 1), ("gB", 3), ("PT2", 1), ("PT3", 1)]
                      + [("O0", 1), ("O2", 1), ("O1", 1), ("OT0", 1), ("O3", 1), ("OT2", 1), ("y2T", 3)]
                      + [("OT1", 1), ("OT3", 1)])

        constants_ready = sem("constants_ready")
        rotary_in = sem("rotary_in")
        zeros_ready = sem("zeros_ready")
        xs_in = [sem(f"xs_in{i}") for i in range(2)]
        xr_in = [sem(f"xr_in{i}") for i in range(2)]
        xs1_in = [sem(f"xs1_in{i}") for i in range(2)]
        v_back_in = [sem(f"v_back_in{i}") for i in range(2)]
        x1_out, x2_out = sem("x1_out"), sem("x2_out")
        wqk_in, wv_in, wo_in, wffn_in, qkrow_in = sem("wqk_in"), sem("wv_in"), sem("wo_in"), sem("wffn_in"), sem("qkrow_in")
        d_filled, d_free = sem("d_filled"), sem("d_free")
        a_filled, a_free = sem("a_filled"), sem("a_free")
        squared = sem("squared")
        norm_ready = sem("norm_ready")
        qk_ready = sem("qk_ready")
        table_ready = sem("table_ready")
        scores_ready, scores_used = sem("scores_ready"), sem("scores_used")
        maximum = sem("maximum")
        exp_done, inv_ready, prob_ready = sem("exp_done"), sem("inv_ready"), sem("prob_ready")
        xn_ready = sem("xn_ready")
        v_link = sem("v_link")
        p_link = sem("p_link")

        INIT = 4
        block = ctx.enter_context(nc.Block())

        def rounds(eng, step_fn, last_fn=None):
            for p in range(POS):
                step_fn(Step(0, p))
            with eng.Fori(1, ROUNDS) as f:
                for p in range(POS):
                    step_fn(Step(f, p))
            for t in range(PAIRS, PAIRS + MAX_LAG):
                step_fn(Step(ROUNDS, t - PAIRS))

        def prev(s):
            return Step(s.f, s.p - 1) if s.p else Step(s.f - 1, POS - 1)

        def chunk_at(pair, i):
            s = pair.step
            if i < EARLY and pair.lag == 0:
                s = prev(s)
            return ring_d.at(s, chunks[i])

        def in_rounds(s):
            return not isinstance(s.t, int) or s.t < PAIRS

        def later(n, first=1):
            return not isinstance(n, int) or n >= first

        def runs(pair):
            return pair.exists

        @block.sync
        def _(sp):
            def load_w_qkv(f, lo, hi, done):
                sp.dma_start(w_qkv[:, lo:hi], w["Wqkv"][bass.ds(layer_of(f), 1), :, lo:hi]
                             .rearrange("one k n -> (one k) n")).then_inc(done, 16)

            def load_qk_rows(f):
                sp.dma_start(qk_row[:, :, :], w["qk_rows"][bass.ds(layer_of(f), 1), :]
                             .rearrange("one (r d) -> one r d", d=DH).to_broadcast([P, 4, DH])).then_inc(qkrow_in, 16)

            def load_wo(f):
                sp.dma_start(w_o[:, :, :], w["Wo"][bass.ds(layer_of(f), 1), :, :]
                             .rearrange("one (c k) n -> k (one c) n", k=P)).then_inc(wo_in, 16)

            def load_ffn(f):
                layer = bass.ds(layer_of(f), 1)
                sp.dma_start(w_1[:, :], w["W1"][layer, :, :].rearrange("one k n -> (one k) n")).then_inc(wffn_in, 16)
                sp.dma_start(w_2[:, 0:2, :], w["W2"][layer, 0:2 * P, :]
                             .rearrange("one (c k) n -> k (one c) n", k=P)).then_inc(wffn_in, 16)
                sp.dma_start(w_2[0:FF - 2 * P, 2, :], w["W2"][layer, 2 * P:FF, :]
                             .rearrange("one k n -> (one k) n")).then_inc(wffn_in, 16)
                sp.dma_start(small[:, :], w["small"][layer, :, :].rearrange("one k n -> (one k) n")).then_inc(wffn_in, 16)

            def load_shifted(dst, region, f, p, s):
                row = 1 + PAIR * p
                lo = dram_rows(region, f, row, PAIR).rearrange("(a t) d -> t a d", a=2)
                hi = dram_rows(region, f, row - 1, PAIR).rearrange("(a t) d -> t a d", a=2)
                sp.dma_start(dst[:, :, 0:DIM // 2], lo[:, :, 0:DIM // 2]).then_inc(s, 16)
                sp.dma_start(dst[:, :, DIM // 2:DIM], hi[:, :, DIM // 2:DIM]).then_inc(s, 16)

            def load_xs(pair):
                load_shifted(xs[pair.par], x_dram, pair.f, pair.p, xs_in[pair.par])

            sp.dma_start(rotary[:, :, :, :], w["rotary"]).then_inc(rotary_in, 16)
            load_xs(Step(0, 0).pair(0))
            load_w_qkv(0, 0, 2 * INNER, wqk_in)
            load_qk_rows(0)
            load_w_qkv(0, 2 * INNER, 3 * INNER, wv_in)
            load_wo(0)
            load_ffn(0)

            def step(s):
                new, now, back1, back2, back3 = (s.pair(lag) for lag in (-1, 0, 1, 2, 3))
                if not isinstance(s.t, int) or s.t > MAX_LAG:
                    sp.wait_ge(x2_out, 16 * (s.t - MAX_LAG))
                if runs(now):
                    load_xs(new)
                if runs(back2):
                    sp.dma_start(xr[back2.par][:, :, :], dram_rows(x_dram, back2.f, 1 + PAIR * back2.p, PAIR)
                                 .rearrange("(a t) d -> t a d", a=2)).then_inc(xr_in[back2.par], 16)
                if runs(now) and s.p == 0:
                    sp.wait_ge(table_ready, s.f + 1)
                    load_qk_rows(s.f + 1)
                if runs(now) and s.p == POS - 1:
                    sp.wait_ge(d_filled, chunk_at(now, 7)[1] + 1)
                    load_w_qkv(s.f + 1, 0, 2 * INNER, wqk_in)
                if runs(back2):
                    sp.wait_ge(d_free, ring_d.at(s, "y")[1] + 1)
                    sp.dma_start(x1_dram[1 + PAIR * back2.p:1 + PAIR * (back2.p + 1), :]
                                 .rearrange("(a t) d -> t a d", a=2), x1[back2.par][:, :, :]).then_inc(x1_out, 16)
                    sp.wait_ge(x1_out, 16 * (back2.n + 1))
                    if later(back2.n, 2):
                        sp.wait_ge(xn_ready, back2.n - 1)
                    row = 1 + PAIR * back2.p
                    for lo, hi, r in ((0, DIM // 2, row), (DIM // 2, DIM, row - 1)):
                        sp.dma_start(xs1[back2.par][:, :, lo:hi], x1_dram[r:r + PAIR, lo:hi]
                                     .rearrange("(a t) d -> t a d", a=2)).then_inc(xs1_in[back2.par], 16)
                if runs(back2) and s.p == 1 and in_rounds(s):
                    load_wo(s.f)
                if runs(now):
                    sp.wait_ge(d_free, ring_d.at(s, (1, "v", 1))[1] + 1)
                    q = WINDOW
                    src, old, dst = v[now.par], v[1 - now.par], v_back[now.par]
                    done = v_back_in[now.par]
                    sp.dma_start(dst[q:P, :, :], src[0:P - q, :, :]).then_inc(done, 16)
                    sp.dma_start(dst[0:q, 1, :], src[P - q:P, 0, :]).then_inc(done, 16)
                    sp.dma_start(dst[0:q, 0, :], old[P - q:P, 1, :]).then_inc(done, 16)
                    if s.p == POS - 1:
                        load_w_qkv(s.f + 1, 2 * INNER, 3 * INNER, wv_in)
                if runs(back3):
                    sp.wait_ge(d_free, ring_d.at(s, "y2")[1] + 1)
                    sp.dma_start(dram_rows(x_dram, back3.f + BATCH, 1 + PAIR * back3.p, PAIR)
                                 .rearrange("(a t) d -> t a d", a=2), x2[back3.par][:, :, :]).then_inc(x2_out, 16)
                    if s.p == 2 and in_rounds(s):
                        load_ffn(s.f)

            rounds(sp, step)
            sp.wait_ge(x2_out, 16 * PAIRS)

        @block.tensor
        def _(pe):
            def fill_d(s, name):
                slot, n = ring_d.at(s, name)
                if later(n, 3):
                    pe.wait_ge(d_free, n - 2)
                return bank_d[slot]

            def fill_a(s, name, after=None):
                slot, n = ring_a.at(s, name)
                order = ring_a.names(s.t)
                if after and order.index(after) + 1 >= order.index(name) - 2:
                    pe.wait_ge(a_free, ring_a.at(s, after)[1] + 1)
                elif later(n, 3):
                    pe.wait_ge(a_free, n - 2)
                return bank_a[slot]

            def transpose_x(s):
                new = s.pair(-1)
                pe.wait_ge(xs_in[new.par], 32 * (new.k + 1))
                bank = fill_d(s, "xT")
                for a in range(2):
                    last = nc.tensor.transpose(bank[:, P * a:P * (a + 1)], xs[new.par][:, a, :], ident[:, :])
                last.then_inc(d_filled, 1)

            def project(s, i):
                a, kind, c = chunks[i]
                if i == 0:
                    if s.p == POS - 1:
                        pe.wait_ge(wqk_in, 16 * (s.f + 2))
                    pe.wait_ge(d_free, ring_d.at(s, "xT")[1] + 1)
                if i == 8 and s.p == 0:
                    pe.wait_ge(wv_in, 16 * (s.f + 1))
                bank = fill_d(s, chunks[i])
                col = INNER * "qkv".index(kind) + 512 * c
                nc.tensor.matmul(bank[:, :], xT[:, P * a:P * (a + 1)], w_qkv[:, col:col + 512],
                                 start=True, stop=True).then_inc(d_filled, 1)

            def transpose_probs(s, pair, ph):
                pe.wait_ge(prob_ready, 2 * pair.n + ph + 1)
                for half in range(2):
                    i = 2 * ph + half
                    bank = fill_a(s, f"PT{i}")
                    for j in range(4):
                        hp = 4 * half + j
                        last = nc.tensor.transpose(
                            bank[:, P * j:P * (j + 1)],
                            prob[ph][:, 2 * hp:2 * hp + 2, :].rearrange("p u k -> p (u k)"), ident[:, :])
                    last.then_inc(a_filled, 1)

            def times_v(s, pair, i):
                a, half = divmod(i, 2)
                if i == 0:
                    pe.wait_ge(v_back_in[pair.par], 48 * (pair.k + 1))
                bank = fill_a(s, f"O{i}", after="PT3")
                nc.tensor.matmul(bank[:, 0:2], ident_b[:, :], ident_b[:, 0:2], start=True, stop=True)
                for hp in range(4 * half, 4 * half + 4):
                    for h2 in range(2):
                        h = 2 * hp + h2
                        for win in range(4):
                            u, ph = divmod(win, 2)
                            src = (v if ph else v_back)[pair.par]
                            last = nc.tensor.matmul(
                                bank[32 * win:32 * win + 32, DH * (h - 8 * half):DH * (h - 8 * half + 1)],
                                probT[ph][64 * u:64 * u + 64, hp, 32 * (2 * h2 + a):32 * (2 * h2 + a) + 32],
                                src[64 * u:64 * u + 64, a, DH * h:DH * (h + 1)],
                                start=True, stop=True)
                last.then_inc(a_filled, 1)

            def transpose_qk(s, pair, i):
                a, kind, half = i // 4, (i // 2) % 2, i % 2
                if i % 4 == 0:
                    pe.wait_ge(qk_ready, 2 * pair.n + a + 1)
                bank = fill_a(s, f"qk{i}")
                for j in range(4):
                    col = INNER * kind + P * (4 * half + j)
                    last = nc.tensor.transpose(bank[:, P * j:P * (j + 1)], qk_rot[:, a, col:col + P], ident[:, :])
                last.then_inc(a_filled, 1)

            def transpose_attn(s, i):
                a, half = divmod(i, 2)
                bank = fill_a(s, f"OT{i}", after=f"O{i}")
                for j in range(4):
                    hp = 4 * half + j
                    last = nc.tensor.transpose(bank[:, P * j:P * (j + 1)], attn[:, a, P * hp:P * (hp + 1)], ident[:, :])
                last.then_inc(a_filled, 1)

            def score(s, pair, ph, half):
                if half == 0:
                    pe.wait_ge(a_free, ring_a.at(s, "qk7")[1] + 1)
                    n = 2 * pair.n + ph
                    if later(n):
                        pe.wait_ge(scores_used, n)
                first = pair.p == 0 and ph == 0
                bank = scores[:, 4 * half:4 * half + 4, :, :]
                nc.tensor.matmul(bank, ident_b[:, :], mask[:, int(first), :, :, :], start=True, stop=False,
                                 skip_group_check=True)
                for hp in range(4 * half, 4 * half + 4):
                    for u in range(2):
                        for h2 in range(2):
                            for a in range(2):
                                win = 4 * a + 2 * u + ph
                                row = 32 * (2 * h2 + a)
                                last = nc.tensor.matmul(
                                    scores[row:row + 32, hp, u, :],
                                    qT[64 * h2:64 * h2 + 64, hp, 32 * win:32 * win + 32],
                                    kT[pair.par][64 * h2:64 * h2 + 64, hp, 32 * win:32 * win + 64],
                                    start=False, stop=True, skip_group_check=True)
                if half:
                    last.then_inc(scores_ready, 1)

            def times_wo(s):
                if s.p == 2:
                    pe.wait_ge(wo_in, 16 * (s.f + 1))
                pe.wait_ge(a_free, ring_a.at(prev(s), "OT3")[1] + 1)
                bank = fill_d(s, "yT")
                for hp in range(HP):
                    last = nc.tensor.matmul(bank[:, 0:PAIR], w_o[:, hp, :], attnT[:, hp, :],
                                            start=(hp == 0), stop=(hp == HP - 1))
                last.then_inc(d_filled, 1)

            def transpose_pair(s, name, src):
                on_a = name == "xn"
                bank = (fill_a if on_a else fill_d)(s, name)
                for a in range(2):
                    last = nc.tensor.transpose(bank[:, P * a:P * (a + 1)], src(a), ident[:, :])
                last.then_inc(a_filled if on_a else d_filled, 1)

            def ffn_up(s, name):
                group = (0, 1) if name[1] == "A" else (2,)
                on_a, lo = (True, FF) if name[0] == "g" else (False, 0)
                bank = fill_a(s, name, after="xn") if on_a else fill_d(s, name)
                for k in group:
                    first, width = FF_BLOCKS[k]
                    col = PAIR * (k - group[0])
                    last = nc.tensor.matmul(bank[0:width, col:col + PAIR], w_1[:, lo + first:lo + first + width],
                                            xnT[:, :], start=True, stop=True)
                last.then_inc(a_filled if on_a else d_filled, 1)

            def ffn_down(s):
                pe.wait_ge(d_free, ring_d.at(s, "aB")[1] + 1)
                bank = fill_a(s, "y2T")
                for k, (first, width) in enumerate(FF_BLOCKS):
                    last = nc.tensor.matmul(bank[:, 0:PAIR], w_2[0:width, k, :], hidden[0:width, k, :],
                                            start=(k == 0), stop=(k == 2))
                last.then_inc(a_filled, 1)

            pe.wait_ge(constants_ready, INIT)
            transpose_x(Step(-1, POS - 1))
            for i in range(EARLY):
                project(Step(-1, POS - 1), i)

            def step(s):
                now, back1, back2, back3 = (s.pair(lag) for lag in (0, 1, 2, 3))

                def project_now(*which):
                    if runs(now):
                        for i in which:
                            project(s, i)

                def project_next(i):
                    if s.pair(-1).exists:
                        project(s, i)

                for i in range(4):
                    if runs(back1):
                        transpose_qk(s, back1, 2 * i)
                        transpose_qk(s, back1, 2 * i + 1)
                    if i in (1, 3):
                        project_now(4 + i // 2)
                if runs(back1):
                    score(s, back1, 0, 0)
                    score(s, back1, 0, 1)
                project_now(6, 7, 8)
                if runs(back1):
                    score(s, back1, 1, 0)
                    score(s, back1, 1, 1)
                if runs(back3):
                    pe.wait_ge(xn_ready, back3.n + 1)
                    transpose_pair(s, "xn", lambda a: xn[:, a, :])
                if runs(back2):
                    times_wo(s)
                if runs(back3):
                    if s.p == 3:
                        pe.wait_ge(wffn_in, 64 * (s.f + 1))
                    ffn_up(s, "gA")
                if runs(back1):
                    transpose_probs(s, back1, 0)
                if runs(back3):
                    ffn_up(s, "aA")
                project_now(9)
                if runs(back3):
                    ffn_up(s, "gB")
                    ffn_up(s, "aB")
                project_now(10)
                if runs(back2):
                    pe.wait_ge(d_free, ring_d.at(s, "yT")[1] + 1)
                    transpose_pair(s, "y", lambda a: yT[:, P * a:P * (a + 1)])
                if runs(back1):
                    transpose_probs(s, back1, 1)
                project_now(11)
                if s.pair(-1).exists:
                    transpose_x(s)
                if runs(back1):
                    times_v(s, back1, 0)
                    times_v(s, back1, 2)
                project_next(0)
                if runs(back1):
                    times_v(s, back1, 1)
                    transpose_attn(s, 0)
                project_next(1)
                if runs(back1):
                    times_v(s, back1, 3)
                    transpose_attn(s, 2)
                project_next(2)
                if runs(back3):
                    ffn_down(s)
                if runs(back1):
                    transpose_attn(s, 1)
                    transpose_attn(s, 3)
                project_next(3)
                if runs(back3):
                    pe.wait_ge(a_free, ring_a.at(s, "y2T")[1] + 1)
                    transpose_pair(s, "y2", lambda a: y2T[:, P * a:P * (a + 1)])

            rounds(pe, step)

        @block.scalar
        def _(act):
            def filled(s, name):
                slot, n = ring_a.at(s, name)
                act.wait_ge(a_filled, n + 1)
                return bank_a[slot]

            def square(pair, i):
                if not runs(pair):
                    return
                slot, n = chunk_at(pair, i)
                act.wait_ge(d_filled, n + 1)
                if i >= 2 or later(pair.n):
                    m = chunk_at(pair, i - 2)[1] if i >= 2 else chunk_at(pair.step.pair(pair.lag + 1), 6 + i)[1]
                    act.wait_ge(d_free, m + 1)
                nc.scalar.activation(sq[i % 2][:, :, :], bank_d[slot][:, :].rearrange("p (h d) -> p h d", d=DH),
                                     ACT.Square).then_inc(squared, 1)

            def copy_qk(s, pair, i):
                a, kind, half = i // 4, (i // 2) % 2, i % 2
                bank = filled(s, f"qk{i}")[:, :].rearrange("p (j t) -> p j t", t=P)
                hps = slice(4 * half, 4 * half + 4)
                if kind == 0:
                    out = qT[:, hps, P * a:P * (a + 1)]
                else:
                    out = kT[pair.par][:, hps, WINDOW + P * a:WINDOW + P * (a + 1)]
                    if a == 1:
                        nxt = kT[1 - pair.par][:, hps, 0:WINDOW]
                        nc.scalar.activation(nxt, bank[:, :, P - WINDOW:P], ACT.Copy,
                                             scale=0.0 if pair.p == POS - 1 else 1.0)
                nc.scalar.activation(out, bank, ACT.Copy).then_inc(a_free, 1)

            def exponentials(pair, ph):
                act.wait_ge(scores_used, 2 * pair.n + ph + 1)
                nc.scalar.activation(prob[ph][:, :, :], prob[ph][:, :, :], ACT.Exp).then_inc(exp_done, 1)

            def copy_probs(s, ph):
                for half in range(2):
                    bank = filled(s, f"PT{2 * ph + half}")
                    nc.scalar.activation(probT[ph][:, 4 * half:4 * half + 4, :], bank[:, :].rearrange("p (j t) -> p j t", t=P),
                                         ACT.Copy).then_inc(a_free, 1)

            def copy_attn(s, i):
                a, half = divmod(i, 2)
                bank = filled(s, f"O{i}")
                nc.scalar.activation(attn[:, a, 512 * half:512 * (half + 1)], bank[:, :], ACT.Copy).then_inc(a_free, 1)

            def copy_attnT(s, i):
                a, half = divmod(i, 2)
                bank = filled(s, f"OT{i}")
                nc.scalar.activation(attnT[:, 4 * half:4 * half + 4, P * a:P * (a + 1)],
                                     bank[:, :].rearrange("p (j t) -> p j t", t=P), ACT.Copy).then_inc(a_free, 1)

            def gates(s, part):
                bank = filled(s, "g" + part)
                group = (0, 1) if part == "A" else (2,)
                for k in group:
                    width = FF_BLOCKS[k][1]
                    last = nc.scalar.activation(gate[0:width, k, :], bank[0:width, PAIR * (k - group[0]):PAIR * (k - group[0] + 1)],
                                                ACT.Gelu, bias=small[0:width, SMALL["b1g"] + k:SMALL["b1g"] + k + 1])
                last.then_inc(a_free, 1)

            def step(s):
                new, now, back1, back2, back3 = (s.pair(lag) for lag in (-1, 0, 1, 2, 3))
                for i in range(4):
                    if runs(back1):
                        copy_qk(s, back1, 2 * i)
                        copy_qk(s, back1, 2 * i + 1)
                    if i in (1, 3):
                        square(now, 4 + i // 2)
                square(now, 6)
                if runs(back1):
                    exponentials(back1, 0)
                square(now, 7)
                if runs(back3):
                    if s.p == 3:
                        act.wait_ge(wffn_in, 64 * (s.f + 1))
                    bank = filled(s, "xn")
                    nc.scalar.activation(xnT[:, :], bank[:, 0:PAIR], ACT.Identity, scale=small[:, SMALL["g"]:SMALL["g"] + 1],
                                         bias=small[:, SMALL["b"]:SMALL["b"] + 1]).then_inc(a_free, 1)
                if runs(back1):
                    exponentials(back1, 1)
                if runs(back3):
                    gates(s, "A")
                if runs(back1):
                    copy_probs(s, 0)
                if runs(back3):
                    gates(s, "B")
                if runs(back1):
                    copy_probs(s, 1)
                    copy_attn(s, 0)
                    copy_attn(s, 2)
                square(new, 0)
                if runs(back1):
                    copy_attn(s, 1)
                    copy_attnT(s, 0)
                square(new, 1)
                if runs(back1):
                    copy_attn(s, 3)
                    copy_attnT(s, 2)
                square(new, 2)
                if runs(back3):
                    bank = filled(s, "y2T")
                    nc.scalar.activation(y2T[:, :], bank[:, 0:PAIR], ACT.Identity,
                                         bias=small[:, SMALL["b2"]:SMALL["b2"] + 1]).then_inc(a_free, 1)
                if runs(back1):
                    copy_attnT(s, 1)
                    copy_attnT(s, 3)
                square(new, 3)

            act.wait_ge(constants_ready, INIT)
            for i in range(EARLY):
                square(Step(-1, POS - 1).pair(-1), i)
            rounds(act, step)

        @block.vector
        def _(dve):
            links, chain = [0], [0]

            def link(ins):
                links[0] += 1
                ins.then_inc(v_link, 1)
                dve.wait_ge(v_link, links[0])

            def filled(s, name):
                slot, n = ring_d.at(s, name)
                dve.wait_ge(d_filled, n + 1)
                return bank_d[slot]

            def rsqrt_step(out, x, tmp, k):
                if k == 0:
                    return nc.vector.tensor_scalar(out.bitcast(i32), x.bitcast(i32), 1, None, ALU.logical_shift_right)
                if k == 1:
                    return nc.vector.tensor_scalar(out.bitcast(i32), out.bitcast(i32), -1.0, float(RSQRT_MAGIC), ALU.mult, ALU.add)
                if k % 3 == 2:
                    return nc.vector.tensor_tensor(tmp, out, out, ALU.mult)
                if k % 3 == 0:
                    return nc.vector.scalar_tensor_tensor(tmp, tmp, -0.5, x, ALU.mult, ALU.mult)
                return nc.vector.scalar_tensor_tensor(out, tmp, 1.5, out, ALU.add, ALU.mult)

            def softmax_shift(s, ph):
                if not runs(s.pair(1)):
                    return
                n = 2 * s.pair(1).n + ph
                dve.wait_ge(scores_ready, n + 1)
                sc = scores[:, :, :, :].rearrange("p h u k -> p (h u) k")
                ins = nc.vector.tensor_reduce(row_max[:, ph, :], sc, AX.X, ALU.max)
                if ph == 0:
                    ins.then_inc(maximum, 1)
                    first_norm(s, 1)
                    dve.wait_ge(maximum, s.pair(1).n + 1)
                else:
                    link(ins)
                if later(n, 2):
                    dve.wait_ge(a_filled, ring_a.at(prev(s), f"PT{2 * ph + 1}")[1] + 1)
                nc.vector.tensor_tensor(prob[ph][:, :, :], sc,
                                        row_max[:, ph, :].unsqueeze(2).to_broadcast([P, HEADS, 2 * WINDOW]),
                                        ALU.subtract).then_inc(scores_used, 1)

            def softmax_sum(s, ph):
                if not runs(s.pair(1)):
                    return
                n = 2 * s.pair(1).n + ph
                dve.wait_ge(exp_done, n + 1)
                link(nc.vector.tensor_reduce(row_sum[:, ph, :], prob[ph][:, :, :], AX.X, ALU.add))
                nc.vector.reciprocal(inv_sum[:, ph, :], row_sum[:, ph, :]).then_inc(inv_ready, 1)

            def rotate(s, pair, i, norm_step=None):
                if not runs(pair):
                    return
                a, kind, c = chunks[i]
                if i == 0 and pair.p == 0:
                    dve.wait_ge(table_ready, pair.f + 1)
                slot, n = chunk_at(pair, i)
                bank = bank_d[slot]
                t4 = table[:, 2 * pair.p + a, :, :]
                kq = "qk".index(kind)
                col = INNER * kq + 512 * c
                if i % 4 == 0 and later(pair.n):
                    dve.wait_ge(qk_ready, 2 * pair.n + a - 1)
                if norm_step is not None:
                    first_norm(s, norm_step)
                dve.wait_ge(squared, 8 * pair.n + i + 1)
                cos = t4[:, 2 * kq, :].unsqueeze(1).to_broadcast([P, 8, DH])
                nc.vector.tensor_tensor(by_cos[:, a, col:col + 512].rearrange("p (h d) -> p h d", d=DH),
                                        bank[:, :].rearrange("p (h d) -> p h d", d=DH), cos, ALU.mult)
                if norm_step is not None:
                    first_norm(s, norm_step + 1)
                nc.vector.tensor_reduce(ss[:, a, HEADS * kq + 8 * c:HEADS * kq + 8 * c + 8], sq[i % 2][:, :, :], AX.X, ALU.add)
                if norm_step is not None:
                    first_norm(s, norm_step + 2)
                sin = t4[:, 2 * kq + 1, :].rearrange("p (r d) -> p r d", r=2).unsqueeze(1).to_broadcast([P, 8, 2, DH // 2])
                swapped = bank[:, :].rearrange("p (h r d) -> p h r d", r=2, d=DH // 2)[:, :, ::-1, :]
                nc.vector.tensor_tensor(by_sin[:, a, col:col + 512].rearrange("p (h r d) -> p h r d", r=2, d=DH // 2),
                                        swapped, sin, ALU.mult).then_inc(d_free, 1)
                if norm_step is not None:
                    first_norm(s, norm_step + 3)
                if i % 4 == 3:
                    dve.wait_ge(d_free, n + 1)

            def copy_x(s):
                bank = filled(s, "xT")
                nc.vector.tensor_copy(xT[:, :], bank[:, 0:PAIR]).then_inc(d_free, 1)

            def variances(s):
                back3 = s.pair(3)
                dve.wait_ge(xs1_in[back3.par], 32 * (back3.k + 1))
                for a in range(2):
                    last = nc.vector.bn_stats(stats[:, a, :], xs1[back3.par][:, a, :])
                link(last)
                for a in range(2):
                    last = nc.vector.bn_aggr(mean_var[:, a, :], stats[:, a, :])
                link(last)
                link(nc.vector.tensor_scalar(ss[:, 0, 2 * HEADS:], mean_var[:, :, 1], 1e-5, None, ALU.add))

            def first_norm(s, step):
                now, back3 = s.pair(0), s.pair(3)
                lo = 0 if runs(now) else 2 * HEADS
                hi = 2 * HEADS + 2 if runs(back3) else 2 * HEADS
                if lo == hi:
                    return
                x, out, tmp = ss[:, 0, lo:hi], rnorm[:, 0, lo:hi], newton[:, lo:hi]
                if step > 0 and chain[0]:
                    dve.wait_ge(v_link, chain[0])
                if step == 0:
                    chain[0] = 0
                    if not runs(now):
                        return
                    ins = nc.vector.tensor_scalar(ss[:, 0, 0:2 * HEADS], ss[:, 0, 0:2 * HEADS], 1e-24, None, ALU.max)
                else:
                    ins = rsqrt_step(out, x, tmp, step - 1)
                if step == 11 and runs(now):
                    ins.then_inc(norm_ready, 1)
                    return
                ins.then_inc(v_link, 1)
                links[0] += 1
                chain[0] = links[0]

            def second_norm(s):
                link(nc.vector.tensor_scalar(ss[:, 1, 0:2 * HEADS], ss[:, 1, 0:2 * HEADS], 1e-24, None, ALU.max))
                for k in range(11):
                    ins = rsqrt_step(rnorm[:, 1, 0:2 * HEADS], ss[:, 1, 0:2 * HEADS], newton[:, 0:2 * HEADS], k)
                    if k < 10:
                        link(ins)
                    else:
                        ins.then_inc(norm_ready, 1)

            def normalise(s):
                now, back3 = s.pair(0), s.pair(3)
                if runs(now):
                    dve.wait_ge(norm_ready, 2 * now.n + 1)
                else:
                    dve.wait_ge(v_link, chain[0])
                for a in range(2):
                    last = nc.vector.tensor_scalar(xn[:, a, :], xs1[back3.par][:, a, :], mean_var[:, a, 0:1],
                                                   rnorm[:, 0, 2 * HEADS + a:2 * HEADS + a + 1], ALU.subtract, ALU.mult)
                last.then_inc(xn_ready, 1)

            def copy_v(s, i):
                now = s.pair(0)
                if not runs(now):
                    return
                a, _, c = chunks[i]
                bank = filled(s, chunks[i])
                if i == 8 and later(now.n):
                    dve.wait_ge(v_back_in[1 - now.par], 48 * (prev(s).pair(0).k + 1))
                    if later(now.n, 2):
                        dve.wait_ge(a_filled, ring_a.at(prev(s), "O3")[1] + 1)
                nc.vector.tensor_copy(v[now.par][:, a, 512 * c:512 * (c + 1)], bank[:, :]).then_inc(d_free, 1)

            def hidden_units(s, part):
                group = (0, 1) if part == "A" else (2,)
                bank = filled(s, "a" + part)
                dve.wait_ge(a_free, ring_a.at(s, "g" + part)[1] + 1)
                for k in group:
                    width = FF_BLOCKS[k][1]
                    last = nc.vector.scalar_tensor_tensor(
                        hidden[0:width, k, :], bank[0:width, PAIR * (k - group[0]):PAIR * (k - group[0] + 1)],
                        small[0:width, SMALL["b1a"] + k:SMALL["b1a"] + k + 1], gate[0:width, k, :], ALU.add, ALU.mult)
                last.then_inc(d_free, 1)

            def step(s):
                new, now, back1, back2, back3 = (s.pair(lag) for lag in (-1, 0, 1, 2, 3))
                rotate(s, now, 4)
                rotate(s, now, 5)
                if runs(back3):
                    variances(s)
                first_norm(s, 0)
                if runs(back1):
                    softmax_shift(s, 0)
                else:
                    first_norm(s, 1)
                first_norm(s, 2)
                first_norm(s, 3)
                if runs(now):
                    rotate(s, now, 6, norm_step=4)
                else:
                    for k in range(4, 8):
                        first_norm(s, k)
                for k in range(8, 12):
                    first_norm(s, k)
                if runs(back3):
                    normalise(s)
                softmax_sum(s, 0)
                softmax_shift(s, 1)
                rotate(s, now, 7)
                copy_v(s, 8)
                if runs(back2):
                    bank = filled(s, "yT")
                    nc.vector.tensor_copy(yT[:, :], bank[:, 0:PAIR]).then_inc(d_free, 1)
                softmax_sum(s, 1)
                if runs(back3):
                    if s.p == 3:
                        dve.wait_ge(wffn_in, 64 * (s.f + 1))
                    hidden_units(s, "A")
                copy_v(s, 9)
                if runs(back3):
                    hidden_units(s, "B")
                copy_v(s, 10)
                if runs(back2):
                    bank = filled(s, "y")
                    dve.wait_ge(xr_in[back2.par], 16 * (back2.k + 1))
                    if later(back2.n, 2):
                        dve.wait_ge(x1_out, 16 * (back2.n - 1))
                    nc.vector.tensor_tensor(x1[back2.par][:, :, :], bank[:, 0:PAIR].rearrange("p (a d) -> p a d", a=2),
                                            xr[back2.par][:, :, :], ALU.add).then_inc(d_free, 1)
                if runs(now):
                    second_norm(s)
                copy_v(s, 11)
                if new.exists:
                    copy_x(s)
                rotate(s, new, 0)
                rotate(s, new, 1)
                rotate(s, new, 2)
                rotate(s, new, 3)
                if runs(back3):
                    bank = filled(s, "y2")
                    if later(back3.n, 2):
                        dve.wait_ge(x2_out, 16 * (back3.n - 1))
                    nc.vector.tensor_tensor(x2[back3.par][:, :, :], bank[:, 0:PAIR].rearrange("p (a d) -> p a d", a=2),
                                            x1[back3.par][:, :, :], ALU.add).then_inc(d_free, 1)
                if s.p == POS - 1:
                    nc.vector.sem_clear(v_link)
                    links[0] = 0

            nc.vector.memset(v[1][:, :, :], 0.0)
            dve.wait_ge(zeros_ready, 3)
            nc.vector.tensor_copy(ident_b[:, :], ident[:, :]).then_inc(constants_ready, 1)
            nc.vector.memset(kT[0][:, :, 0:WINDOW], 0.0).then_inc(constants_ready, 1)
            copy_x(Step(-1, POS - 1))
            for i in range(EARLY):
                rotate(None, Step(-1, POS - 1).pair(-1), i)
            rounds(dve, step)


        @block.gpsimd
        def _(pool):
            links = [0]

            def link(ins):
                links[0] += 1
                ins.then_inc(p_link, 1)
                pool.wait_ge(p_link, links[0])

            nc.gpsimd.memset(ident[:, :], 0.0).then_inc(zeros_ready, 1)
            nc.gpsimd.memset(mask[:, :, :, :, :], 0.0).then_inc(zeros_ready, 1)
            pool.wait_ge(zeros_ready, 2)
            nc.gpsimd.affine_select(out=ident[:, :], in_=ident[:, :], compare_op=ALU.not_equal, fill=1.0, base=0,
                                    pattern=[[-1, P]], channel_multiplier=1).then_inc(zeros_ready, 1)
            for q in range(4):
                rows = mask[32 * q:32 * q + 32, :, :, :, :].rearrange("p m h u k -> p (m h u) k")
                for own, sign in ((0, 1), (1, -1)):
                    part = rows[:, :, WINDOW * own:WINDOW * (own + 1)]
                    link(nc.gpsimd.affine_select(out=part, in_=part, compare_op=ALU.is_ge, fill=MASKED, base=0,
                                                 pattern=[[0, 16], [sign, WINDOW]], channel_multiplier=-sign))
            for q in (0, 2):
                nc.gpsimd.memset(mask[32 * q:32 * q + 32, 1, :, 0, 0:WINDOW], MASKED).then_inc(constants_ready, 1)
            pool.wait_ge(constants_ready, INIT)

            def make_table(f):
                pool.wait_ge(qkrow_in, 16 * (f + 1))
                nc.gpsimd.tensor_tensor(table[:, :, :, :].rearrange("p t r d -> p t (r d)"),
                                        rotary[:, :, :, :].rearrange("p t r d -> p t (r d)"),
                                        qk_row[:, :, :].rearrange("p r d -> p (r d)").unsqueeze(1).to_broadcast([P, SEQ // P, 4 * DH]),
                                        ALU.mult).then_inc(table_ready, 1)

            pool.wait_ge(rotary_in, 16)
            make_table(0)
            def add_products(s, a):
                link(nc.gpsimd.tensor_tensor(by_cos[:, a, :], by_cos[:, a, :], by_sin[:, a, :], ALU.add))

            def norm_qk(s, a):
                now, back1 = s.pair(0), s.pair(1)
                pool.wait_ge(norm_ready, 2 * now.n + a + 1)
                if runs(back1):
                    pool.wait_ge(a_filled, ring_a.at(s, f"qk{4 * a + 3}")[1] + 1)
                nc.gpsimd.tensor_tensor(qk_rot[:, a, :].rearrange("p (h d) -> p h d", d=DH),
                                        by_cos[:, a, :].rearrange("p (h d) -> p h d", d=DH),
                                        rnorm[:, a, 0:2 * HEADS].unsqueeze(2).to_broadcast([P, 2 * HEADS, DH]),
                                        ALU.mult).then_inc(qk_ready, 1)

            def normalise(pair, ph):
                pool.wait_ge(inv_ready, 2 * pair.n + ph + 1)
                nc.gpsimd.tensor_tensor(prob[ph][:, :, :], prob[ph][:, :, :],
                                        inv_sum[:, ph, :].unsqueeze(2).to_broadcast([P, HEADS, 2 * WINDOW]),
                                        ALU.mult).then_inc(prob_ready, 1)

            def step(s):
                now, back1 = s.pair(0), s.pair(1)
                if runs(now):
                    pool.wait_ge(d_free, chunk_at(now, 3)[1] + 1)
                    add_products(s, 0)
                if runs(back1):
                    normalise(back1, 0)
                if runs(now):
                    norm_qk(s, 0)
                if runs(back1):
                    normalise(back1, 1)
                if runs(now):
                    pool.wait_ge(d_free, chunk_at(now, 7)[1] + 1)
                    if s.p == POS - 1:
                        make_table(s.f + 1)
                    add_products(s, 1)
                    norm_qk(s, 1)
                if s.p == POS - 1:
                    nc.gpsimd.sem_clear(p_link)
                    links[0] = 0

            rounds(pool, step)


A_HEADS, A_KV, A_DH = 16, 4, 8
Q_RANK, KV_RANK = 64, 32
TILES = SEQ // P
HALF = SEQ // 2
QB = PAIR
PARTS = 6
SPLIT = PARTS * A_DH
Q_PART, K_PART = (0, 0, 1, 0, 1, 2), (0, 1, 0, 2, 1, 0)
MAX_UNITS = [(i, half) for i in range(TILES) for half in range(1 + (i >= 4))]
MAXIMA = 4 * len(MAX_UNITS)
UNITS = [(qb, kt) for qb in range(SEQ // QB) for kt in range(2 * qb + 2)]
N_UNITS = len(UNITS)
HALF_DONE = UNITS.index((1, 3))
NEG_UNIT = N_UNITS - 3
MAX_PER_UNIT = MAXIMA // (NEG_UNIT - 1)


def rsqrt(nc, link, out, x, tmp, last):
    link(nc.vector.tensor_scalar(out.bitcast(i32), x.bitcast(i32), 1, None, ALU.logical_shift_right))
    link(nc.vector.tensor_scalar(out.bitcast(i32), out.bitcast(i32), -1.0, float(RSQRT_MAGIC), ALU.mult, ALU.add))
    for k in range(3):
        link(nc.vector.tensor_tensor(tmp, out, out, ALU.mult))
        link(nc.vector.scalar_tensor_tensor(tmp, tmp, -0.5, x, ALU.mult, ALU.mult))
        (last if k == 2 else link)(nc.vector.scalar_tensor_tensor(out, tmp, 1.5, out, ALU.add, ALU.mult))


def maxima_at(u):
    return range(MAXIMA)[MAX_PER_UNIT * u:MAX_PER_UNIT * (u + 1)]


PREPARE = ["xT0", "xT1", "pr0", "pr1", "kv0", "kv1", "kv2", "kv3"]


class MiscFills:

    def __init__(self):
        start = ["tq0", "tq1", "tk", "next tq0", "next tq1", "next tk", "nm"]
        self.names = [(-1, name) for name in start]
        for g in range(A_KV):
            for u in range(N_UNITS):
                self.names += [(g, name) for name in self.at_unit(g, u)]
            self.names.append((g, "oa1"))
        self.names += [(A_KV, name) for name in ("ao0", "ao1", "y0", "y1")]

    @staticmethod
    def at_unit(g, u):
        at = {HALF_DONE + 2: ["oa0"]}
        if g < A_KV - 1:
            at[NEG_UNIT] = ["nm"]
        if g < A_KV - 2:
            at |= {NEG_UNIT + 1: ["tq0", "tq1"], NEG_UNIT + 2: ["tk"]}
        if g == A_KV - 1:
            free = [v for v in range(N_UNITS) if v not in at]
            at |= {v: [name] for v, name in zip(free, PREPARE)}
        return at.get(u, [])

    def number(self, b, g, name):
        if isinstance(b, int) and b == -1:
            return PREPARE.index(name)
        return len(self.names) * b + (len(PREPARE) + self.names.index((g, name)))

    def prepared(self, b, name):
        if isinstance(b, int) and b == 0:
            return self.number(-1, None, name)
        return self.number(b - 1, A_KV - 1, name)


def mla_attention(nc, x_in, x_dram, neg_dram, w):
    with ExitStack() as ctx:
        def sb(name, shape, dt=fp32):
            return ctx.enter_context(nc.sbuf_tensor(name, shape, dt))

        def sem(name):
            return ctx.enter_context(nc.semaphore(name))

        def psum(name, shape):
            return ctx.enter_context(nc.psum_tensor(name, shape, fp32))

        w_a = sb("w_a", [P, Q_RANK + KV_RANK])
        w_b = sb("w_b", [Q_RANK + KV_RANK, DIM + 2 * A_KV * A_DH])
        w_out = sb("w_out", [P, DIM])
        b_out = sb("b_out", [P, DIM])
        rope_q = sb("rope_q", [P, TILES, 2, DIM])
        rope_k = sb("rope_k", [P, TILES, 2, A_KV * A_DH])
        ident = sb("a_ident", [P, P])
        ident_b = sb("a_ident_b", [P, P], bf16)
        mask_q = sb("mask_q", [P, P], bf16)
        mask_k = sb("mask_k", [P, P], bf16)
        x = sb("a_x", [P, TILES, DIM])
        xr = sb("a_xr", [P, TILES, DIM])
        xT = sb("a_xT", [P, SEQ])
        latent = sb("latent", [Q_RANK + KV_RANK, SEQ])
        qkv = sb("qkv", [P, TILES, DIM + 2 * A_KV * A_DH])
        t_cos, t_sin = sb("t_cos", [P, TILES, DIM]), sb("t_sin", [P, TILES, DIM])
        q_rot = sb("q_rot", [P, TILES, DIM])
        k_cos, k_sin = sb("k_cos", [P, TILES, A_KV * A_DH]), sb("k_sin", [P, TILES, A_KV * A_DH])
        k_rot = sb("k_rot", [P, TILES, A_KV * A_DH])
        q_split = sb("q_split", [P, TILES, A_HEADS, 64], bf16)
        k_split = sb("k_split", [P, TILES, A_KV, 2, 64], bf16)
        qx = [sb(f"qx{g}", [P, 2, SEQ], bf16) for g in range(A_KV)]
        kx = [sb(f"kx{g}", [P, 2, SEQ], bf16) for g in range(A_KV)]
        vx = [sb(f"vx{g}", [P, TILES, 32]) for g in range(A_KV)]
        part_max = sb("part_max", [P, 4, 12])
        neg = sb("neg", [P, 4, TILES])
        neg_split = sb("neg_split", [P, 2, 3, 2, TILES], bf16)
        negT = sb("negT", [96, P], bf16)
        probT = [sb(f"a_probT{i}", [P, 4, QB]) for i in range(3)]
        accT = [sb(f"accT{i}", [P, HALF]) for i in range(2)]
        recip = sb("recip", [P, 4, 4])
        attn = sb("a_attn", [P, TILES, DIM])
        attnT = sb("a_attnT", [P, SEQ])
        z = sb("z", [P, TILES, DIM])
        stats = sb("a_stats", [P, TILES, 6])
        mean_var = sb("a_mean_var", [P, TILES, 2])
        var_eps, rstd, nwt = sb("a_var_eps", [P, TILES]), sb("a_rstd", [P, TILES]), sb("a_nwt", [P, TILES])
        y = sb("a_y", [P, TILES, DIM])

        s_max = [psum(f"s_max{i}", [P, 512]) for i in range(2)]
        s_T = [psum(f"s_T{i}", [P, 4, QB]) for i in range(2)]
        acc = psum("acc", [P, HALF])
        misc = psum("misc", [P, 512])
        misc_b = misc[:, :].bitcast(bf16)
        fills = MiscFills()

        w_in, x_load, xr_in, y_out = sem("a_w_in"), sem("a_x_load"), sem("a_xr_in"), sem("a_y_out")
        zeroed, masked, ready = sem("a_zeroed"), sem("a_masked"), sem("a_ready")
        m_filled, m_free = sem("m_filled"), sem("m_free")
        max_filled, max_free = sem("max_filled"), sem("max_free")
        st_filled, exp_done, av_done, acc_free = sem("st_filled"), sem("a_exp_done"), sem("av_done"), sem("acc_free")
        split_ready, neg_ready = sem("split_ready"), sem("neg_ready")
        neg_out, neg_in = sem("neg_out"), sem("neg_in")
        y_ready = sem("a_y_ready")
        v_link = sem("a_v_link")
        NEXT_AT = {11: "tq0", 23: "tq1", 35: "tk"}
        READY = 3

        block = ctx.enter_context(nc.Block())

        def batches(eng, body):
            body(0)
            with eng.Fori(1, BATCH) as b:
                body(b)

        def later(b):
            return not isinstance(b, int) or b > 0

        @block.sync
        def _(sp):
            def load_x(b):
                sp.dma_start(x[:, :, :], x_in[bass.ds(b, 1), :, :].rearrange("one (t p) d -> p (one t) d", p=P)).then_inc(x_load, 16)

            load_x(0)
            sp.dma_start(w_a[:, 0:Q_RANK], w["Wqa"]).then_inc(w_in, 16)
            sp.dma_start(w_a[:, Q_RANK:], w["Wkva"]).then_inc(w_in, 16)
            sp.wait_ge(zeroed, 1)
            sp.dma_start(w_b[0:Q_RANK, 0:DIM], w["Wqb"]).then_inc(w_in, 16)
            sp.dma_start(w_b[Q_RANK:, DIM:], w["Wkvb"]).then_inc(w_in, 16)
            sp.dma_start(rope_q[:, :, :, :], w["rope_q"]).then_inc(w_in, 16)
            sp.dma_start(rope_k[:, :, :, :], w["rope_k"]).then_inc(w_in, 16)
            sp.dma_start(w_out[:, :], w["Wout"]).then_inc(w_in, 16)
            sp.dma_start(b_out[:, :], w["bout"].rearrange("(one d) -> one d", one=1).to_broadcast([P, DIM])).then_inc(w_in, 16)

            def neg_rows(g, G, number):
                sp.wait_ge(m_free, number + 1)
                sp.dma_start(neg_dram, negT[:, :]).then_inc(neg_out, 16)
                sp.wait_ge(neg_out, 16 * (G + 1))
                for h2 in range(2):
                    row = 64 * h2 + SPLIT
                    sp.dma_start(qx[g][row:row + 3, :, :].rearrange("r j q -> r (j q)"),
                                 neg_dram[48 * h2:48 * h2 + 48, :].rearrange("(r c) q -> r (c q)", r=3)).then_inc(neg_in, 16)

            def body(b):
                if later(b):
                    sp.wait_ge(y_ready, b)
                sp.dma_start(xr[:, :, :], x_in[bass.ds(b, 1), :, :].rearrange("one (t p) d -> p (one t) d", p=P)).then_inc(xr_in, 16)
                sp.wait_ge(m_free, fills.prepared(b, "xT1") + 1)
                load_x((b + 1) % BATCH)
                for g in range(A_KV):
                    neg_rows(g, A_KV * b + g, fills.number(b, g - 1, "nm"))
                sp.wait_ge(y_ready, b + 1)
                sp.dma_start(x_dram[bass.ds(b, 1), 1:1 + SEQ, :].rearrange("one (t p) d -> p (one t) d", p=P), y[:, :, :]).then_inc(y_out, 16)

            batches(sp, body)
            sp.wait_ge(y_out, 16 * BATCH)
            sp.wait_ge(x_load, 16 * (BATCH + 1))

        @block.tensor
        def _(pe):
            def fill(number):
                if not isinstance(number, int) or number >= 1:
                    pe.wait_ge(m_free, number)

            def prep(num, name):
                n = num(name)
                k = int(name[-1])
                if name[:2] == "xT":
                    fill(n)
                    for t in range(4):
                        last = nc.tensor.transpose(misc[:, P * t:P * (t + 1)], x[:, 4 * k + t, :], ident[:, :])
                elif name[:2] == "pr":
                    fill(n)
                    last = nc.tensor.matmul(misc[0:Q_RANK + KV_RANK, :], w_a[:, :], xT[:, HALF * k:HALF * (k + 1)], start=True, stop=True)
                else:
                    fill(n)
                    for t in range(2):
                        tile = 2 * k + t
                        last = nc.tensor.matmul(misc[:, 192 * t:192 * (t + 1)], latent[:, P * tile:P * (tile + 1)], w_b[:, :],
                                                start=True, stop=True)
                last.then_inc(m_filled, 1)

            def transpose_split(n, g, name):
                fill(n)
                for t in range(TILES):
                    if name == "tk":
                        src = k_split[:, t, g, :, :]
                    else:
                        h = 4 * g + 2 * int(name[-1])
                        src = q_split[:, t, h:h + 2, :]
                    last = nc.tensor.transpose(misc_b[:, P * t:P * (t + 1)], src.rearrange("p a c -> p (a c)"), ident_b[:, :])
                last.then_inc(m_filled, 1)

            def max_unit(g, G, m):
                head, (i, half) = m // 12, MAX_UNITS[m % 12]
                hpl, h2 = divmod(head, 2)
                n = MAXIMA * G + m
                if not isinstance(n, int) or n >= 2:
                    pe.wait_ge(max_free, n - 1)
                bank = s_max[m % 2]
                width = min(512, P * (i + 1) - 512 * half)
                diagonal = P * i // 512 == half
                last = nc.tensor.matmul(bank[:, 0:width], qx[g][:, hpl, P * i:P * (i + 1)],
                                        kx[g][:, h2, 512 * half:512 * half + width],
                                        start=True, stop=not diagonal, skip_group_check=True)
                if diagonal:
                    last = nc.tensor.matmul(bank[:, width - P:width], ident_b[:, :], mask_q[:, :], start=False, stop=True,
                                            skip_group_check=True)
                last.then_inc(max_filled, 1)

            def transposed_scores(g, G, u):
                qb, kt = UNITS[u]
                n = N_UNITS * G + u
                if not isinstance(n, int) or n >= 2:
                    pe.wait_ge(exp_done, n - 1)
                lo = max(0, P * kt - QB * qb)
                diagonal = P * kt >= QB * qb
                for h2 in range(2):
                    for hpl in range(2):
                        tile = s_T[u % 2][:, 2 * h2 + hpl, :]
                        last = nc.tensor.matmul(tile[:, lo:QB], kx[g][:, h2, P * kt:P * (kt + 1)],
                                                qx[g][:, hpl, QB * qb + lo:QB * (qb + 1)],
                                                start=True, stop=not diagonal, skip_group_check=True)
                        if diagonal:
                            last = nc.tensor.matmul(tile[:, lo:lo + P], ident_b[:, :], mask_k[:, :], start=False, stop=True,
                                                    skip_group_check=True)
                last.then_inc(st_filled, 1)

            def times_v(g, G, u):
                qb, kt = UNITS[u]
                if u in (0, HALF_DONE + 1):
                    n = 2 * G + (u > 0)
                    if not isinstance(n, int) or n >= 1:
                        pe.wait_ge(acc_free, n)
                pe.wait_ge(exp_done, N_UNITS * G + u + 1)
                lo = max(0, P * kt - QB * qb)
                col = QB * (qb % 2)
                for head in range(4):
                    hpl, h2 = divmod(head, 2)
                    last = nc.tensor.matmul(acc[32 * head:32 * head + 32, col + lo:col + QB], vx[g][:, kt, :],
                                            probT[u % 3][:, 2 * h2 + hpl, lo:QB],
                                            start=(kt == 0), stop=(kt == 2 * qb + 1), skip_group_check=True)
                last.then_inc(av_done, 1)

            def transpose_max(n):
                fill(n)
                nc.tensor.transpose(misc_b[0:96, 0:P], neg_split[:, :, :, :, :].rearrange("p a r j i -> p (a r j i)"),
                                    ident_b[:, :]).then_inc(m_filled, 1)

            def transpose_acc(n, qb):
                fill(n)
                for t in range(4):
                    last = nc.tensor.transpose(misc[:, P * t:P * (t + 1)], accT[qb][:, P * t:P * (t + 1)], ident[:, :])
                last.then_inc(m_filled, 1)

            pe.wait_ge(ready, READY)
            pe.wait_ge(w_in, 16 * 8)

            pe.wait_ge(x_load, 16)
            for name in PREPARE:
                prep(lambda name: fills.prepared(0, name), name)

            def body(b):
                num = lambda name: fills.number(b, -1, name)
                pe.wait_ge(split_ready, b + 1)
                for name in ("tq0", "tq1", "tk"):
                    transpose_split(num(name), 0, name)
                pe.wait_ge(m_free, num("tk") + 1)
                for m in range(MAXIMA):
                    max_unit(0, A_KV * b, m)
                    if m in NEXT_AT:
                        transpose_split(num("next " + NEXT_AT[m]), 1, NEXT_AT[m])
                pe.wait_ge(neg_ready, A_KV * b + 1)
                transpose_max(num("nm"))
                for g in range(A_KV):
                    attend(b, g)
                num = lambda name: fills.number(b, A_KV, name)
                for k in range(2):
                    fill(num(f"ao{k}"))
                    for t in range(4):
                        last_t = nc.tensor.transpose(misc[:, P * t:P * (t + 1)], attn[:, 4 * k + t, :], ident[:, :])
                    last_t.then_inc(m_filled, 1)
                for k in range(2):
                    fill(num(f"y{k}"))
                    for t in range(4):
                        tile = 4 * k + t
                        last_t = nc.tensor.matmul(misc[:, P * t:P * (t + 1)], attnT[:, P * tile:P * (tile + 1)], w_out[:, :],
                                                  start=True, stop=True)
                    last_t.then_inc(m_filled, 1)

            def attend(b, g):
                G = A_KV * b + g
                num = lambda name: fills.number(b, g, name)
                pe.wait_ge(neg_in, 32 * (G + 1))
                transposed_scores(g, G, 0)
                if g < A_KV - 1:
                    pe.wait_ge(m_free, (fills.number(b, g - 1, "tk") if g else fills.number(b, -1, "next tk")) + 1)
                for u in range(N_UNITS):
                    maxima = maxima_at(u) if g < A_KV - 1 else []
                    for m in maxima[:1]:
                        max_unit(g + 1, G + 1, m)
                    if u + 1 < N_UNITS:
                        transposed_scores(g, G, u + 1)
                    for m in maxima[1:2]:
                        max_unit(g + 1, G + 1, m)
                    for name in fills.at_unit(g, u):
                        if name == "oa0":
                            pe.wait_ge(acc_free, 2 * G + 1)
                            transpose_acc(num(name), 0)
                        elif name == "nm":
                            pe.wait_ge(neg_ready, G + 2)
                            transpose_max(num(name))
                        elif name in PREPARE:
                            if name == "xT0":
                                pe.wait_ge(x_load, 16 * (b + 2))
                            prep(num, name)
                        else:
                            transpose_split(num(name), g + 2, name)
                    times_v(g, G, u)
                    for m in maxima[2:]:
                        max_unit(g + 1, G + 1, m)
                pe.wait_ge(acc_free, 2 * G + 2)
                transpose_acc(num("oa1"), 1)

            batches(pe, body)

        @block.scalar
        def _(act):
            def filled(n):
                act.wait_ge(m_filled, n + 1)

            def prep(num, name):
                filled(num(name))
                k = int(name[-1])
                if name[:2] == "xT":
                    nc.scalar.activation(xT[:, HALF * k:HALF * (k + 1)], misc[:, :], ACT.Copy).then_inc(m_free, 1)
                elif name[:2] == "pr":
                    r = Q_RANK + KV_RANK
                    nc.scalar.activation(latent[:, HALF * k:HALF * (k + 1)], misc[0:r, :], ACT.Copy).then_inc(m_free, 1)
                else:
                    nc.scalar.activation(qkv[:, 2 * k:2 * k + 2, :], misc[:, 0:384].rearrange("p (t c) -> p t c", t=2),
                                         ACT.Copy).then_inc(m_free, 1)

            def split_out(n, g, name):
                filled(n)
                if name == "tk":
                    nc.scalar.activation(kx[g][0:64, 0, :], misc_b[0:64, :], ACT.Copy)
                    nc.scalar.activation(kx[g][64:P, 1, :], misc_b[64:P, :], ACT.Copy).then_inc(m_free, 1)
                else:
                    nc.scalar.activation(qx[g][:, int(name[-1]), :], misc_b, ACT.Copy).then_inc(m_free, 1)

            def neg_evacuate(n):
                filled(n)
                nc.scalar.activation(negT[:, :], misc_b[0:96, 0:P], ACT.Copy).then_inc(m_free, 1)

            for name in PREPARE:
                prep(lambda name: fills.prepared(0, name), name)

            def body(b):
                num = lambda name: fills.number(b, -1, name)
                for name in ("tq0", "tq1", "tk"):
                    split_out(num(name), 0, name)
                for name in ("tq0", "tq1", "tk"):
                    split_out(num("next " + name), 1, name)
                neg_evacuate(num("nm"))
                for g in range(A_KV):
                    G = A_KV * b + g
                    num = lambda name: fills.number(b, g, name)
                    for u, (qb, kt) in enumerate(UNITS):
                        n = N_UNITS * G + u
                        act.wait_ge(st_filled, n + 1)
                        if not isinstance(n, int) or n >= 3:
                            act.wait_ge(av_done, n - 2)
                        lo = max(0, P * kt - QB * qb)
                        nc.scalar.activation(probT[u % 3][:, :, lo:QB], s_T[u % 2][:, :, lo:QB], ACT.Exp).then_inc(exp_done, 1)
                        if u == HALF_DONE + 1:
                            evacuate(G, 0)
                        for name in fills.at_unit(g, u):
                            if name == "nm":
                                neg_evacuate(num(name))
                            elif name in PREPARE:
                                prep(num, name)
                            elif name != "oa0":
                                split_out(num(name), g + 2, name)
                    evacuate(G, 1)
                for k in range(2):
                    filled(fills.number(b, A_KV, f"ao{k}"))
                    nc.scalar.activation(attnT[:, HALF * k:HALF * (k + 1)], misc[:, :], ACT.Copy).then_inc(m_free, 1)

            def evacuate(G, half):
                act.wait_ge(av_done, N_UNITS * G + (N_UNITS if half else HALF_DONE + 1))
                nc.scalar.activation(accT[half][:, :], acc[:, :], ACT.Copy).then_inc(acc_free, 1)

            batches(act, body)

        @block.vector
        def _(dve):
            links = [0]

            def link(ins):
                links[0] += 1
                ins.then_inc(v_link, 1)
                dve.wait_ge(v_link, links[0])

            def rope():
                q_in = qkv[:, :, 0:DIM]
                nc.vector.tensor_tensor(t_cos[:, :, :], q_in, rope_q[:, :, 0, :], ALU.mult)
                nc.vector.tensor_tensor(t_sin[:, :, :].rearrange("p t (c r) -> p t c r", r=2),
                                        q_in.rearrange("p t (c r) -> p t c r", r=2)[:, :, :, ::-1],
                                        rope_q[:, :, 1, :].rearrange("p t (c r) -> p t c r", r=2), ALU.mult)
                k_in = qkv[:, :, DIM:].rearrange("p t (c r v) -> p t c r v", r=2, v=2)[:, :, :, :, 0]
                nc.vector.tensor_tensor(k_cos[:, :, :].rearrange("p t (c r) -> p t c r", r=2), k_in,
                                        rope_k[:, :, 0, :].rearrange("p t (c r) -> p t c r", r=2), ALU.mult)
                link(nc.vector.tensor_tensor(k_sin[:, :, :].rearrange("p t (c r) -> p t c r", r=2), k_in[:, :, :, ::-1],
                                             rope_k[:, :, 1, :].rearrange("p t (c r) -> p t c r", r=2), ALU.mult))
                nc.vector.tensor_tensor(q_rot[:, :, :], t_cos[:, :, :], t_sin[:, :, :], ALU.add)
                link(nc.vector.tensor_tensor(k_rot[:, :, :], k_cos[:, :, :], k_sin[:, :, :], ALU.add))

            def split():
                qs = [q_split[:, :, :, A_DH * j:A_DH * (j + 1)] for j in range(PARTS)]
                ks = [[k_split[:, :, :, d, A_DH * j:A_DH * (j + 1)] for d in range(2)] for j in range(PARTS)]
                q_f = q_rot[:, :, :].rearrange("p t (h d) -> p t h d", d=A_DH)
                k_f = k_rot[:, :, :].rearrange("p t (h d) -> p t h d", d=A_DH)
                for part in range(3):
                    mine_q = [j for j in range(PARTS) if Q_PART[j] == part]
                    mine_k = [j for j in range(PARTS) if K_PART[j] == part]
                    nc.vector.tensor_copy(qs[mine_q[0]], q_f)
                    link(nc.vector.tensor_copy(ks[mine_k[0]][0], k_f))
                    if part < 2:
                        nc.vector.tensor_tensor(q_f, q_f, qs[mine_q[0]], ALU.subtract)
                        nc.vector.tensor_tensor(k_f, k_f, ks[mine_k[0]][0], ALU.subtract)
                    for j in mine_q[1:]:
                        nc.vector.tensor_copy(qs[j], qs[mine_q[0]])
                    for j in mine_k:
                        for d in range(2):
                            if (j, d) != (mine_k[0], 0):
                                last = nc.vector.tensor_copy(ks[j][d], ks[mine_k[0]][0])
                    if part < 2:
                        link(last)
                last.then_inc(split_ready, 1)

            def copy_v(g):
                v_in = qkv[:, :, DIM + 16 * g:DIM + 16 * (g + 1)].rearrange("p t (d v) -> p t d v", v=2)[:, :, :, 1]
                nc.vector.tensor_copy(vx[g][:, :, 0:A_DH], v_in)

            def reduce_unit(G, m):
                head, (i, half) = m // 12, MAX_UNITS[m % 12]
                n = MAXIMA * G + m
                dve.wait_ge(max_filled, n + 1)
                width = min(512, P * (i + 1) - 512 * half)
                col = i + 4 * half
                nc.vector.tensor_reduce(part_max[:, head, col:col + 1], s_max[m % 2][:, 0:width], AX.X, ALU.max).then_inc(max_free, 1)

            def split_max(G):
                dve.wait_ge(max_free, MAXIMA * (G + 1))
                link(nc.vector.tensor_tensor(part_max[:, :, 4:8], part_max[:, :, 4:8], part_max[:, :, 8:12], ALU.max))
                link(nc.vector.tensor_scalar(neg[:, :, :], part_max[:, :, 0:8], -1.0, None, ALU.mult))
                rest = neg[:, :, :].rearrange("p (j a) i -> p j a i", a=2)
                for r in range(3):
                    part = neg_split[:, :, r, :, :].rearrange("p a j i -> p j a i")
                    ins = nc.vector.tensor_copy(part, rest)
                    if r == 2:
                        ins.then_inc(neg_ready, 1)
                    else:
                        link(ins)
                        link(nc.vector.tensor_tensor(rest, rest, part, ALU.subtract))

            def normalise(g, qb, n):
                dve.wait_ge(m_filled, n + 1)
                heads = misc[:, :].rearrange("p (t h c) -> p t h c", t=4, c=32)
                link(nc.vector.reciprocal(recip[:, :, :], heads[:, :, :, A_DH]))
                nc.vector.tensor_tensor(
                    attn[:, 4 * qb:4 * qb + 4, 32 * g:32 * (g + 1)].rearrange("p t (h d) -> p t h d", d=A_DH),
                    heads[:, :, :, 0:A_DH], recip[:, :, :].unsqueeze(3).to_broadcast([P, 4, 4, A_DH]), ALU.mult).then_inc(m_free, 1)

            nc.vector.memset(w_b[:, :], 0.0).then_inc(zeroed, 1)
            nc.vector.memset(q_split[:, :, :, :], 0.0)
            nc.vector.memset(k_split[:, :, :, :, :], 0.0)
            for g in range(A_KV):
                nc.vector.memset(vx[g][:, :, :], 0.0)
                nc.vector.memset(kx[g][:, :, :], 0.0)
            link(nc.vector.memset(recip[:, :, :], 0.0))
            for g in range(A_KV):
                nc.vector.memset(vx[g][:, :, A_DH:A_DH + 1], 1.0)
            nc.vector.memset(k_split[:, :, :, :, SPLIT:SPLIT + 3], 1.0).then_inc(ready, 1)
            dve.wait_ge(masked, 3)
            link(nc.vector.tensor_copy(ident_b[:, :], ident[:, :]))
            nc.vector.memset(recip[:, :, :], 0.0).then_inc(ready, 1)

            dve.wait_ge(w_in, 16 * 8)

            def prepare(b):
                dve.wait_ge(m_free, fills.prepared(b, "kv3") + 1)
                rope()
                split()

            prepare(0)

            def body(b):
                for g in range(A_KV):
                    copy_v(g)
                for m in range(MAXIMA):
                    reduce_unit(A_KV * b, m)
                split_max(A_KV * b)
                for g in range(A_KV):
                    G = A_KV * b + g
                    for u in range(N_UNITS):
                        if u == HALF_DONE + 3:
                            normalise(g, 0, fills.number(b, g, "oa0"))
                        if g < A_KV - 1:
                            for m in maxima_at(u):
                                reduce_unit(G + 1, m)
                                if m == MAXIMA - 1:
                                    split_max(G + 1)
                    if g == A_KV - 1:
                        prepare(b + 1)
                    normalise(g, 1, fills.number(b, g, "oa1"))
                dve.wait_ge(xr_in, 16 * (b + 1))
                for k in range(2):
                    dve.wait_ge(m_filled, fills.number(b, A_KV, f"y{k}") + 1)
                    nc.vector.tensor_tensor(z[:, 4 * k:4 * k + 4, :], misc[:, :].rearrange("p (t d) -> p t d", t=4),
                                            xr[:, 4 * k:4 * k + 4, :], ALU.add).then_inc(m_free, 1)
                dve.wait_ge(m_free, fills.number(b, A_KV, "y1") + 1)
                link(nc.vector.tensor_tensor(z[:, :, :], z[:, :, :], b_out[:, :].unsqueeze(1).to_broadcast([P, TILES, DIM]), ALU.add))
                if later(b):
                    dve.wait_ge(y_out, 16 * b)
                layer_norm(nc, link, z, y, TILES, stats, mean_var, var_eps, rstd, nwt, lambda ins: ins.then_inc(y_ready, 1))
                nc.vector.sem_clear(v_link)
                links[0] = 0

            nc.vector.sem_clear(v_link)
            links[0] = 0
            batches(dve, body)

        @block.gpsimd
        def _(pool):
            nc.gpsimd.memset(ident[:, :], 0.0).then_inc(masked, 1)
            nc.gpsimd.memset(mask_q[:, :], 0.0).then_inc(masked, 1)
            pool.wait_ge(masked, 2)
            nc.gpsimd.affine_select(out=ident[:, :], in_=ident[:, :], compare_op=ALU.not_equal, fill=1.0, base=0,
                                    pattern=[[-1, P]], channel_multiplier=1).then_inc(masked, 1)
            nc.gpsimd.affine_select(out=mask_k[:, :], in_=mask_q[:, :], compare_op=ALU.is_ge, fill=MASKED, base=0,
                                    pattern=[[1, P]], channel_multiplier=-1).then_inc(masked, 1)
            pool.wait_ge(masked, 4)
            nc.gpsimd.affine_select(out=mask_q[:, :], in_=mask_q[:, :], compare_op=ALU.is_ge, fill=MASKED, base=0,
                                    pattern=[[-1, P]], channel_multiplier=1).then_inc(ready, 1)


def layer_norm(nc, link, src, out, tiles, stats, mean_var, var_eps, rstd, tmp, last):
    for t in range(tiles):
        ins = nc.vector.bn_stats(stats[:, t, :], src[:, t, :])
    link(ins)
    for t in range(tiles):
        ins = nc.vector.bn_aggr(mean_var[:, t, :], stats[:, t, :])
    link(ins)
    link(nc.vector.tensor_scalar(var_eps[:, 0:tiles], mean_var[:, 0:tiles, 1], 1e-5, None, ALU.add))
    rsqrt(nc, link, rstd[:, 0:tiles], var_eps[:, 0:tiles], tmp[:, 0:tiles], link)
    for t in range(tiles):
        ins = nc.vector.tensor_scalar(out[:, t, :], src[:, t, :], mean_var[:, t, 0:1], rstd[:, t:t + 1], ALU.subtract, ALU.mult)
    last(ins)


def closing_norm(nc, x_dram, out):
    with ExitStack() as ctx:
        def sb(name, shape, dt=fp32):
            return ctx.enter_context(nc.sbuf_tensor(name, shape, dt))

        def sem(name):
            return ctx.enter_context(nc.semaphore(name))

        x_first = [sb(f"x_first{b}", [P, TILES, DIM]) for b in range(BATCH)]
        x_last = [sb(f"x_last{b}", [P, TILES, DIM]) for b in range(BATCH)]
        normed = [sb(f"normed{b}", [P, TILES, DIM]) for b in range(BATCH)]
        stats = sb("c_stats", [P, TILES, 6])
        mean_var = sb("c_mean_var", [P, TILES, 2])
        var_eps, rstd, nwt = (sb(f"c_{n}", [P, TILES]) for n in ("var_eps", "rstd", "nwt"))
        loaded = [sem(f"c_loaded{b}") for b in range(BATCH)]
        norm_done, stored, v_link = sem("c_norm_done"), sem("c_stored"), sem("c_v_link")
        block = ctx.enter_context(nc.Block())

        def tiled(rows):
            return rows.rearrange("(t p) d -> p t d", p=P)

        @block.sync
        def _(sp):
            for b in range(BATCH):
                sp.dma_start(x_first[b][:, :, :], tiled(x_dram[b, 1:1 + SEQ, :])).then_inc(loaded[b], 16)
                sp.dma_start(x_last[b][:, :, :], tiled(x_dram[ROUNDS + b, 1:1 + SEQ, :])).then_inc(loaded[b], 16)
            for b in range(BATCH):
                sp.wait_ge(norm_done, b + 1)
                sp.dma_start(tiled(out[b, :, :]), normed[b][:, :, :]).then_inc(stored, 16)
            sp.wait_ge(stored, 16 * BATCH)

        @block.vector
        def _(dve):
            links = [0]

            def link(ins):
                links[0] += 1
                ins.then_inc(v_link, 1)
                dve.wait_ge(v_link, links[0])

            for b in range(BATCH):
                dve.wait_ge(loaded[b], 32)
                link(nc.vector.tensor_tensor(x_first[b][:, :, :], x_first[b][:, :, :], x_last[b][:, :, :], ALU.add))
                layer_norm(nc, link, x_first[b], normed[b], TILES, stats, mean_var, var_eps, rstd, nwt,
                           lambda ins: ins.then_inc(norm_done, 1))


def clear_first_rows(nc, x_dram, x1_dram):
    with ExitStack() as ctx:
        zeros = ctx.enter_context(nc.sbuf_tensor("zeros", [P, DIM], fp32))
        zeroed, rows_out = ctx.enter_context(nc.semaphore("zeroed")), ctx.enter_context(nc.semaphore("rows_out"))
        block = ctx.enter_context(nc.Block())

        @block.vector
        def _(dve):
            nc.vector.memset(zeros[:, :], 0.0).then_inc(zeroed, 1)

        @block.sync
        def _(sp):
            sp.wait_ge(zeroed, 1)
            sp.dma_start(x_dram[:, 0, :], zeros[0:ROUNDS + BATCH, :]).then_inc(rows_out, 16)
            sp.dma_start(x1_dram[0:1, :], zeros[0:1, :]).then_inc(rows_out, 16)
            sp.wait_ge(rows_out, 32)


def build(nc, w, out):
    x_dram = nc.dram_tensor("x_layers", [ROUNDS + BATCH, 1 + SEQ, DIM], fp32, kind="Internal").ap()
    x1_dram = nc.dram_tensor("x1", [1 + SEQ, DIM], fp32, kind="Internal").ap()
    neg_dram = nc.dram_tensor("neg_max", [96, P], bf16, kind="Internal").ap()
    clear_first_rows(nc, x_dram, x1_dram)
    mla_attention(nc, w["x"], x_dram, neg_dram, w)
    local_layers(nc, x_dram, x1_dram, w)
    closing_norm(nc, x_dram, out)



def rope_tables(np):
    D = A_DH
    inv_freq = 1.0 / 10000.0 ** (np.arange(0, D, 2, dtype=np.float32) / np.float32(D))
    freqs = (np.arange(SEQ, dtype=np.float32)[:, None] * inv_freq.astype(np.float32)[None, :]).astype(np.float64)
    cos = np.repeat(np.cos(freqs), 2, axis=1)
    sin = np.repeat(np.sin(freqs), 2, axis=1) * np.where(np.arange(D) % 2, 1.0, -1.0)
    tables = []
    for heads, scale in ((A_HEADS, D ** -0.5), (A_KV, 1.0)):
        both = np.stack([np.tile(cos, (1, heads)), np.tile(sin, (1, heads))], 1) * scale
        both = both.reshape(TILES, P, 2, heads * D).transpose(1, 0, 2, 3)
        tables.append(np.ascontiguousarray(both.astype(np.float32)))
    return tables


def rotary_table(np):
    half = np.arange(0, DH, 2, dtype=np.float32)
    inv_freq = (1.0 / np.power(np.float32(10000.0), half / np.float32(DH))).astype(np.float32)
    t = np.arange(SEQ, dtype=np.float32)
    freqs = (t[:, None] * inv_freq[None, :]).astype(np.float64)
    freqs = np.concatenate([freqs, freqs], -1)
    base_scale = ((half + np.float32(0.4 * DH)) / np.float32(1.4 * DH)).astype(np.float64)
    power = ((t - SEQ // 2) / (WINDOW // 2)).astype(np.float64)
    scale = base_scale[None, :] ** power[:, None]
    scale = np.concatenate([scale, scale], -1)
    cos, sin = np.cos(freqs), np.sin(freqs) * np.where(np.arange(DH) < DH // 2, -1.0, 1.0)
    rows = np.stack([cos * scale * QK_SCALE, sin * scale * QK_SCALE, cos / scale, sin / scale], 1)
    return np.ascontiguousarray(rows.reshape(TILES, P, 4, DH).transpose(1, 0, 2, 3).astype(np.float32))


def pack_vectors(np, a):
    def swap(v):
        return np.concatenate([v[:, DH // 2:], v[:, :DH // 2]], 1)

    qs, ks = a["L0_ffn_q_scale"], a["L0_ffn_k_scale"]
    qk_rows = np.concatenate([qs, swap(qs), ks, swap(ks)], 1)
    small = np.zeros((DEPTH, P, N_SMALL), np.float32)
    small[:, :, SMALL["g"]], small[:, :, SMALL["b"]] = a["L0_ffn_ln_g"], a["L0_ffn_ln_b"]
    for k, (first, width) in enumerate(FF_BLOCKS):
        small[:, :width, SMALL["b1a"] + k] = a["L0_ffn_b1"][:, first:first + width]
        small[:, :width, SMALL["b1g"] + k] = a["L0_ffn_b1"][:, FF + first:FF + first + width]
    small[:, :, SMALL["b2"]] = a["L0_ffn_b2"]
    return np.ascontiguousarray(qk_rows), small


def kernel(**inputs):
    import numpy as np
    import concourse.bacc as bacc
    from concourse.bass_utils import run_bass_kernel_spmd

    nc = bacc.Bacc("TRN2", target_bir_lowering=False, num_devices=1)
    a = {name: np.ascontiguousarray(value) for name, value in inputs.items()}
    rope_q, rope_k = rope_tables(np)
    qk_rows, small = pack_vectors(np, a)
    tensors = dict(x=a["L0_attn_x"], Wqa=a["L0_attn_Wqa"], Wqb=a["L0_attn_Wqb"], Wkva=a["L0_attn_Wkva"],
                   Wkvb=a["L0_attn_Wkvb"], Wout=a["L0_attn_Wout"], bout=a["L0_attn_bout"], rope_q=rope_q, rope_k=rope_k,
                   Wqkv=a["L0_ffn_Wqkv"], Wo=a["L0_ffn_Wo"], W1=a["L0_ffn_W1"], W2=a["L0_ffn_W2"],
                   qk_rows=qk_rows, small=small, rotary=rotary_table(np))
    arrays = {f"in_{name}_dram": value for name, value in tensors.items()}
    w = {name: nc.dram_tensor(f"in_{name}_dram", value.shape, fp32, kind="ExternalInput").ap()
         for name, value in tensors.items()}
    out = nc.dram_tensor("out_dram", (BATCH, SEQ, DIM), fp32, kind="ExternalOutput").ap()
    build(nc, w, out)
    return run_bass_kernel_spmd(nc, [arrays], core_ids=[0]).results[0]["out_dram"]
```
